# Optimizing a Trainium2 kernel written in Bass

```python
import numpy as np
import jax
import jax.numpy as jnp

def _softmax(x, axis=-1):
    return jax.nn.softmax(x, axis=axis)

def _gelu(x):
    return jax.nn.gelu(x, approximate=True)

def _silu(x):
    return jax.nn.silu(x)

def _sigmoid(x):
    return jax.nn.sigmoid(x)

def _layernorm(x, axis=-1, eps=1e-05):
    m = jnp.mean(x, axis=axis, keepdims=True)
    v = jnp.var(x, axis=axis, keepdims=True)
    return (x - m) / jnp.sqrt(v + eps)

def _scatter_add(tgt, idx, src, axis=0):
    return tgt.at[idx].add(src)

def _segment_sum(src, seg, n):
    return jax.ops.segment_sum(src, seg, n)
kernel_name = 'mk_perceiver_d1_seqx_r8_9ed46f'

def setup_inputs(seed: int=0):
    np.random.seed(seed)
    _w = jnp.asarray

    def _rec_inputs():
        import jax
        import jax.numpy as jnp
        _rk = jax.random.key(seed)
        x = -0.0005146 + 1 * jax.random.normal(jax.random.fold_in(_rk, 1), (16, 32, 512), jnp.float32)
        _lenS = 32 - jax.random.randint(jax.random.fold_in(_rk, 7), (16,), 0, max(1, 32 // 4) + 1, jnp.int32)
        _lenS2 = 512 - jax.random.randint(jax.random.fold_in(_rk, 8), (16,), 0, max(1, 512 // 4) + 1, jnp.int32)
        _ctx_4096P = jax.random.normal(jax.random.fold_in(_rk, 11), (16, 16, 512), jnp.float32)
        _ctx_4096c = jax.random.dirichlet(jax.random.fold_in(_rk, 511), 0.3 * jnp.ones((16,), jnp.float32), (16, 512))
        _ctx_4096t = jnp.einsum('bsk,bkd->bsd', _ctx_4096c, _ctx_4096P)
        _ctx_4096t = _ctx_4096t * jax.lax.rsqrt(jnp.mean(jnp.square(_ctx_4096t)) + 1e-12) * 0.953939
        ctx_4096 = -0.0142356 + 1.00583 * (_ctx_4096t + 0.3 * jax.random.normal(jax.random.fold_in(_rk, 611), (16, 512, 512), jnp.float32))
        return (x, ctx_4096)
    x, ctx_4096 = _rec_inputs()

    def _L0_xattn_setup():
        import jax, jax.numpy as jnp
        import numpy as np
        K = 10
        NUM_BITS = 10
        M_METHODS = 4

        def _quantize(coords, num_bits=NUM_BITS):
            cmin = coords.min(axis=1, keepdims=True)
            cmax = coords.max(axis=1, keepdims=True)
            scale = (2 ** num_bits - 1) / (cmax - cmin + 1e-06)
            q = jnp.floor((coords - cmin) * scale)
            return jnp.clip(q, 0, 2 ** num_bits - 1).astype(jnp.int32)

        def _morton_key(q):
            x, y, z = (q[..., 0], q[..., 1], q[..., 2])
            key = jnp.zeros(x.shape, dtype=jnp.int32)
            for b in range(NUM_BITS):
                key = key | (x >> b & 1) << 3 * b + 2 | (y >> b & 1) << 3 * b + 1 | (z >> b & 1) << 3 * b
            return key

        def _hilbert_key(q, num_bits=NUM_BITS):
            n = 3
            X = [q[..., i] for i in range(n)]
            M = 1 << num_bits - 1
            Q = M
            while Q > 1:
                P = Q - 1
                for i in range(n):
                    cond = X[i] & Q > 0
                    t = (X[0] ^ X[i]) & P
                    new_X0 = jnp.where(cond, X[0] ^ P, X[0] ^ t)
                    if i != 0:
                        X[i] = jnp.where(cond, X[i], X[i] ^ t)
                    X[0] = new_X0
                Q >>= 1
            for i in range(1, n):
                X[i] = X[i] ^ X[i - 1]
            t = jnp.zeros_like(X[0])
            Q = M
            while Q > 1:
                t = jnp.where(X[n - 1] & Q > 0, t ^ Q - 1, t)
                Q >>= 1
            X = [xi ^ t for xi in X]
            key = jnp.zeros(X[0].shape, dtype=jnp.int32)
            for b in range(num_bits - 1, -1, -1):
                for i in range(n):
                    key = key << 1 | X[i] >> b & 1
            return key

        def _sorted_indices(coords_bn3):
            q = _quantize(coords_bn3)
            qt = q[..., jnp.array([1, 0, 2])]
            keys = [_morton_key(q), _morton_key(qt), _hilbert_key(q), _hilbert_key(qt)]
            return [jnp.argsort(kk, axis=1) for kk in keys]

        def _window_inds(sorted_idx, k=K):
            B, N = sorted_idx.shape
            i = jnp.arange(N)
            start = jnp.maximum(0, i - k // 2)
            end = jnp.minimum(N, i + k // 2 + 1)
            pos = jnp.minimum(start[:, None] + jnp.arange(k)[None, :], (end - 1)[:, None])
            return jnp.take(sorted_idx, pos, axis=1)

        def _get_graph_features(feats, inds_list, perm, W_lin, b_lin, k=K):
            B, N, C = feats.shape
            center = feats[:, :, None, :]
            gather = jax.vmap(lambda f, idx: f[idx])
            per_method = []
            for inds in inds_list:
                neigh = gather(feats, inds)
                gf = jnp.concatenate([jnp.broadcast_to(center, (B, N, k, C)), neigh - center], axis=-1)
                per_method.append(gf)
            allf = jnp.stack(per_method, axis=-1)
            allf = allf[..., perm]
            total = 2 * C * M_METHODS
            x = allf.reshape(B * N, k, total)
            x16 = x.astype(jnp.float16).astype(jnp.float32)
            headdim = min(32, total)
            nheads = total // headdim
            qh = x16.reshape(B * N, k, nheads, headdim)
            scores = jnp.einsum('bihd,bjhd->bhij', qh, qh) / np.float32(np.sqrt(headdim))
            attn = jax.nn.softmax(scores, axis=-1)
            out = jnp.einsum('bhij,bjhd->bihd', attn, qh).reshape(B * N, k, total)
            fused = out @ W_lin.T + b_lin
            return fused.reshape(B, N, k, 64)

        def _instance_norm(x, axes):
            mu = x.mean(axis=axes, keepdims=True)
            var = x.var(axis=axes, keepdims=True)
            return (x - mu) / jnp.sqrt(var + 1e-05)

        def _lrelu(x):
            return jnp.where(x > 0, x, 0.2 * x)
        key = jax.random.key(seed)
        ks = jax.random.split(key, 8)
        B, N, C = (2, 512, 32)
        tot = M_METHODS * 2 * C
        s = 0.02
        return {'coords': jax.random.normal(ks[0], (B, 3, N), jnp.float32), 'feats': jax.random.normal(ks[1], (B, C, N), jnp.float32), 'W_lin1': jax.random.normal(ks[2], (64, tot), jnp.float32) * s, 'b_lin1': jnp.zeros((64,), jnp.float32), 'W_lin2': jax.random.normal(ks[3], (64, tot), jnp.float32) * s, 'b_lin2': jnp.zeros((64,), jnp.float32), 'W_conv1': jax.random.normal(ks[4], (C, 2 * C), jnp.float32) * s, 'W_conv2': jax.random.normal(ks[5], (2 * C, 2 * C), jnp.float32) * s, 'W_conv3': jax.random.normal(ks[6], (C, 4 * C), jnp.float32) * s}
    _L0_xattn_all = _L0_xattn_setup()
    _L0_xattn_in = {k: v for k, v in _L0_xattn_all.items() if k in ('W_lin1', 'b_lin1', 'W_lin2', 'b_lin2', 'W_conv1', 'W_conv2', 'W_conv3')}
    del _L0_xattn_all

    def _L0_attn_setup():
        import jax, jax.numpy as jnp
        import numpy as np
        B, C, L = (64, 64, 512)
        key = jax.random.key(seed)
        x = jax.random.normal(key, (B, C, L), dtype=jnp.float32)
        return {'x': x}
    _L0_attn_all = _L0_attn_setup()
    _L0_attn_in = {k: v for k, v in _L0_attn_all.items() if k in ()}
    del _L0_attn_all

    def _L0_ffn_setup():
        import jax, jax.numpy as jnp
        import numpy as np

        def _dequant_linear(x, wq, scale):
            w = wq.astype(jnp.float32) * scale[:, None]
            return jnp.einsum('bsh,oh->bso', x, w)
        key = jax.random.key(seed)
        ks = jax.random.split(key, 7)
        B, S, H, I = (2, 256, 512, 1792)
        x = jax.random.normal(ks[0], (B, S, H), dtype=jnp.float32)
        gate_wq = jax.random.randint(ks[1], (I, H), -128, 128, dtype=jnp.int32)
        up_wq = jax.random.randint(ks[2], (I, H), -128, 128, dtype=jnp.int32)
        down_wq = jax.random.randint(ks[3], (H, I), -128, 128, dtype=jnp.int32)
        gate_scale = jax.random.uniform(ks[4], (I,), dtype=jnp.float32, minval=0.5, maxval=1.5) / (127.0 * np.sqrt(H))
        up_scale = jax.random.uniform(ks[5], (I,), dtype=jnp.float32, minval=0.5, maxval=1.5) / (127.0 * np.sqrt(H))
        down_scale = jax.random.uniform(ks[6], (H,), dtype=jnp.float32, minval=0.5, maxval=1.5) / (127.0 * np.sqrt(I))
        return {'x': x, 'gate_wq': gate_wq, 'gate_scale': gate_scale, 'up_wq': up_wq, 'up_scale': up_scale, 'down_wq': down_wq, 'down_scale': down_scale}
    _L0_ffn_all = _L0_ffn_setup()
    _L0_ffn_in = {k: v for k, v in _L0_ffn_all.items() if k in ('gate_wq', 'gate_scale', 'up_wq', 'up_scale', 'down_wq', 'down_scale')}
    del _L0_ffn_all
    return {'x': x, 'ctx_4096': ctx_4096, 'L0_xattn_W_lin1': _L0_xattn_in['W_lin1'], 'L0_xattn_b_lin1': _L0_xattn_in['b_lin1'], 'L0_xattn_W_lin2': _L0_xattn_in['W_lin2'], 'L0_xattn_b_lin2': _L0_xattn_in['b_lin2'], 'L0_xattn_W_conv1': _L0_xattn_in['W_conv1'], 'L0_xattn_W_conv2': _L0_xattn_in['W_conv2'], 'L0_xattn_W_conv3': _L0_xattn_in['W_conv3'], 'L0_ffn_gate_wq': _L0_ffn_in['gate_wq'], 'L0_ffn_gate_scale': _L0_ffn_in['gate_scale'], 'L0_ffn_up_wq': _L0_ffn_in['up_wq'], 'L0_ffn_up_scale': _L0_ffn_in['up_scale'], 'L0_ffn_down_wq': _L0_ffn_in['down_wq'], 'L0_ffn_down_scale': _L0_ffn_in['down_scale']}

def reference(x, ctx_4096, L0_xattn_W_lin1, L0_xattn_b_lin1, L0_xattn_W_lin2, L0_xattn_b_lin2, L0_xattn_W_conv1, L0_xattn_W_conv2, L0_xattn_W_conv3, L0_ffn_gate_wq, L0_ffn_gate_scale, L0_ffn_up_wq, L0_ffn_up_scale, L0_ffn_down_wq, L0_ffn_down_scale):
    import jax
    import jax.numpy as jnp

    def _L0_xattn_ref(coords, feats, W_lin1, b_lin1, W_lin2, b_lin2, W_conv1, W_conv2, W_conv3):
        import jax, jax.numpy as jnp
        import numpy as np
        K = 10
        NUM_BITS = 10
        M_METHODS = 4

        def _quantize(coords, num_bits=NUM_BITS):
            cmin = coords.min(axis=1, keepdims=True)
            cmax = coords.max(axis=1, keepdims=True)
            scale = (2 ** num_bits - 1) / (cmax - cmin + 1e-06)
            q = jnp.floor((coords - cmin) * scale)
            return jnp.clip(q, 0, 2 ** num_bits - 1).astype(jnp.int32)

        def _morton_key(q):
            x, y, z = (q[..., 0], q[..., 1], q[..., 2])
            key = jnp.zeros(x.shape, dtype=jnp.int32)
            for b in range(NUM_BITS):
                key = key | (x >> b & 1) << 3 * b + 2 | (y >> b & 1) << 3 * b + 1 | (z >> b & 1) << 3 * b
            return key

        def _hilbert_key(q, num_bits=NUM_BITS):
            n = 3
            X = [q[..., i] for i in range(n)]
            M = 1 << num_bits - 1
            Q = M
            while Q > 1:
                P = Q - 1
                for i in range(n):
                    cond = X[i] & Q > 0
                    t = (X[0] ^ X[i]) & P
                    new_X0 = jnp.where(cond, X[0] ^ P, X[0] ^ t)
                    if i != 0:
                        X[i] = jnp.where(cond, X[i], X[i] ^ t)
                    X[0] = new_X0
                Q >>= 1
            for i in range(1, n):
                X[i] = X[i] ^ X[i - 1]
            t = jnp.zeros_like(X[0])
            Q = M
            while Q > 1:
                t = jnp.where(X[n - 1] & Q > 0, t ^ Q - 1, t)
                Q >>= 1
            X = [xi ^ t for xi in X]
            key = jnp.zeros(X[0].shape, dtype=jnp.int32)
            for b in range(num_bits - 1, -1, -1):
                for i in range(n):
                    key = key << 1 | X[i] >> b & 1
            return key

        def _sorted_indices(coords_bn3):
            q = _quantize(coords_bn3)
            qt = q[..., jnp.array([1, 0, 2])]
            keys = [_morton_key(q), _morton_key(qt), _hilbert_key(q), _hilbert_key(qt)]
            return [jnp.argsort(kk, axis=1) for kk in keys]

        def _window_inds(sorted_idx, k=K):
            B, N = sorted_idx.shape
            i = jnp.arange(N)
            start = jnp.maximum(0, i - k // 2)
            end = jnp.minimum(N, i + k // 2 + 1)
            pos = jnp.minimum(start[:, None] + jnp.arange(k)[None, :], (end - 1)[:, None])
            return jnp.take(sorted_idx, pos, axis=1)

        def _get_graph_features(feats, inds_list, perm, W_lin, b_lin, k=K):
            B, N, C = feats.shape
            center = feats[:, :, None, :]
            gather = jax.vmap(lambda f, idx: f[idx])
            per_method = []
            for inds in inds_list:
                neigh = gather(feats, inds)
                gf = jnp.concatenate([jnp.broadcast_to(center, (B, N, k, C)), neigh - center], axis=-1)
                per_method.append(gf)
            allf = jnp.stack(per_method, axis=-1)
            allf = allf[..., perm]
            total = 2 * C * M_METHODS
            x = allf.reshape(B * N, k, total)
            x16 = x.astype(jnp.float16).astype(jnp.float32)
            headdim = min(32, total)
            nheads = total // headdim
            qh = x16.reshape(B * N, k, nheads, headdim)
            scores = jnp.einsum('bihd,bjhd->bhij', qh, qh) / np.float32(np.sqrt(headdim))
            attn = jax.nn.softmax(scores, axis=-1)
            out = jnp.einsum('bhij,bjhd->bihd', attn, qh).reshape(B * N, k, total)
            fused = out @ W_lin.T + b_lin
            return fused.reshape(B, N, k, 64)

        def _instance_norm(x, axes):
            mu = x.mean(axis=axes, keepdims=True)
            var = x.var(axis=axes, keepdims=True)
            return (x - mu) / jnp.sqrt(var + 1e-05)

        def _lrelu(x):
            return jnp.where(x > 0, x, 0.2 * x)
        inds_sorted = _sorted_indices(coords.transpose(0, 2, 1))
        inds_list = [_window_inds(s) for s in inds_sorted]
        perm1 = jnp.array([2, 0, 3, 1])
        perm2 = jnp.array([1, 3, 0, 2])
        f0 = feats.transpose(0, 2, 1)
        g1 = _get_graph_features(f0, inds_list, perm1, W_lin1, b_lin1)
        h1 = jnp.einsum('oc,bnkc->bonk', W_conv1, g1)
        h1 = _lrelu(_instance_norm(h1, (2, 3)))
        feats1 = h1.max(axis=-1)
        g2 = _get_graph_features(feats1.transpose(0, 2, 1), inds_list, perm2, W_lin2, b_lin2)
        h2 = jnp.einsum('oc,bnkc->bonk', W_conv2, g2)
        h2 = _lrelu(_instance_norm(h2, (2, 3)))
        feats2 = h2.max(axis=-1)
        f3 = jnp.concatenate([feats, feats1, feats2], axis=1)
        h3 = jnp.einsum('oc,bcn->bon', W_conv3, f3)
        return _lrelu(_instance_norm(h3, (2,)))

    def _L0_attn_ref(x):
        import jax, jax.numpy as jnp
        import numpy as np
        B, C, L = (64, 64, 512)
        b, c, l = x.shape
        q = jnp.transpose(x, (2, 0, 1))
        scale = jnp.asarray(c, x.dtype) ** 0.5
        scores = jnp.einsum('lnc,lmc->lnm', q, q) / scale
        prob = jax.nn.softmax(scores, axis=-1)
        msg = jnp.einsum('lnm,lmc->lnc', prob, q)
        return x + jnp.transpose(msg, (1, 2, 0))

    def _L0_ffn_ref(x, gate_wq, gate_scale, up_wq, up_scale, down_wq, down_scale):
        import jax, jax.numpy as jnp
        import numpy as np

        def _dequant_linear(x, wq, scale):
            w = wq.astype(jnp.float32) * scale[:, None]
            return jnp.einsum('bsh,oh->bso', x, w)
        gate = _dequant_linear(x, gate_wq, gate_scale)
        up = _dequant_linear(x, up_wq, up_scale)
        h = jax.nn.silu(gate) * up
        return _dequant_linear(h, down_wq, down_scale)
    x = x + _L0_xattn_ref(ctx_4096, _layernorm(x, axis=-1), L0_xattn_W_lin1, L0_xattn_b_lin1, L0_xattn_W_lin2, L0_xattn_b_lin2, L0_xattn_W_conv1, L0_xattn_W_conv2, L0_xattn_W_conv3)
    x = x + _L0_attn_ref(_layernorm(x, axis=-1))
    x = x + _L0_ffn_ref(_layernorm(x, axis=-1), L0_ffn_gate_wq, L0_ffn_gate_scale, L0_ffn_up_wq, L0_ffn_up_scale, L0_ffn_down_wq, L0_ffn_down_scale)
    return x

_drawn_inputs = setup_inputs


def setup_inputs(seed=0):
    import zlib

    import numpy as np

    out = dict(_drawn_inputs(seed))
    spreads = {'L0_xattn_b_lin1': (0.0, 0.8), 'L0_xattn_b_lin2': (0.0, 0.8)}
    factors = {'L0_ffn_gate_scale': 4.513, 'L0_ffn_up_scale': 5.087, 'L0_ffn_down_scale': 5.132}
    for name, (base, spread) in spreads.items():
        noise = np.random.default_rng([zlib.crc32(name.encode()), seed]).standard_normal(out[name].shape)
        drawn = base * np.exp(spread * noise) if base else spread * noise
        out[name] = jnp.asarray(drawn.astype(out[name].dtype))
    for name, factor in factors.items():
        out[name] = (out[name] * factor).astype(out[name].dtype)
    return out
```

```python
from contextlib import ExitStack

import numpy as np
import concourse.bass as bass
from concourse import mybir

ALU = mybir.AluOpType
ACT = mybir.ActivationFunctionType
AX_X = mybir.AxisListType.X
F32, F16, BF16 = mybir.dt.float32, mybir.dt.float16, mybir.dt.bfloat16
I32, U32 = mybir.dt.int32, mybir.dt.uint32

P = 128
B, C, N, H = 16, 32, 512, 512
FF = 1792
RT = B * C // P
BPT = P // C
NBITS = 10
METHODS, WIN, HEADS, HD = 4, 10, 4, 32
PERMS = ((2, 0, 3, 1), (1, 3, 0, 2))
BACK = 5
SQRT_HD = float(np.float32(np.sqrt(HD)))
EPS = 1e-5

STRIPS, SUB, TRI = 4, 4, 3
PTS = SUB * TRI
SP_PTS = N // STRIPS
CHUNKS = -(-SP_PTS // PTS)
SP_PAD = CHUNKS * PTS
COLS = STRIPS * PTS * WIN
BLK = TRI * WIN
NBLK = STRIPS * SUB
SW = BACK + N + 8
MASK = float(2 ** 22)
FLOOR = float(2 ** 23)


class Step:

    def __init__(self, engine, sem):
        self.engine, self.sem, self.count = engine, sem, 0

    def then_wait(self, ins):
        self.count += 1
        ins.then_inc(self.sem, 1)
        self.engine.wait_ge(self.sem, self.count)


class LoopStep:

    def __init__(self, engine, sem, i, per):
        self.engine, self.sem, self.i, self.per, self.count = engine, sem, i, per, 0

    def __call__(self, ins):
        self.count += 1
        assert self.count <= self.per
        ins.then_inc(self.sem, 1)
        self.engine.wait_ge(self.sem, self.i * self.per + self.count)


def clear_semaphores(nc, handles):
    with nc.Block() as block:
        @block.sync
        def _(sp):
            numbers = sorted(h.num for h in handles)
            start = numbers[0]
            for n, after in zip(numbers, numbers[1:] + [None]):
                if after != n + 1:
                    sp.sem_clear(range(start, n + 1))
                    start = after


class Newton:

    def __init__(self, nc, work, std_ready):
        self.nc, self.work, self.std_ready = nc, work, std_ready

    def on_scalar(self, act, shifted_ready, count, value):
        act.wait_ge(shifted_ready, value)
        self.nc.scalar.activation(self.work[1], self.work[0], ACT.Sqrt).then_inc(self.std_ready, 1)

    def on_vector(self, dve, link, var, rstd, shifted_ready, value):
        vec = self.nc.vector
        a, s, t = self.work[0], self.work[1], self.work[2]
        vec.tensor_scalar(a, var, EPS, None, ALU.add).then_inc(shifted_ready, 1)
        dve.wait_ge(self.std_ready, value)
        link(vec.reciprocal(rstd, s))
        link(vec.tensor_tensor(t, rstd, rstd, ALU.mult))
        link(vec.tensor_tensor(t, t, a, ALU.mult))
        link(vec.tensor_scalar(t, t, -0.5, 1.5, ALU.mult, ALU.add))
        link(vec.tensor_tensor(rstd, rstd, t, ALU.mult))


def sort_and_prepare(nc, g):
    ctx_in, x_in, feats, orders = g["ctx"], g["x"], g["feats"], g["orders"]
    with ExitStack() as ctx:
        def sb(name, shape, dt):
            return ctx.enter_context(nc.sbuf_tensor(name, shape, dt))

        handles = []

        def sem(name):
            handles.append(ctx.enter_context(nc.semaphore(name)))
            return handles[-1]

        coords = sb("coords", [P, 3, N], F32)
        lo = sb("lo", [P, 3], F32)
        hi = sb("hi", [P, 3], F32)
        small = sb("small", [P, 14, 3], F32)
        pos = sb("pos", [P, 3, P], F32)
        near = sb("near", [P, 3, P], F32)
        over = sb("over", [P, 3, P], F32)
        code = sb("code", [P, 2, 3, P], I32)
        spread = sb("spread", [P, 2, 3, P], I32)
        bit = sb("bit", [P, P], I32)
        notbit = sb("notbit", [P, P], I32)
        diff = sb("diff", [P, P], I32)
        key = sb("key", [P, 2, P], I32)
        high = sb("high", [P, 2, P], I32)
        low = sb("low", [P, 2, P], I32)
        keys = sb("keys", [METHODS * B, N], F32)
        top = sb("top", [METHODS * B, 2, 8], F32)
        where = sb("where", [METHODS * B, N], U32)
        order = sb("order", [METHODS * B, N], F16)
        rows = sb("rows", [P, RT, N], F32)
        normed = sb("normed", [P, RT, N], F32)
        stats = sb("stats", [P, RT, 6], F32)
        mean_var = sb("mean_var", [P, RT, 2], F32)
        rstd = sb("rstd", [P, RT], F32)
        work = sb("work", [P, 3, RT], F32)
        newton_std = sem("newton_std")
        newton = Newton(nc, [work[:, i, :] for i in range(3)], newton_std)
        raw = sb("raw", [P, 2, FF], I32)
        scales = sb("scales", [P, 32], F32)
        deq = sb("deq", [P, 2, FF], F32)
        turned = [ctx.enter_context(nc.psum_tensor(f"turned{i}", [P, 4, P], F32)) for i in range(4)]

        coords_in, x_loaded, raw_in = sem("coords_in"), sem("x_loaded"), [sem("raw_in0"), sem("raw_in1")]
        scales_in = sem("scales_in")
        step, var_ready, normed_ready = sem("step"), sem("var_ready"), sem("normed_ready")
        code_ready, keys_in, order_ready, stored = sem("code_ready"), sem("keys_in"), sem("order_ready"), sem("stored")
        deq_ready, turned_ready, turned_out = sem("deq_ready"), sem("turned_ready"), sem("turned_out")
        ctx.callback(lambda: clear_semaphores(nc, handles))
        block = ctx.enter_context(nc.Block())

        gate_blocks = [("gate", i, H) for i in range(FF // P)]
        up_blocks = [("up", i, H) for i in range(FF // P)]
        down_blocks = [("down", i, FF) for i in range(H // P)]
        loads = []
        for name in ("gate", "up"):
            i = 0
            while i < FF // P:
                m = min(3, FF // P - i)
                loads.append((name, i, m))
                i += m
        loads += [("down", i, 1) for i in range(H // P)]

        def scale_col(name, i):
            return {"gate": 0, "up": FF // P, "down": 2 * (FF // P)}[name] + i

        def groups():
            out = []
            for n, (name, i0, m) in enumerate(loads):
                if name == "down":
                    for j in range(0, FF // P, 4):
                        k = min(4, FF // P - j)
                        out.append((n, [(j + t) * P for t in range(k)],
                                    g["downT"][:, j:j + k, i0 * P:(i0 + 1) * P]))
                else:
                    for r in range(m):
                        out.append((n, [r * H + t * P for t in range(4)],
                                    g[name + "T"][:, :, (i0 + r) * P:(i0 + r + 1) * P]))
            return out

        GROUPS = groups()

        @block.sync
        def _(sp):
            for quarter in range(4):
                at = quarter * 32
                sp.dma_start(coords[at:at + B, :, :], ctx_in[:, 0:3, :]).then_inc(coords_in, 16)
                for slot, row in enumerate((1, 0, 2)):
                    sp.dma_start(coords[at + B:at + 2 * B, slot, :], ctx_in[:, row, :]).then_inc(coords_in, 16)
            sp.dma_start(rows[:], x_in.rearrange("(t q) c n -> (q c) t n", q=BPT)).then_inc(x_loaded, 16)
            sp.wait_ge(normed_ready, RT)
            for t in range(RT):
                for q in range(BPT):
                    sp.dma_start(feats[t * BPT + q, 0:C, :], normed[q * C:(q + 1) * C, t, :]).then_inc(stored, 16)
            sp.wait_ge(code_ready, 1)
            for kind in range(2):
                for quarter in range(4):
                    sp.dma_start(keys[kind * 32:kind * 32 + 32, quarter * P:(quarter + 1) * P],
                                 key[quarter * 32:quarter * 32 + 32, kind, :].bitcast(F32)).then_inc(keys_in, 16)
            sp.wait_ge(order_ready, 1)
            sp.dma_start(orders[:, :], order[:]).then_inc(stored, 16)
            sp.wait_ge(stored, 16 * (B + 1))

        @block.gpsimd
        def _(pool):
            wq = {"gate": g["gate_wq"], "up": g["up_wq"], "down": g["down_wq"]}
            for name in ("gate", "up", "down"):
                n = FF // P if name != "down" else H // P
                c = scale_col(name, 0)
                with nc.allow_non_contiguous_dma("scales, one per partition"):
                    pool.dma_start(scales[:, c:c + n], g[name + "_scale"].rearrange("(n p) -> p n", p=P))\
                        .then_inc(scales_in, 16)
            for n, (name, i, m) in enumerate(loads):
                if n >= 2:
                    pool.wait_ge(deq_ready, n - 1)
                width = H if name != "down" else FF
                src = wq[name][i * P:(i + m) * P, :].rearrange("(m p) w -> p m w", p=P)
                dst = raw[:, n % 2, 0:m * width].rearrange("p (m w) -> p m w", m=m)
                pool.dma_start(dst, src).then_inc(raw_in[n % 2], 16)

        @block.scalar
        def _(act):
            newton.on_scalar(act, var_ready, 1, 1)
            act.wait_ge(scales_in, 48)
            done = 0
            for n, (name, i, m) in enumerate(loads):
                width = H if name != "down" else FF
                act.wait_ge(raw_in[n % 2], 16 * (n // 2 + 1))
                if n >= 2:
                    act.wait_ge(turned_ready, sum(1 for q in GROUPS if q[0] <= n - 2))
                for r in range(m):
                    c = scale_col(name, i + r)
                    ins = nc.scalar.activation(deq[:, n % 2, r * width:(r + 1) * width],
                                               raw[:, n % 2, r * width:(r + 1) * width], ACT.Copy,
                                               scale=scales[:, c:c + 1])
                ins.then_inc(deq_ready, 1)
                if n >= 1:
                    for k, (load, cols, dst) in enumerate(GROUPS):
                        if load == n - 1:
                            act.wait_ge(turned_ready, k + 1)
                            nc.scalar.activation(dst, turned[k % 4][:, 0:len(cols), :], ACT.Copy)\
                                .then_inc(turned_out, 1)
            for k, (load, cols, dst) in enumerate(GROUPS):
                if load == len(loads) - 1:
                    act.wait_ge(turned_ready, k + 1)
                    nc.scalar.activation(dst, turned[k % 4][:, 0:len(cols), :], ACT.Copy).then_inc(turned_out, 1)

        @block.tensor
        def _(pe):
            for k, (load, cols, dst) in enumerate(GROUPS):
                pe.wait_ge(deq_ready, load + 1)
                if k >= 4:
                    pe.wait_ge(turned_out, k - 3)
                for t, c in enumerate(cols):
                    ins = nc.tensor.transpose(turned[k % 4][:, t, :], deq[:, load % 2, c:c + P], g["ident"][:])
                ins.then_inc(turned_ready, 1)

        @block.vector
        def _(dve):
            chain = Step(dve, step)
            link = chain.then_wait
            vec = nc.vector
            dve.wait_ge(x_loaded, 16)
            for t in range(RT):
                link(vec.bn_stats(stats[:, t, :], rows[:, t, :]))
                ins = vec.bn_aggr(mean_var[:, t, :], stats[:, t, :])
            link(ins)
            newton.on_vector(dve, link, mean_var[:, :, 1], rstd[:], var_ready, 1)
            for t in range(RT):
                vec.tensor_scalar(normed[:, t, :], rows[:, t, :], mean_var[:, t, 0:1], rstd[:, t:t + 1],
                                  ALU.subtract, ALU.mult).then_inc(normed_ready, 1)

            dve.wait_ge(coords_in, 256)
            vec.tensor_reduce(lo[:], coords[:], AX_X, ALU.min)
            link(vec.tensor_reduce(hi[:], coords[:], AX_X, ALU.max))
            top_q = float(2 ** NBITS - 1)
            d, r, y, t0, t1, yh, yl, dh, dl, pr, er, sc = (small[:, i, :] for i in range(12))
            link(vec.tensor_tensor(d, hi[:], lo[:], ALU.subtract))
            link(vec.tensor_scalar(d, d, 1e-6, None, ALU.add))
            link(vec.reciprocal(r, d))
            link(vec.tensor_scalar(y, r, top_q, None, ALU.mult))

            def halves(v, vh, vl):
                link(vec.tensor_scalar(t0, v, 4097.0, None, ALU.mult))
                link(vec.tensor_tensor(t1, t0, v, ALU.subtract))
                link(vec.tensor_tensor(vh, t0, t1, ALU.subtract))
                link(vec.tensor_tensor(vl, v, vh, ALU.subtract))

            halves(y, yh, yl)
            halves(d, dh, dl)
            link(vec.tensor_tensor(pr, y, d, ALU.mult))
            link(vec.tensor_tensor(er, yh, dh, ALU.mult))
            link(vec.tensor_tensor(er, er, pr, ALU.subtract))
            for a, b in ((yh, dl), (yl, dh), (yl, dl)):
                link(vec.tensor_tensor(t0, a, b, ALU.mult))
                link(vec.tensor_tensor(er, er, t0, ALU.add))
            link(vec.tensor_scalar(t0, pr, -1.0, top_q, ALU.mult, ALU.add))
            link(vec.tensor_tensor(t0, t0, er, ALU.subtract))
            link(vec.tensor_tensor(t0, t0, r, ALU.mult))
            link(vec.tensor_tensor(sc, y, t0, ALU.add))
            for quarter in range(4):
                at = slice(quarter * 32, quarter * 32 + 32)
                ins = vec.tensor_tensor(pos[at], coords[at, :, quarter * P:(quarter + 1) * P],
                                        lo[at].unsqueeze(2).broadcast_to([32, 3, P]), ALU.subtract)
            link(ins)
            link(vec.tensor_tensor(pos[:], pos[:], sc.unsqueeze(2).broadcast_to([P, 3, P]), ALU.mult))
            link(vec.tensor_scalar(near[:], pos[:], FLOOR, FLOOR, ALU.add, ALU.subtract))
            link(vec.tensor_tensor(over[:], near[:], pos[:], ALU.is_gt))
            link(vec.tensor_tensor(near[:], near[:], over[:], ALU.subtract))
            for kind in range(2):
                ins = vec.tensor_scalar(code[:, kind], near[:], 0.0, top_q, ALU.max, ALU.min)
            link(ins)

            X = [code[:, 1, i, :] for i in range(3)]
            for k in range(NBITS - 1, 0, -1):
                mask = (1 << k) - 1
                for i in range(3):
                    link(vec.tensor_scalar(bit[:], X[i], 31 - k, 31, ALU.logical_shift_left,
                                           ALU.arith_shift_right))
                    if i:
                        vec.tensor_tensor(diff[:], X[0], X[i], ALU.bitwise_xor)
                        link(vec.tensor_scalar(notbit[:], bit[:], -1, mask, ALU.bitwise_xor, ALU.bitwise_and))
                        link(vec.tensor_tensor(diff[:], diff[:], notbit[:], ALU.bitwise_and))
                        vec.tensor_tensor(X[i], X[i], diff[:], ALU.bitwise_xor)
                        link(vec.tensor_tensor(X[0], X[0], diff[:], ALU.bitwise_xor))
                    link(vec.scalar_tensor_tensor(X[0], bit[:], mask, X[0], ALU.bitwise_and, ALU.bitwise_xor))
            for i in (1, 2):
                link(vec.tensor_tensor(X[i], X[i], X[i - 1], ALU.bitwise_xor))
            link(vec.tensor_scalar(bit[:], X[2], 1, None, ALU.logical_shift_right))
            for s in (1, 2, 4, 8):
                link(vec.scalar_tensor_tensor(bit[:], bit[:], s, bit[:], ALU.logical_shift_right,
                                              ALU.bitwise_xor))
            for i in range(3):
                ins = vec.tensor_tensor(X[i], X[i], bit[:], ALU.bitwise_xor)
            link(ins)

            for s, m in ((16, 0x030000FF), (8, 0x0300F00F), (4, 0x030C30C3), (2, 0x09249249)):
                link(vec.scalar_tensor_tensor(spread[:], code[:], s, code[:], ALU.logical_shift_left,
                                              ALU.bitwise_or))
                link(vec.tensor_scalar(code[:], spread[:], m, None, ALU.bitwise_and))
            link(vec.scalar_tensor_tensor(key[:], code[:, :, 0, :], 2, code[:, :, 2, :],
                                          ALU.logical_shift_left, ALU.bitwise_or))
            link(vec.scalar_tensor_tensor(key[:], code[:, :, 1, :], 1, key[:], ALU.logical_shift_left,
                                          ALU.bitwise_or))
            link(vec.tensor_scalar(high[:], key[:], 23, None, ALU.logical_shift_right))
            link(vec.tensor_scalar(high[:], high[:], 1, None, ALU.add))
            link(vec.tensor_scalar(low[:], key[:], (1 << 23) - 1, -(1 << 31), ALU.bitwise_and, ALU.bitwise_or))
            vec.scalar_tensor_tensor(key[:], high[:], 23, low[:], ALU.logical_shift_left,
                                     ALU.bitwise_or).then_inc(code_ready, 1)

            dve.wait_ge(keys_in, 128)
            for t in range(N // 8):
                link(vec.max(top[:, t % 2, :], keys[:]))
                vec.max_index(where[:, 8 * t:8 * t + 8], top[:, t % 2, :], keys[:])
                link(vec.match_replace(keys[:], top[:, t % 2, :], keys[:], -3e38))
            vec.tensor_copy(order[:], where[:]).then_inc(order_ready, 1)


def gather_windows(nc, g, layer, sorted_rows):
    feats, orders, perm = g["feats"], g["orders"], PERMS[layer]
    first = layer * C
    with ExitStack() as ctx:
        def sb(name, shape, dt):
            return ctx.enter_context(nc.sbuf_tensor(f"{name}_{layer}", shape, dt))

        handles = []

        def sem(name):
            handles.append(ctx.enter_context(nc.semaphore(f"{name}_{layer}")))
            return handles[-1]

        rows = sb("feature_rows", [P, RT, N], F32)
        by_point = sb("by_point", [P, 4, B, 3, C], BF16)
        rest = sb("rest", [P, 2, 4, P], F32)
        ordered = sb("ordered", [P, 2, METHODS, N], F16)
        hot = sb("hot", [P, 2, 4, METHODS, N], BF16)
        gathered = sb("gathered", [P, 2, 4, METHODS * C], F32)
        products = ctx.enter_context(nc.psum_tensor(f"products_{layer}", [P, 4, 512], F32))
        turned = ctx.enter_context(nc.psum_tensor(f"turned_{layer}", [P, 2, 512], F32))

        rows_in, turned_ready, step = sem("rows_in"), sem("turned_ready"), sem("split_step")
        split_ready = sem("split_ready")
        order_in = [sem("order_in0"), sem("order_in1")]
        hot_ready, products_ready, gathered_ready = sem("hot_ready"), sem("products_ready"), sem("gathered_ready")
        window_turned, rows_ready = sem("window_turned"), sem("rows_ready")
        ctx.callback(lambda: clear_semaphores(nc, handles))
        block = ctx.enter_context(nc.Block())

        def product_view(rc):
            return products[:, rc, 0:3 * P].rearrange("p (s f) -> p s f", s=3)

        @block.sync
        def _(sp):
            for t in range(RT):
                for q in range(BPT):
                    sp.dma_start(rows[q * C:(q + 1) * C, t, :], feats[t * BPT + q, first:first + C, :])\
                        .then_inc(rows_in, 16)

            def load_orders(b, parity):
                src = bass.AP(orders.tensor, orders.offset + b * N, [[0, P], [B * N, METHODS], [1, N]])
                sp.dma_start(ordered[:, parity], src).then_inc(order_in[parity], 16)

            load_orders(0, 0)
            load_orders(1, 1)
            with sp.Fori(0, B // 2 - 1) as bp:
                for half in range(2):
                    sp.wait_ge(hot_ready, bp * 8 + (4 * half + 4))
                    load_orders(bp * 2 + (2 + half), half)

        @block.vector
        def _(dve):
            vec = nc.vector
            chain = Step(dve, step)
            link = chain.then_wait
            for t in range(RT):
                if t:
                    dve.wait_ge(split_ready, t)
                dve.wait_ge(turned_ready, t + 1)
                src = turned[:, t % 2, :].rearrange("p (c f) -> p c f", c=4)
                parts = by_point[:, :, t * BPT:(t + 1) * BPT, :, :].rearrange("p c q s f -> p s c q f")
                as_rows = [rest[:, i].rearrange("p c (q f) -> p c q f", q=BPT) for i in range(2)]
                part = [parts[:, s] for s in range(3)]
                link(vec.tensor_copy(rest[:, 0], src))
                for c in range(4):
                    ins = vec.tensor_copy(part[0][:, c], as_rows[0][:, c])
                link(ins)
                for s in (1, 2):
                    for c in range(4):
                        ins = vec.tensor_tensor(as_rows[s % 2][:, c], as_rows[(s + 1) % 2][:, c],
                                                part[s - 1][:, c], ALU.subtract)
                    link(ins)
                    for c in range(4):
                        ins = vec.tensor_copy(part[s][:, c], as_rows[s % 2][:, c])
                    if s == 1:
                        link(ins)
                ins.then_inc(split_ready, 1)

            def sum_parts(b, half):
                for rc in range(4):
                    dve.wait_ge(products_ready, b * 4 + (rc + 1))
                    vec.tensor_reduce(
                        gathered[:, half, rc, :], product_view(rc).rearrange("p s f -> p f s"),
                        AX_X, ALU.add).then_inc(gathered_ready, 1)

            def make_hot(pair, half):
                dve.wait_ge(order_in[half], pair * 16 + 16)
                for c in range(4):
                    vec.tensor_scalar(hot[:, half, c], ordered[:, half], g["point"][:, c:c + 1], None,
                                      ALU.is_equal).then_inc(hot_ready, 1)

            make_hot(0, 0)
            with dve.Fori(0, B // 2 - 1) as bp:
                make_hot(bp, 1)
                sum_parts(bp * 2, 0)
                make_hot(bp + 1, 0)
                sum_parts(bp * 2 + 1, 1)
            make_hot(B // 2 - 1, 1)
            sum_parts(B - 2, 0)
            sum_parts(B - 1, 1)
            vec.memset(sorted_rows[:, :, 0:BACK], 0.0)
            dve.wait_ge(rows_ready, B)
            vec.tensor_copy(sorted_rows[:, :, BACK + N:SW],
                            sorted_rows[:, :, BACK + N - 1:BACK + N].broadcast_to([P, B, SW - BACK - N]))

        @block.tensor
        def _(pe):
            for t in range(RT):
                pe.wait_ge(rows_in, 16 * B)
                if t >= 2:
                    pe.wait_ge(split_ready, t - 1)
                for c in range(4):
                    ins = nc.tensor.transpose(turned[:, t % 2, c * P:(c + 1) * P], rows[:, t, c * P:(c + 1) * P],
                                              g["ident"][:])
                ins.then_inc(turned_ready, 1)
            pe.wait_ge(split_ready, RT)

            def one_batch(b, half, first_batch=False):
                pe.wait_ge(hot_ready, b * 4 + 4)
                for rc in range(4):
                    if not first_batch:
                        pe.wait_ge(gathered_ready, b * 4 + (rc - 3))
                    for place in range(METHODS):
                        for c in range(4):
                            ins = nc.tensor.matmul(
                                product_view(rc).rearrange("p s (h m f) -> p m s h f", h=HEADS, m=METHODS)[:, place],
                                hot[:, half, c, perm[place], rc * P:(rc + 1) * P],
                                by_point[:, c, b, :, :].rearrange("p s (h f) -> p s h f", h=HEADS), start=(c == 0), stop=(c == 3))
                    ins.then_inc(products_ready, 1)

            def turn_batch(b, half, early=False):
                for rc in range(4):
                    pe.wait_ge(gathered_ready, b * 4 + (rc + 1))
                    if rc == 0 and not early:
                        pe.wait_ge(rows_ready, b * 1 - 1)
                    ins = nc.tensor.transpose(
                        turned[:, half, rc * P:(rc + 1) * P],
                        gathered[:, half, rc, :], g["ident"][:])
                ins.then_inc(window_turned, 1)

            one_batch(0, 0, True)
            one_batch(1, 1)
            turn_batch(0, 0, True)
            one_batch(2, 0)
            turn_batch(1, 1, True)
            with pe.Fori(1, B // 2 - 1) as bp:
                one_batch(bp * 2 + 1, 1)
                turn_batch(bp * 2, 0)
                one_batch(bp * 2 + 2, 0)
                turn_batch(bp * 2 + 1, 1)
            one_batch(B - 1, 1)
            turn_batch(B - 2, 0)
            turn_batch(B - 1, 1)

        @block.scalar
        def _(act):
            def copy_rows(b, half):
                act.wait_ge(window_turned, b + 1)
                nc.scalar.activation(sorted_rows[:, b, BACK:BACK + N], turned[:, half, :], ACT.Copy)\
                    .then_inc(rows_ready, 1)

            for b in range(B):
                copy_rows(b, b % 2)


def window_attention(nc, g, layer, sorted_rows, hmax, hstats):
    O = g["O"][layer]
    GO = P // O
    GH = STRIPS // GO
    feats = g["feats"]
    first = layer * C
    with ExitStack() as ctx:
        def sb(name, shape, dt):
            return ctx.enter_context(nc.sbuf_tensor(f"{name}_{layer}", shape, dt))

        def ps(name, shape):
            return ctx.enter_context(nc.psum_tensor(f"{name}_{layer}", shape, F32))

        handles = []

        def sem(name):
            handles.append(ctx.enter_context(nc.semaphore(f"{name}_{layer}")))
            return handles[-1]

        w_lin = sb("w_lin", [64, 2 * C * METHODS], F32)
        w_conv = sb("w_conv", [O, 64], F32)
        b_lin = sb("b_lin", [64, 1], F32)
        w_convT = sb("w_convT", [64, O], F32)
        w_lin_near = sb("w_lin_near", [64, HEADS, METHODS, 8], F32)
        w_near = sb("w_near", [P, 3, O], BF16)
        w_rest = sb("w_rest", [P, 2, O], F32)
        w_centre = sb("w_centre", [C + 1, O], F32)
        mask_row = sb("mask_row", [P, P], BF16)
        mask_col = sb("mask_col", [P, COLS], BF16)
        first_windows = sb("first_windows", [P, B, BACK, WIN], F32)
        centre = sb("centre", [P, 2, SP_PTS * STRIPS + PTS], F32)
        raw_centre = sb("raw_centre", [C, N + PTS], F32)
        half_centre = sb("half_centre", [C, N + PTS], F16)
        centre_in = sb("centre_in", [C + 1, N + PTS], F32)
        centre_out = sb("centre_out", [P, 2, GH, SP_PAD], F32)
        vectors = sb("vectors", [P, 2, COLS + 2], F16)
        by_head = sb("by_head", [P, 2, NBLK, HEADS, 32], F16)
        row_max = sb("row_max", [P, NBLK], F32)
        shifted = sb("shifted", [P, NBLK, 32], F32)
        probs = sb("probs", [P, 2, NBLK, 32], F32)
        row_sum = sb("row_sum", [P, NBLK], F32)
        row_inv = sb("row_inv", [P, 2, NBLK], F32)
        probsT = sb("probsT", [P, STRIPS, P], F32)
        mapped = sb("mapped", [P, 2, NBLK, O], F32)
        fused = sb("fused", [P, GH, SP_PAD * WIN], F32)
        piece = sb("piece", [P, GH, 4, 6], F32)
        scores = [ps(f"scores{i}", [P, 512]) for i in range(2)]
        ps_mapped = ps("ps_mapped", [P, NBLK, O])
        ps_probsT = ps("ps_probsT", [P, STRIPS, P])
        outs = [ps(f"outs{i}", [P, 512]) for i in range(2)]
        misc = ps("misc", [P, 512])

        weights_in = sem("weights_in")
        centre_loaded = [sem("centre_loaded0"), sem("centre_loaded1")]
        raw_loaded, masks_ready, zeros_ready = sem("raw_loaded"), sem("masks_ready"), sem("zeros_ready")
        conv_turned, conv_ready, joined, split_step = sem("conv_turned"), sem("conv_ready"), sem("joined"), sem("split_step")
        w_ready, near_ready, edge_ready = sem("w_ready"), sem("near_ready"), sem("edge_ready")
        vectors_ready, by_head_ready = sem("vectors_ready"), sem("by_head_ready")
        scores_ready, max_ready, shifted_ready = sem("scores_ready"), sem("max_ready"), sem("shifted_ready")
        exp_ready, sum_ready, inv_ready, probs_ready = sem("exp_ready"), sem("sum_ready"), sem("inv_ready"), sem("probs_ready")
        probs_turned, probsT_ready = sem("probs_turned"), sem("probsT_ready")
        mapped_done, mapped_ready = sem("mapped_done"), sem("mapped_ready")
        outs_ready, fused_ready, pieces_ready = sem("outs_ready"), sem("fused_ready"), sem("pieces_ready")
        batch_closed = sem("batch_closed")
        half_ready, centre_in_ready, centre_done, centre_out_ready = (
            sem("half_ready"), sem("centre_in_ready"), sem("centre_done"), sem("centre_out_ready"))
        ctx.callback(lambda: clear_semaphores(nc, handles))
        block = ctx.enter_context(nc.Block())

        BLOCKS = [(strip, sub) for strip in range(STRIPS) for sub in range(SUB)]

        def out_view(parity):
            return outs[parity][:, 0:GH * PTS * WIN].rearrange("p (g c) -> p g c", g=GH)

        def over_chunks(engine, chunk):
            with engine.Fori(0, B // 2) as pair:
                for half in range(2):
                    at = pair * (2 * CHUNKS) + half * CHUNKS
                    chunk(pair, half, 0, at, half, True)
                    with engine.Fori(0, (CHUNKS - 3) // 2) as i:
                        for j in (1, 2):
                            chunk(pair, half, i * 2 + j, at + (i * 2 + j), (half + j) % 2, False)
                    for k in (CHUNKS - 2, CHUNKS - 1):
                        chunk(pair, half, k, at + k, (half + k) % 2, True)

        @block.sync
        def _(sp):
            sp.dma_start(w_lin[:], g["w_lin"][layer]).then_inc(weights_in, 16)
            sp.dma_start(w_conv[:], g["w_conv"][layer]).then_inc(weights_in, 16)
            sp.dma_start(b_lin[:], g["b_lin"][layer].rearrange("(k a) -> k a", a=1)).then_inc(weights_in, 16)

            def load_centres(b, half):
                for h in range(HEADS):
                    src = bass.AP(feats.tensor, feats.offset + b * (P * N) + (first + 8 * h) * N,
                                  [[0, METHODS], [N, 8], [1, N]])
                    sp.dma_start(centre[32 * h:32 * h + 32, half, 0:N], src).then_inc(centre_loaded[half], 16)

            def load_raw(b):
                sp.dma_start(raw_centre[:, 0:N], bass.AP(feats.tensor, feats.offset + b * (P * N) + first * N,
                                                         [[N, C], [1, N]])).then_inc(raw_loaded, 16)

            load_centres(0, 0)
            load_raw(0)
            with sp.Fori(0, B // 2) as pair:
                for half in range(2):
                    b = pair * 2 + half
                    sp.wait_ge(vectors_ready, b * CHUNKS + 1)
                    load_centres((b + 1) % B, 1 - half)
                    sp.wait_ge(half_ready, b + 1)
                    load_raw((b + 1) % B)
            sp.wait_ge(centre_loaded[0], 64 * (B // 2 + 1))
            sp.wait_ge(raw_loaded, 16 * (B + 1))

        @block.gpsimd
        def _(pool):
            gp = nc.gpsimd
            gp.memset(mask_row[:], 0.0)
            gp.memset(mask_col[:], 0.0)
            gp.memset(centre[:, :, N:], 0.0)
            gp.memset(raw_centre[:, N:], 0.0)
            gp.memset(centre_in[:], 1.0)
            gp.memset(vectors[:, :, COLS:], 0.0)
            gp.memset(by_head[:], 0.0)
            gp.memset(shifted[:], 0.0)
            gp.memset(probs[:], 0.0).then_inc(zeros_ready, 1)
            pool.wait_ge(zeros_ready, 1)
            for t, (tile, blocks) in enumerate(((mask_row, SUB), (mask_col, NBLK))):
                width = 32 if t == 0 else BLK
                view = tile[0:32, :].rearrange("p (b c) -> p b c", b=blocks)
                for point in range(TRI):
                    part = view[:, :, point * WIN:(point + 1) * WIN]
                    ins = gp.affine_select(out=part, in_=part, compare_op=ALU.not_equal,
                                           fill=(MASK if t == 0 else 1.0), base=-(point + 1),
                                           pattern=[[0, blocks], [0, WIN]], channel_multiplier=1)
            ins.then_inc(zeros_ready, 1)
            pool.wait_ge(zeros_ready, 2)
            gp.memset(mask_row[0:1, :], -MASK)
            gp.memset(mask_col[0:1, :], 1.0).then_inc(masks_ready, 1)

            def normalise(pair, half, k, n, parity, peeled):
                pool.wait_ge(inv_ready, n + 1)
                view = probs[:, parity, :, 0:BLK]
                gp.tensor_tensor(view, view, row_inv[:, parity, :].unsqueeze(2).broadcast_to([P, NBLK, BLK]),
                                 ALU.mult).then_inc(probs_ready, 1)

            over_chunks(pool, normalise)

        @block.scalar
        def _(act):
            sc = nc.scalar
            act.wait_ge(conv_turned, 1)
            sc.activation(w_convT[:], misc[0:64, 0:O], ACT.Copy).then_inc(conv_ready, 1)

            def make_centre_in(pair_b):
                act.wait_ge(raw_loaded, pair_b * 16 + 16)
                sc.activation(half_centre[:], raw_centre[:], ACT.Copy).then_inc(half_ready, 1)
                act.wait_ge(half_ready, pair_b + 1)
                sc.activation(centre_in[0:C, :], half_centre[:], ACT.Copy).then_inc(centre_in_ready, 1)

            def copy_centre_out(b, half):
                act.wait_ge(centre_done, b + 1)
                sc.activation(centre_out[:, half], misc[:, 0:GH * SP_PAD].rearrange("p (g c) -> p g c", g=GH),
                              ACT.Copy).then_inc(centre_out_ready, 1)

            def copy_mapped(n, parity):
                act.wait_ge(mapped_done, n + 1)
                sc.activation(mapped[:, parity], ps_mapped[:], ACT.Copy).then_inc(mapped_ready, 1)

            act.wait_ge(zeros_ready, 1)
            make_centre_in(0)
            copy_centre_out(0, 0)
            copy_mapped(0, 0)

            def chunk(pair, half, k, n, parity, peeled):
                act.wait_ge(shifted_ready, n + 1)
                sc.activation(probs[:, parity, :, 0:BLK], shifted[:, :, 0:BLK], ACT.Exp, scale=1.0 / SQRT_HD)\
                    .then_inc(exp_ready, 1)
                copy_mapped(n + 1, 1 - parity)
                act.wait_ge(probs_turned, n + 1)
                sc.activation(probsT[:], ps_probsT[:], ACT.Copy).then_inc(probsT_ready, 1)
                if peeled and k == CHUNKS - 2:
                    make_centre_in(pair * 2 + (half + 1))
                if peeled and k == CHUNKS - 1:
                    copy_centre_out(pair * 2 + (half + 1), 1 - half)

            over_chunks(act, chunk)

        @block.tensor
        def _(pe):
            mm = nc.tensor.matmul
            pe.wait_ge(weights_in, 48)
            nc.tensor.transpose(misc[0:64, 0:O], w_conv[:], g["ident"][0:O, 0:O]).then_inc(conv_turned, 1)
            pe.wait_ge(conv_ready, 1)
            pe.wait_ge(near_ready, 1)
            mm(misc[:, 64:64 + O], w_lin_near[:].rearrange("k h m f -> k (h m f)"), w_convT[:],
               start=True, stop=True)
            for place in range(METHODS):
                mm(misc[0:C, 128:128 + O], w_lin[:, place:C * METHODS:METHODS], w_convT[:],
                   start=(place == 0), stop=(place == METHODS - 1))
            mm(misc[C:C + 1, 128:128 + O], b_lin[:], w_convT[:], start=True, stop=True).then_inc(joined, 1)

            def make_centre_out():
                for strip in range(STRIPS):
                    go, gh = strip % GO, strip // GO
                    ins = mm(misc[go * O:(go + 1) * O, gh * SP_PAD:(gh + 1) * SP_PAD], w_centre[:],
                             centre_in[:, strip * SP_PTS:strip * SP_PTS + SP_PAD], start=True, stop=True)
                ins.then_inc(centre_done, 1)

            def make_scores(parity):
                mm(scores[parity][:, 0:COLS], mask_row[:], mask_col[:], start=True, stop=False,
                   skip_group_check=True)
                for block_, (strip, sub) in enumerate(BLOCKS):
                    out = scores[parity][32 * sub:32 * sub + 32, strip * HEADS * BLK:(strip + 1) * HEADS * BLK]
                    ins = mm(out.rearrange("p (h c) -> p h c", h=HEADS),
                             vectors[:, parity, block_ * BLK:block_ * BLK + 32],
                             by_head[:, parity, block_, :, 0:BLK], start=False, stop=(block_ >= NBLK - SUB),
                             skip_group_check=True)
                ins.then_inc(scores_ready, 1)

            def map_vectors(parity):
                for block_ in range(NBLK):
                    for part in range(3):
                        ins = mm(ps_mapped[:, block_, :],
                                 by_head[:, parity, block_, :, :].rearrange("p h c -> p (h c)"),
                                 w_near[:, part, :], start=(part == 0), stop=(part == 2))
                ins.then_inc(mapped_done, 1)

            pe.wait_ge(w_ready, 1)
            pe.wait_ge(centre_in_ready, 1)
            make_centre_out()
            pe.wait_ge(masks_ready, 1)
            pe.wait_ge(by_head_ready, 1)
            make_scores(0)
            map_vectors(0)

            def chunk(pair, half, k, n, parity, peeled):
                pe.wait_ge(by_head_ready, n + 2)
                make_scores(1 - parity)
                pe.wait_ge(mapped_ready, n + 1)
                map_vectors(1 - parity)
                if peeled and k == CHUNKS - 1:
                    pe.wait_ge(centre_in_ready, pair * 2 + (half + 2))
                    pe.wait_ge(centre_out_ready, pair * 2 + (half + 1))
                pe.wait_ge(probs_ready, n + 1)
                for strip in range(STRIPS):
                    ins = nc.tensor.transpose(
                        ps_probsT[:, strip, :],
                        probs[:, parity, strip * HEADS:(strip + 1) * HEADS, :].rearrange("p h c -> p (h c)"),
                        g["ident"][:])
                ins.then_inc(probs_turned, 1)
                pe.wait_ge(probsT_ready, n + 1)
                for block_, (strip, sub) in enumerate(BLOCKS):
                    go, gh = strip % GO, strip // GO
                    ins = mm(out_view(parity)[go * O:(go + 1) * O, gh, sub * BLK:(sub + 1) * BLK],
                             mapped[:, parity, block_, :], probsT[:, strip, 32 * sub:32 * sub + BLK],
                             start=True, stop=True)
                ins.then_inc(outs_ready, 1)
                if peeled and k == CHUNKS - 1:
                    make_centre_out()

            over_chunks(pe, chunk)

        @block.vector
        def _(dve):
            vec = nc.vector
            chain = Step(dve, split_step)
            link = chain.then_wait
            dve.wait_ge(weights_in, 48)
            vec.tensor_copy(w_lin_near[:], w_lin[:, C * METHODS:].rearrange("k (h f m) -> k h m f", h=HEADS,
                                                                            m=METHODS)).then_inc(near_ready, 1)
            link(vec.tensor_copy(first_windows[:], bass.AP(sorted_rows.tensor, sorted_rows.offset + BACK,
                                                           [sorted_rows.ap[0], [SW, B], [0, BACK], [1, WIN]])))
            for i in range(BACK - 1):
                n_last = WIN - (i + BACK + 1)
                ins = vec.tensor_copy(first_windows[:, :, i, i + BACK + 1:WIN],
                                      sorted_rows[:, :, 2 * BACK + i:2 * BACK + i + 1].broadcast_to([P, B, n_last]))
            link(ins)
            dve.wait_ge(joined, 1)
            near_map = misc[:, 64:64 + O]
            link(vec.tensor_copy(w_near[:, 0], near_map))
            link(vec.tensor_tensor(w_rest[:, 0], near_map, w_near[:, 0], ALU.subtract))
            link(vec.tensor_copy(w_near[:, 1], w_rest[:, 0]))
            link(vec.tensor_tensor(w_rest[:, 1], w_rest[:, 0], w_near[:, 1], ALU.subtract))
            vec.tensor_copy(w_near[:, 2], w_rest[:, 1])
            vec.tensor_copy(w_centre[:], misc[0:C + 1, 128:128 + O]).then_inc(w_ready, 1)

            def make_vectors(b, half, k, count, parity, batch_count=None):
                rows = bass.AP(sorted_rows.tensor, sorted_rows.offset + b * SW + k * PTS,
                               [sorted_rows.ap[0], [SP_PTS, STRIPS], [1, PTS], [1, WIN]])
                row = centre[:, half, 0:1]
                mids = bass.AP(row.tensor, row.offset + k * PTS,
                               [row.ap[0], [SP_PTS, STRIPS], [1, PTS], [0, WIN]])
                vec.tensor_tensor(vectors[:, parity, 0:COLS].rearrange("p (s c j) -> p s c j", s=STRIPS, c=PTS),
                                  rows, mids, ALU.subtract).then_inc(vectors_ready, 1)
                dve.wait_ge(vectors_ready, count)
                if batch_count is not None:
                    whole = first_windows[:]
                    starts = bass.AP(whole.tensor, whole.offset + b * (BACK * WIN),
                                     [whole.ap[0], [WIN, BACK], [1, WIN]])
                    vec.tensor_tensor(vectors[:, parity, 0:BACK * WIN].rearrange("p (i j) -> p i j", i=BACK), starts,
                                      centre[:, half, 0:BACK].unsqueeze(2).broadcast_to([P, BACK, WIN]),
                                      ALU.subtract).then_inc(edge_ready, 1)
                    dve.wait_ge(edge_ready, batch_count)
                for h in range(HEADS):
                    at = slice(32 * h, 32 * h + 32)
                    ins = vec.tensor_copy(by_head[at, parity, :, h, 0:BLK],
                                          vectors[at, parity, 0:COLS].rearrange("p (b c) -> p b c", b=NBLK))
                ins.then_inc(by_head_ready, 1)

            def fuse(parity, k, n, half):
                dve.wait_ge(outs_ready, n + 1)
                row = centre_out[:, half, 0:1, 0:1]
                mids = bass.AP(row.tensor, row.offset + k * PTS, [row.ap[0], [SP_PAD, GH], [1, PTS], [0, WIN]])
                row = fused[:, 0:1, 0:1]
                dst = bass.AP(row.tensor, row.offset + k * (PTS * WIN),
                              [row.ap[0], [SP_PAD * WIN, GH], [WIN, PTS], [1, WIN]])
                vec.tensor_tensor(dst, out_view(parity).rearrange("p g (c j) -> p g c j", c=PTS), mids,
                                  ALU.add).then_inc(fused_ready, 1)

            dve.wait_ge(zeros_ready, 1)
            dve.wait_ge(centre_loaded[0], 64)
            make_vectors(0, 0, 0, 1, 0, 1)

            def chunk(pair, half, k, n, parity, peeled):
                b = pair * 2 + half
                first_of_batch = peeled and k == 0
                last_of_batch = peeled and k == CHUNKS - 1
                dve.wait_ge(scores_ready, n + 1)
                view = scores[parity][:, 0:COLS].rearrange("p (b c) -> p b c", b=NBLK)
                vec.tensor_reduce(row_max[:], view, AX_X, ALU.max).then_inc(max_ready, 1)
                dve.wait_ge(max_ready, n + 1)
                vec.tensor_tensor(shifted[:, :, 0:BLK], view, row_max[:].unsqueeze(2).broadcast_to([P, NBLK, BLK]),
                                  ALU.subtract).then_inc(shifted_ready, 1)
                if last_of_batch:
                    dve.wait_ge(centre_loaded[1 - half], pair * 64 + 64 * (1 + half))
                    make_vectors((b + 1) % B, 1 - half, 0, n + 2, 1 - parity, b + 2)
                else:
                    make_vectors(b, half, k + 1, n + 2, 1 - parity)
                if first_of_batch:
                    dve.wait_ge(centre_out_ready, b + 1)
                else:
                    fuse(1 - parity, k - 1, n - 1, half)
                dve.wait_ge(exp_ready, n + 1)
                vec.tensor_reduce(row_sum[:], probs[:, parity, :, 0:BLK], AX_X, ALU.add).then_inc(sum_ready, 1)
                dve.wait_ge(sum_ready, n + 1)
                vec.reciprocal(row_inv[:, parity, :], row_sum[:]).then_inc(inv_ready, 1)
                if last_of_batch:
                    fuse(parity, k, n, half)
                    dve.wait_ge(fused_ready, n + 1)
                    for gh in range(GH):
                        for q in range(4):
                            w = SP_PTS * WIN // 4
                            ins = vec.bn_stats(piece[:, gh, q, :], fused[:, gh, q * w:(q + 1) * w])
                    ins.then_inc(pieces_ready, 1)
                    vec.tensor_reduce(hmax[:, b, :, :], fused[:, :, 0:SP_PTS * WIN]
                                      .rearrange("p g (c j) -> p g c j", j=WIN), AX_X, ALU.max)
                    dve.wait_ge(pieces_ready, b + 1)
                    vec.tensor_scalar(hstats[:, b], piece[:].rearrange("p g q s -> p (g q s)"), 1.0, None,
                                      ALU.mult).then_inc(batch_closed, 1)

            over_chunks(dve, chunk)


def close_layer(nc, g, layer, hmax, hstats):
    O = g["O"][layer]
    GO = P // O
    GH = STRIPS // GO
    dst = C if layer == 0 else 2 * C
    with ExitStack() as ctx:
        def sb(name, shape):
            return ctx.enter_context(nc.sbuf_tensor(f"{name}_{layer}", shape, F32))

        handles = []

        def sem(name):
            handles.append(ctx.enter_context(nc.semaphore(f"{name}_{layer}")))
            return handles[-1]

        strip_stats = sb("strip_stats", [P, B, GH, 2])
        mean = sb("mean", [P, B])
        away = sb("away", [P, B, GH])
        var = sb("var", [P, B])
        rstd = sb("norm_rstd", [P, B])
        work = sb("norm_work", [P, 3, B])
        relu = sb("relu", [P, B, GH, SP_PTS])
        sums = ctx.enter_context(nc.psum_tensor(f"sums_{layer}", [P, 2, 512], F32))
        step, aggregated, mean_done, spread_ready, var_done = (
            sem("close_step"), sem("aggregated"), sem("mean_done"), sem("spread_ready"), sem("var_done"))
        eps_ready, std_ready, relu_ready, stored = sem("eps_ready"), sem("std"), sem("relu_ready"), sem("feats_stored")
        newton = Newton(nc, [work[:, i, :] for i in range(3)], std_ready)
        ctx.callback(lambda: clear_semaphores(nc, handles))
        block = ctx.enter_context(nc.Block())

        @block.tensor
        def _(pe):
            pe.wait_ge(aggregated, 1)
            for gh in range(GH):
                ins = nc.tensor.matmul(sums[:, 0, 0:B], g["average"][layer][:], strip_stats[:, :, gh, 0],
                                       start=(gh == 0), stop=(gh == GH - 1))
            ins.then_inc(mean_done, 1)
            pe.wait_ge(spread_ready, 1)
            for gh in range(GH):
                ins = nc.tensor.matmul(sums[:, 1, 0:B], g["average"][layer][:], strip_stats[:, :, gh, 1],
                                       start=(gh == 0), stop=(gh == GH - 1))
            ins.then_inc(var_done, 1)

        @block.scalar
        def _(act):
            newton.on_scalar(act, eps_ready, 1, 1)

        @block.vector
        def _(dve):
            vec = nc.vector
            chain = Step(dve, step)
            link = chain.then_wait
            for b in range(B):
                for gh in range(GH):
                    ins = vec.bn_aggr(strip_stats[:, b, gh, :], hstats[:, b, gh * 24:(gh + 1) * 24])
            ins.then_inc(aggregated, 1)
            dve.wait_ge(mean_done, 1)
            link(vec.tensor_copy(mean[:], sums[:, 0, 0:B]))
            link(vec.tensor_tensor(away[:], strip_stats[:, :, :, 0], mean[:].unsqueeze(2).broadcast_to([P, B, GH]),
                                   ALU.subtract))
            link(vec.tensor_tensor(away[:], away[:], away[:], ALU.mult))
            vec.tensor_tensor(strip_stats[:, :, :, 1], strip_stats[:, :, :, 1], away[:], ALU.add)\
                .then_inc(spread_ready, 1)
            dve.wait_ge(var_done, 1)
            link(vec.tensor_copy(var[:], sums[:, 1, 0:B]))
            newton.on_vector(dve, link, var[:], rstd[:], eps_ready, 1)
            for b in range(B):
                ins = vec.tensor_scalar(hmax[:, b], hmax[:, b], mean[:, b:b + 1], rstd[:, b:b + 1],
                                        ALU.subtract, ALU.mult)
            link(ins)
            flat = "p b g n -> p (b g n)"
            vec.scalar_tensor_tensor(relu[:].rearrange(flat), hmax.rearrange(flat), 0.2, hmax.rearrange(flat),
                                     ALU.mult, ALU.max).then_inc(relu_ready, 1)

        @block.sync
        def _(sp):
            sp.wait_ge(relu_ready, 1)
            for strip in range(STRIPS):
                go, gh = strip % GO, strip // GO
                sp.dma_start(g["feats"][:, dst:dst + O, strip * SP_PTS:(strip + 1) * SP_PTS]
                             .rearrange("b o n -> o b n"), relu[go * O:(go + 1) * O, :, gh, :]).then_inc(stored, 16)
            sp.wait_ge(stored, 16 * STRIPS)


def mix_features(nc, g, x1, query):
    with ExitStack() as ctx:
        def sb(name, shape):
            return ctx.enter_context(nc.sbuf_tensor(name, shape, F32))

        handles = []

        def sem(name):
            handles.append(ctx.enter_context(nc.semaphore(name)))
            return handles[-1]

        mixed = sb("mixed", [P, B, N])
        w_mix = sb("w_mix", [C, P])
        w_mixT = sb("w_mixT", [P, C])
        x_rows = sb("x_rows", [P, RT, N])
        stats = sb("mix_stats", [P, RT, 6])
        mean_var = sb("mix_mean_var", [P, RT, 2])
        rstd = sb("mix_rstd", [P, RT])
        work = sb("mix_work", [P, 3, RT])
        fused = sb("mix_fused", [P, RT, N])
        normed = sb("mix_normed", [P, RT, N])
        products = ctx.enter_context(nc.psum_tensor("mix_products", [P, RT, N], F32))
        turned = ctx.enter_context(nc.psum_tensor("mix_turned", [P, 512], F32))
        w_in, x_in = sem("w_in"), sem("x_in")
        mixed_in = [sem(f"mixed_in{t}") for t in range(RT)]
        w_turned, w_ready, products_ready = sem("w_turned"), sem("mix_w_ready"), sem("mix_products_ready")
        step, eps_ready, std_ready, normed_ready, stored = (
            sem("mix_step"), sem("mix_eps"), sem("mix_std"), sem("mix_normed_ready"), sem("query_stored"))
        newton = Newton(nc, [work[:, i, :] for i in range(3)], std_ready)
        ctx.callback(lambda: clear_semaphores(nc, handles))
        block = ctx.enter_context(nc.Block())

        @block.sync
        def _(sp):
            sp.dma_start(w_mix[:], g["w_mix"]).then_inc(w_in, 16)
            for t in range(RT):
                sp.dma_start(mixed[:, t * BPT:(t + 1) * BPT, :],
                             g["feats"][t * BPT:(t + 1) * BPT].rearrange("b f n -> f b n")).then_inc(mixed_in[t], 16)
            sp.dma_start(x_rows[:], g["x"].rearrange("(t q) c n -> (q c) t n", q=BPT)).then_inc(x_in, 16)
            sp.wait_ge(normed_ready, 1)
            for q in range(BPT):
                sp.dma_start(query.rearrange("(t q) c n -> q c t n", q=BPT)[q], normed[q * C:(q + 1) * C])\
                    .then_inc(stored, 16)
            sp.wait_ge(stored, 16 * BPT)

        @block.tensor
        def _(pe):
            pe.wait_ge(w_in, 16)
            nc.tensor.transpose(turned[:, 0:C], w_mix[:], g["ident"][0:C, 0:C]).then_inc(w_turned, 1)
            pe.wait_ge(w_ready, 1)
            for t in range(RT):
                pe.wait_ge(mixed_in[t], 16)
                for q in range(BPT):
                    ins = nc.tensor.matmul(products[q * C:(q + 1) * C, t, :], w_mixT[:], mixed[:, t * BPT + q, :],
                                           start=True, stop=True)
                ins.then_inc(products_ready, 1)

        @block.scalar
        def _(act):
            act.wait_ge(w_turned, 1)
            nc.scalar.activation(w_mixT[:], turned[:, 0:C], ACT.Copy).then_inc(w_ready, 1)
            newton.on_scalar(act, eps_ready, 1, 1)
            newton.on_scalar(act, eps_ready, 2, 2)

        @block.vector
        def _(dve):
            vec = nc.vector
            chain = Step(dve, step)
            link = chain.then_wait

            def row_stats(tiles):
                for t in range(RT):
                    if tiles is products:
                        dve.wait_ge(products_ready, t + 1)
                    ins = vec.bn_stats(stats[:, t, :], tiles[:, t, :])
                link(ins)
                for t in range(RT):
                    ins = vec.bn_aggr(mean_var[:, t, :], stats[:, t, :])
                link(ins)

            row_stats(products)
            newton.on_vector(dve, link, mean_var[:, :, 1], rstd[:], eps_ready, 1)
            for t in range(RT):
                ins = vec.tensor_scalar(fused[:, t, :], products[:, t, :], mean_var[:, t, 0:1], rstd[:, t:t + 1],
                                        ALU.subtract, ALU.mult)
            link(ins)
            dve.wait_ge(x_in, 16)
            flat = "p t n -> p (t n)"
            link(vec.scalar_tensor_tensor(fused[:].rearrange(flat), fused[:].rearrange(flat), 0.2,
                                          fused[:].rearrange(flat), ALU.mult, ALU.max))
            link(vec.tensor_tensor(x1[:], x_rows[:], fused[:], ALU.add))
            row_stats(x1)
            newton.on_vector(dve, link, mean_var[:, :, 1], rstd[:], eps_ready, 2)
            for t in range(RT):
                ins = vec.tensor_scalar(normed[:, t, :], x1[:, t, :], mean_var[:, t, 0:1], rstd[:, t:t + 1],
                                        ALU.subtract, ALU.mult)
            ins.then_inc(normed_ready, 1)


def batch_attention(nc, g, query, message):
    QL = N // 4
    STEPS, SPAN = 4, QL // 4
    ITS, GROUPS, PAIR = SPAN // 8, 4, 2
    with ExitStack() as ctx:
        def sb(name, shape):
            return ctx.enter_context(nc.sbuf_tensor(name, shape, F32))

        handles = []

        def sem(name):
            handles.append(ctx.enter_context(nc.semaphore(name)))
            return handles[-1]

        queries = sb("queries", [P, B, QL])
        stage = sb("stage", [P, SPAN, B])
        values = sb("values", [P, ITS, P])
        row_max = sb("b_row_max", [P, 4 * ITS])
        logits = sb("logits", [P, 4, ITS, 32])
        row_sum = sb("b_row_sum", [P, 4 * ITS])
        attn = sb("attn", [P, 4, ITS, 32])
        attnT = sb("attnT", [P, 4, ITS, 32])
        said = sb("said", [P, B, QL])
        banks = ctx.enter_context(nc.psum_tensor("attn_banks", [P, 4, 512], F32))
        turned = ctx.enter_context(nc.psum_tensor("attn_turned", [P, ITS, P], F32))
        queries_in, stage_ready, mask_ready = sem("queries_in"), sem("stage_ready"), sem("apart_ready")
        scored, turned_ready, values_ready = sem("scored"), sem("values_turned"), sem("values_ready")
        logits_ready, exp_ready, attnT_ready, weighed, said_ready, stored = (
            sem("logits_ready"), sem("b_exp_ready"), sem("attnT_ready"), sem("weighed"), sem("said_ready"),
            sem("message_stored"))
        chained = sem("softmax_step")
        ctx.callback(lambda: clear_semaphores(nc, handles))
        block = ctx.enter_context(nc.Block())
        LINKS = 7

        @block.sync
        def _(sp):
            for quarter in range(4):
                sp.dma_start(queries[quarter * C:(quarter + 1) * C, :, :],
                             query[:, :, quarter * QL:(quarter + 1) * QL].rearrange("b c l -> c b l"))\
                    .then_inc(queries_in, 16)
            sp.wait_ge(said_ready, STEPS * GROUPS)
            for quarter in range(4):
                sp.dma_start(message[:, :, quarter * QL:(quarter + 1) * QL].rearrange("b c l -> c b l"),
                             said[quarter * C:(quarter + 1) * C, :, :]).then_inc(stored, 16)
            sp.wait_ge(stored, 64)

        @block.tensor
        def _(pe):
            for i in range(STEPS):
                pe.wait_ge(stage_ready, i + 1)
                for run in range(ITS):
                    ins = nc.tensor.transpose(turned[:, run, :], stage[:, run * 8:(run + 1) * 8, :]
                                              .rearrange("p l b -> p (l b)"), g["ident"][:])
                ins.then_inc(turned_ready, 1)
                for run in range(ITS):
                    for quarter in range(4):
                        for group in range(GROUPS):
                            at = run * 8 + group * PAIR
                            pair = stage[32 * quarter:32 * quarter + 32, at:at + PAIR, :].rearrange("p l b -> p (l b)")
                            ins = nc.tensor.matmul(
                                banks[32 * group:32 * group + 32, quarter, run * 32:run * 32 + 32], pair, pair,
                                start=True, stop=True)
                ins.then_inc(scored, 1)
                pe.wait_ge(values_ready, i + 1)
                pe.wait_ge(attnT_ready, i + 1)
                for run in range(ITS):
                    for quarter in range(4):
                        for group in range(GROUPS):
                            rows = slice(32 * group, 32 * group + 32)
                            ins = nc.tensor.matmul(
                                banks[32 * quarter:32 * quarter + 32, group, 256 + run * 32:256 + run * 32 + 32],
                                values[rows, run, 32 * quarter:32 * quarter + 32], attnT[rows, quarter, run, :],
                                start=True, stop=True)
                ins.then_inc(weighed, 1)

        @block.scalar
        def _(act):
            with act.Fori(0, STEPS) as i:
                act.wait_ge(turned_ready, i + 1)
                nc.scalar.activation(values[:], turned[:], ACT.Copy).then_inc(values_ready, 1)
                act.wait_ge(logits_ready, i + 1)
                nc.scalar.activation(attn[:], logits[:], ACT.Exp).then_inc(exp_ready, 1)

        @block.vector
        def _(dve):
            vec = nc.vector
            dve.wait_ge(queries_in, 64)
            whole = queries[:]
            with dve.Fori(0, STEPS) as i:
                vec.tensor_copy(stage[:], bass.AP(whole.tensor, whole.offset + i * SPAN,
                                                  [whole.ap[0], [1, SPAN], [QL, B]])).then_inc(stage_ready, 1)
                link = LoopStep(dve, chained, i, 5)
                dve.wait_ge(scored, i + 1)
                flat = "p q r c -> p (q r) c"
                link(vec.scalar_tensor_tensor(logits[:].rearrange("p q r c -> p q (r c)"), banks[:, :, 0:ITS * 32],
                                              1.0 / SQRT_HD, g["apart"][:].unsqueeze(1).broadcast_to([P, 4, ITS * 32]),
                                              ALU.mult, ALU.add))
                link(vec.tensor_reduce(row_max[:], logits[:].rearrange(flat), AX_X, ALU.max))
                vec.tensor_tensor(logits[:].rearrange(flat), logits[:].rearrange(flat),
                                  row_max[:].unsqueeze(2).broadcast_to([P, 4 * ITS, 32]), ALU.subtract)\
                    .then_inc(logits_ready, 1)
                dve.wait_ge(exp_ready, i + 1)
                link(vec.tensor_reduce(row_sum[:], attn[:].rearrange(flat), AX_X, ALU.add))
                link(vec.reciprocal(row_sum[:], row_sum[:]))
                link(vec.tensor_tensor(attn[:].rearrange(flat), attn[:].rearrange(flat),
                                       row_sum[:].unsqueeze(2).broadcast_to([P, 4 * ITS, 32]), ALU.mult))
                vec.transpose(attnT[:].rearrange("p q r c -> p (q r c)"), attn[:].rearrange("p q r c -> p (q r c)"))\
                    .then_inc(attnT_ready, 1)
                dve.wait_ge(weighed, i + 1)
                for group in range(GROUPS):
                    there, here = (bass.AP(tile.tensor, tile.offset + (i * SPAN + group * PAIR),
                                           [tile.ap[0], [8, ITS], [1, PAIR], [QL, B]]) for tile in (said[:], whole))
                    vec.tensor_tensor(there, banks[:, group, 256:256 + ITS * 32]
                                      .rearrange("p (r l b) -> p r l b", r=ITS, l=PAIR), here, ALU.add)\
                        .then_inc(said_ready, 1)


def feed_forward(nc, g, x1, message, out):
    HC, FC = H // P, FF // P
    with ExitStack() as ctx:
        def sb(name, shape):
            return ctx.enter_context(nc.sbuf_tensor(name, shape, F32))

        handles = []

        def sem(name):
            handles.append(ctx.enter_context(nc.semaphore(name)))
            return handles[-1]

        x2 = sb("x2", [P, RT, N])
        stats = sb("ff_stats", [P, RT, 6])
        mean_var = sb("ff_mean_var", [P, RT, 2])
        rstd = sb("ff_rstd", [P, RT])
        work = sb("ff_work", [P, 3, RT])
        normed = sb("ff_normed", [P, RT, H])
        normedT = sb("normedT", [P, HC, RT * P])
        sig = sb("sig", [P, 2, RT * P])
        silu = sb("silu", [P, 2, RT * P])
        hidden = sb("hidden", [P, FC, RT * P])
        result = sb("result", [P, RT, H])
        banks = ctx.enter_context(nc.psum_tensor("ff_banks", [P, 8, 512], F32))
        said_in, step, eps_ready, std_ready = sem("said_in"), sem("ff_step"), sem("ff_eps"), sem("ff_std")
        normed_ready, turned_ready, normedT_ready = sem("ff_normed_ready"), sem("ff_turned"), sem("normedT_ready")
        gated, sig_ready, silu_ready, hidden_ready = sem("gated"), sem("sig_ready"), sem("silu_ready"), sem("hidden_ready")
        down_done, result_ready, out_stored = sem("down_done"), sem("result_ready"), sem("out_stored")
        newton = Newton(nc, [work[:, i, :] for i in range(3)], std_ready)
        block = ctx.enter_context(nc.Block())

        @block.sync
        def _(sp):
            for q in range(BPT):
                sp.dma_start(x2[q * C:(q + 1) * C], message.rearrange("(t q) c n -> q c t n", q=BPT)[q])\
                    .then_inc(said_in, 16)
            for t in range(RT):
                sp.wait_ge(result_ready, t + 1)
                for q in range(BPT):
                    sp.dma_start(out[t * BPT + q], result[q * C:(q + 1) * C, t, :]).then_inc(out_stored, 16)
            sp.wait_ge(out_stored, 16 * B)

        @block.tensor
        def _(pe):
            for t in range(RT):
                pe.wait_ge(normed_ready, t + 1)
                for c in range(HC):
                    ins = nc.tensor.transpose(banks[:, t, c * P:(c + 1) * P], normed[:, t, c * P:(c + 1) * P],
                                              g["ident"][:])
                ins.then_inc(turned_ready, 1)
            pe.wait_ge(normedT_ready, RT)
            for f in range(FC):
                if f >= 2:
                    pe.wait_ge(hidden_ready, f - 1)
                for bank, w in ((4 + f % 2, g["gateT"]), (6 + f % 2, g["upT"])):
                    for c in range(HC):
                        ins = nc.tensor.matmul(banks[:, bank, :], w[:, c, f * P:(f + 1) * P], normedT[:, c, :],
                                               start=(c == 0), stop=(c == HC - 1))
                ins.then_inc(gated, 1)
            for t in range(RT):
                for f in range(FC):
                    if t == 0:
                        pe.wait_ge(hidden_ready, f + 1)
                    ins = nc.tensor.matmul(banks[:, t, :], hidden[:, f, t * P:(t + 1) * P], g["downT"][:, f, :],
                                           start=(f == 0), stop=(f == FC - 1))
                ins.then_inc(down_done, 1)

        @block.scalar
        def _(act):
            newton.on_scalar(act, eps_ready, 1, 1)
            for t in range(RT):
                act.wait_ge(turned_ready, t + 1)
                nc.scalar.activation(normedT[:, :, t * P:(t + 1) * P],
                                     banks[:, t, :].rearrange("p (c k) -> p c k", c=HC), ACT.Copy)\
                    .then_inc(normedT_ready, 1)
            for f in range(FC):
                act.wait_ge(gated, f + 1)
                if f >= 2:
                    act.wait_ge(silu_ready, f - 1)
                nc.scalar.activation(sig[:, f % 2], banks[:, 4 + f % 2, :], ACT.Sigmoid).then_inc(sig_ready, 1)

        @block.vector
        def _(dve):
            vec = nc.vector
            chain = Step(dve, step)
            link = chain.then_wait
            dve.wait_ge(said_in, 16 * BPT)
            link(vec.tensor_tensor(x2[:], x2[:], x1[:], ALU.add))
            for t in range(RT):
                ins = vec.bn_stats(stats[:, t, :], x2[:, t, :])
            link(ins)
            for t in range(RT):
                ins = vec.bn_aggr(mean_var[:, t, :], stats[:, t, :])
            link(ins)
            newton.on_vector(dve, link, mean_var[:, :, 1], rstd[:], eps_ready, 1)
            for t in range(RT):
                vec.tensor_scalar(normed[:, t, :], x2[:, t, :], mean_var[:, t, 0:1], rstd[:, t:t + 1],
                                  ALU.subtract, ALU.mult).then_inc(normed_ready, 1)
            for f in range(FC):
                dve.wait_ge(sig_ready, f + 1)
                vec.tensor_tensor(silu[:, f % 2], sig[:, f % 2], banks[:, 4 + f % 2, :], ALU.mult)\
                    .then_inc(silu_ready, 1)
                dve.wait_ge(silu_ready, f + 1)
                vec.tensor_tensor(hidden[:, f, :], silu[:, f % 2], banks[:, 6 + f % 2, :], ALU.mult)\
                    .then_inc(hidden_ready, 1)
            for t in range(RT):
                dve.wait_ge(down_done, t + 1)
                vec.tensor_tensor(result[:, t, :], banks[:, t, :], x2[:, t, :], ALU.add).then_inc(result_ready, 1)


def setup_constants(nc, g):
    with ExitStack() as ctx:
        done = ctx.enter_context(nc.semaphore("constants_step"))
        made = ctx.enter_context(nc.semaphore("partition_bit"))
        number = ctx.enter_context(nc.sbuf_tensor("partition_number", [P, P], I32))
        ctx.callback(lambda: clear_semaphores(nc, [done, made]))
        block = ctx.enter_context(nc.Block())

        @block.gpsimd
        def _(pool):
            gp = nc.gpsimd
            count = 0
            gp.iota(number[:], pattern=[[0, P]], base=0, channel_multiplier=1).then_inc(made, 1)
            gp.iota(g["point"][:], pattern=[[P, 4]], base=0, channel_multiplier=1,
                    allow_small_or_imprecise_dtypes=True)
            for tile, period, value in ((g["ident"], P, 1.0), (g["average"][0], g["O"][0], 1.0 / STRIPS),
                                        (g["average"][1], g["O"][1], 1.0 / STRIPS)):
                ins = gp.memset(tile[:], 0.0)
                for shift in range(-(P // period - 1) * period, P, period):
                    count += 1
                    ins.then_inc(done, 1)
                    pool.wait_ge(done, count)
                    ins = gp.affine_select(out=tile[:], in_=tile[:], compare_op=ALU.not_equal, fill=value,
                                           base=shift, pattern=[[-1, P]], channel_multiplier=1)

        @block.vector
        def _(dve):
            vec = nc.vector
            chain = Step(dve, made)
            chain.count = 1
            dve.wait_ge(made, 1)
            chain.then_wait(vec.tensor_scalar(number[:], number[:], 4, 1, ALU.logical_shift_right, ALU.bitwise_and))
            halves = [v[:].rearrange("p (r j b) -> p r j b", j=2, b=B) for v in (g["apart"], number)]
            vec.tensor_scalar(halves[0][:, :, 0, :], halves[1][:, :, 0, :], -MASK, None, ALU.mult)
            vec.tensor_scalar(halves[0][:, :, 1, :], halves[1][:, :, 1, :], MASK, -MASK, ALU.mult, ALU.add)


def program(nc, g, out):
    g["O"] = (C, 2 * C)
    with ExitStack() as ctx:
        def sb(name, shape, dt=F32):
            return ctx.enter_context(nc.sbuf_tensor(name, shape, dt))

        g["feats"] = nc.dram_tensor("feats_scratch", [B, P, N], F32).ap()
        g["orders"] = nc.dram_tensor("orders_scratch", [METHODS * B, N], F16).ap()
        query = nc.dram_tensor("query_scratch", [B, C, N], F32).ap()
        message = nc.dram_tensor("message_scratch", [B, C, N], F32).ap()
        g["gateT"] = sb("gateT", [P, H // P, FF])
        g["upT"] = sb("upT", [P, H // P, FF])
        g["downT"] = sb("downT", [P, FF // P, H])
        g["ident"] = sb("ident", [P, P])
        g["average"] = [sb("average0", [P, P]), sb("average1", [P, P])]
        g["point"] = sb("point", [P, 4])
        g["apart"] = sb("apart", [P, P])
        setup_constants(nc, g)
        sort_and_prepare(nc, g)
        for layer in range(2):
            strips = P // g["O"][layer]
            with nc.sbuf_tensor(f"sorted_rows_{layer}", [P, B, SW], F32) as sorted_rows, \
                 nc.sbuf_tensor(f"hmax_{layer}", [P, B, STRIPS // strips, SP_PTS], F32) as hmax, \
                 nc.sbuf_tensor(f"hstats_{layer}", [P, B, STRIPS // strips * 24], F32) as hstats:
                gather_windows(nc, g, layer, sorted_rows[:])
                window_attention(nc, g, layer, sorted_rows[:], hmax[:], hstats[:])
                close_layer(nc, g, layer, hmax[:], hstats[:])
        x1 = sb("x1", [P, RT, N])
        mix_features(nc, g, x1, query)
        batch_attention(nc, g, query, message)
        feed_forward(nc, g, x1, message, out)


_INS = ["x", "ctx_4096", "L0_xattn_W_lin1", "L0_xattn_b_lin1", "L0_xattn_W_lin2", "L0_xattn_b_lin2",
        "L0_xattn_W_conv1", "L0_xattn_W_conv2", "L0_xattn_W_conv3", "L0_ffn_gate_wq", "L0_ffn_gate_scale",
        "L0_ffn_up_wq", "L0_ffn_up_scale", "L0_ffn_down_wq", "L0_ffn_down_scale"]


def kernel(**inputs):
    import concourse.bacc as bacc
    from concourse.bass_utils import run_bass_kernel_spmd

    nc = bacc.Bacc("TRN2", target_bir_lowering=False, num_devices=1)
    arrays, aps = {}, {}
    for name in _INS:
        a = np.ascontiguousarray(inputs[name])
        arrays[f"in_{name}"] = a
        aps[name] = nc.dram_tensor(f"in_{name}", a.shape, mybir.dt.from_np(a.dtype), kind="ExternalInput").ap()
    out = nc.dram_tensor("out_x", (B, C, N), F32, kind="ExternalOutput").ap()
    x = "L0_xattn_"
    g = {"x": aps["x"], "ctx": aps["ctx_4096"],
         "w_lin": [aps[x + "W_lin1"], aps[x + "W_lin2"]], "b_lin": [aps[x + "b_lin1"], aps[x + "b_lin2"]],
         "w_conv": [aps[x + "W_conv1"], aps[x + "W_conv2"]], "w_mix": aps[x + "W_conv3"]}
    for name in ("gate", "up", "down"):
        g[name + "_wq"] = aps[f"L0_ffn_{name}_wq"]
        g[name + "_scale"] = aps[f"L0_ffn_{name}_scale"]
    program(nc, g, out)
    r = run_bass_kernel_spmd(nc, [arrays], core_ids=[0])
    return r.results[0]["out_x"]
```

```python
from contextlib import ExitStack

import numpy as np
import concourse.bass as bass
from concourse import mybir

ALU = mybir.AluOpType
ACT = mybir.ActivationFunctionType
AX_X = mybir.AxisListType.X
F32, F16, BF16 = mybir.dt.float32, mybir.dt.float16, mybir.dt.bfloat16
I32, U32 = mybir.dt.int32, mybir.dt.uint32

P = 128
B, C, N, H = 16, 32, 512, 512
FF = 1792
RT = B * C // P
BPT = P // C
NBITS = 10
METHODS, WIN, HEADS, HD = 4, 10, 4, 32
PERMS = ((2, 0, 3, 1), (1, 3, 0, 2))
BACK = 5
SQRT_HD = float(np.float32(np.sqrt(HD)))
EPS = 1e-5

STRIPS, SUB, TRI = 4, 4, 3
PTS = SUB * TRI
SP_PTS = N // STRIPS
CHUNKS = -(-SP_PTS // PTS)
SP_PAD = CHUNKS * PTS
COLS = STRIPS * PTS * WIN
BLK = TRI * WIN
PITCH = 32 + WIN
NBLK = STRIPS * SUB
SW = BACK + N + 8
MASK = float(2 ** 22)
VECTOR_HEADS = 2
WARM_FIRST, WARM_EACH = 24, 2
FLOOR = float(2 ** 23)


class Step:

    def __init__(self, engine, sem):
        self.engine, self.sem, self.count = engine, sem, 0

    def then_wait(self, ins):
        self.count += 1
        ins.then_inc(self.sem, 1)
        self.engine.wait_ge(self.sem, self.count)


class LoopStep:

    def __init__(self, engine, sem, i, per):
        self.engine, self.sem, self.i, self.per, self.count = engine, sem, i, per, 0

    def __call__(self, ins):
        self.count += 1
        assert self.count <= self.per
        ins.then_inc(self.sem, 1)
        self.engine.wait_ge(self.sem, self.i * self.per + self.count)


def clear_semaphores(nc, handles):
    with nc.Block() as block:
        @block.sync
        def _(sp):
            numbers = sorted(h.num for h in handles)
            start = numbers[0]
            for n, after in zip(numbers, numbers[1:] + [None]):
                if after != n + 1:
                    sp.sem_clear(range(start, n + 1))
                    start = after


class Newton:

    def __init__(self, nc, work, std_ready):
        self.nc, self.work, self.std_ready = nc, work, std_ready

    def on_scalar(self, act, shifted_ready, count, value):
        act.wait_ge(shifted_ready, value)
        self.nc.scalar.activation(self.work[1], self.work[0], ACT.Sqrt).then_inc(self.std_ready, 1)

    def on_vector(self, dve, link, var, rstd, shifted_ready, value):
        vec = self.nc.vector
        a, s, t = self.work[0], self.work[1], self.work[2]
        vec.tensor_scalar(a, var, EPS, None, ALU.add).then_inc(shifted_ready, 1)
        dve.wait_ge(self.std_ready, value)
        link(vec.reciprocal(rstd, s))
        link(vec.tensor_tensor(t, rstd, rstd, ALU.mult))
        link(vec.tensor_tensor(t, t, a, ALU.mult))
        link(vec.tensor_scalar(t, t, -0.5, 1.5, ALU.mult, ALU.add))
        link(vec.tensor_tensor(rstd, rstd, t, ALU.mult))


def sort_and_prepare(nc, g):
    ctx_in, x_in, feats, orders = g["ctx"], g["x"], g["feats"], g["orders"]
    with ExitStack() as ctx:
        def sb(name, shape, dt):
            return ctx.enter_context(nc.sbuf_tensor(name, shape, dt))

        handles = []

        def sem(name):
            handles.append(ctx.enter_context(nc.semaphore(name)))
            return handles[-1]

        coords = sb("coords", [P, 3, N], F32)
        lo = sb("lo", [P, 3], F32)
        hi = sb("hi", [P, 3], F32)
        small = sb("small", [P, 14, 3], F32)
        pos = sb("pos", [P, 3, P], F32)
        near = sb("near", [P, 3, P], F32)
        over = sb("over", [P, 3, P], F32)
        code = sb("code", [P, 2, 3, P], I32)
        spread = sb("spread", [P, 2, 3, P], I32)
        bit = sb("bit", [P, P], I32)
        notbit = sb("notbit", [P, P], I32)
        diff = sb("diff", [P, P], I32)
        key = sb("key", [P, 2, P], I32)
        high = sb("high", [P, 2, P], I32)
        low = sb("low", [P, 2, P], I32)
        keys = sb("keys", [METHODS * B, N], F32)
        top = sb("top", [METHODS * B, 2, 8], F32)
        where = sb("where", [METHODS * B, N], U32)
        order = sb("order", [METHODS * B, N], F16)
        rows = sb("rows", [P, RT, N], F32)
        normed = sb("normed", [P, RT, N], F32)
        stats = sb("stats", [P, RT, 6], F32)
        mean_var = sb("mean_var", [P, RT, 2], F32)
        rstd = sb("rstd", [P, RT], F32)
        work = sb("work", [P, 3, RT], F32)
        newton_std = sem("newton_std")
        newton = Newton(nc, [work[:, i, :] for i in range(3)], newton_std)
        raw = sb("raw", [P, 2, FF], I32)
        scales = sb("scales", [P, 32], F32)
        deq = sb("deq", [P, 2, FF], F32)
        turned = [ctx.enter_context(nc.psum_tensor(f"turned{i}", [P, 4, P], F32)) for i in range(4)]

        coords_in, x_loaded = sem("coords_in"), sem("x_loaded")
        raw_in, scales_in = g["raw_in"], g["scales_in"]
        step, var_ready, normed_ready = sem("step"), sem("var_ready"), sem("normed_ready")
        code_ready, keys_in, order_ready, stored = sem("code_ready"), sem("keys_in"), sem("order_ready"), sem("stored")
        deq_ready, turned_ready, turned_out = sem("deq_ready"), sem("turned_ready"), sem("turned_out")
        ctx.callback(lambda: clear_semaphores(nc, handles))
        block = ctx.enter_context(nc.Block())

        gate_blocks = [("gate", i, H) for i in range(FF // P)]
        up_blocks = [("up", i, H) for i in range(FF // P)]
        down_blocks = [("down", i, FF) for i in range(H // P)]
        loads = []
        for name in ("gate", "up"):
            i = 0
            while i < FF // P:
                m = min(3, FF // P - i)
                loads.append((name, i, m))
                i += m
        loads += [("down", i, 1) for i in range(H // P)]

        def scale_col(name, i):
            return {"gate": 0, "up": FF // P, "down": 2 * (FF // P)}[name] + i

        def groups():
            out = []
            for n, (name, i0, m) in enumerate(loads):
                if name == "down":
                    for j in range(0, FF // P, 4):
                        k = min(4, FF // P - j)
                        out.append((n, [(j + t) * P for t in range(k)],
                                    g["downT"][:, j:j + k, i0 * P:(i0 + 1) * P]))
                else:
                    for r in range(m):
                        out.append((n, [r * H + t * P for t in range(4)],
                                    g[name + "T"][:, :, (i0 + r) * P:(i0 + r + 1) * P]))
            return out

        GROUPS = groups()

        @block.sync
        def _(sp):
            for quarter in range(4):
                at = quarter * 32
                sp.dma_start(coords[at:at + B, :, :], ctx_in[:, 0:3, :]).then_inc(coords_in, 16)
                for slot, row in enumerate((1, 0, 2)):
                    sp.dma_start(coords[at + B:at + 2 * B, slot, :], ctx_in[:, row, :]).then_inc(coords_in, 16)
            sp.dma_start(rows[:], x_in.rearrange("(t q) c n -> (q c) t n", q=BPT)).then_inc(x_loaded, 16)
            sp.wait_ge(normed_ready, RT)
            for t in range(RT):
                for q in range(BPT):
                    sp.dma_start(feats[t * BPT + q, 0:C, :], normed[q * C:(q + 1) * C, t, :]).then_inc(stored, 16)
            sp.wait_ge(code_ready, 1)
            for kind in range(2):
                for quarter in range(4):
                    sp.dma_start(keys[kind * 32:kind * 32 + 32, quarter * P:(quarter + 1) * P],
                                 key[quarter * 32:quarter * 32 + 32, kind, :].bitcast(F32)).then_inc(keys_in, 16)
            sp.wait_ge(order_ready, 1)
            sp.dma_start(orders[:, :], order[:]).then_inc(stored, 16)
            sp.wait_ge(stored, 16 * (B + 1))

        @block.gpsimd
        def _(pool):
            wq = {"gate": g["gate_wq"], "up": g["up_wq"], "down": g["down_wq"]}
            for name in ("gate", "up", "down"):
                n = FF // P if name != "down" else H // P
                c = scale_col(name, 0)
                with nc.allow_non_contiguous_dma("scales, one per partition"):
                    pool.dma_start(scales[:, c:c + n], g[name + "_scale"].rearrange("(n p) -> p n", p=P))\
                        .then_inc(scales_in, 16)
            for n, (name, i, m) in enumerate(loads):
                if n >= 2:
                    pool.wait_ge(deq_ready, n - 1)
                width = H if name != "down" else FF
                src = wq[name][i * P:(i + m) * P, :].rearrange("(m p) w -> p m w", p=P)
                dst = raw[:, n % 2, 0:m * width].rearrange("p (m w) -> p m w", m=m)
                pool.dma_start(dst, src).then_inc(raw_in[n % 2], 16)

        @block.scalar
        def _(act):
            newton.on_scalar(act, var_ready, 1, 1)
            act.wait_ge(scales_in, 48)
            done = 0
            for n, (name, i, m) in enumerate(loads):
                width = H if name != "down" else FF
                act.wait_ge(raw_in[n % 2], 16 * (n // 2 + 1))
                if n >= 2:
                    act.wait_ge(turned_ready, sum(1 for q in GROUPS if q[0] <= n - 2))
                for r in range(m):
                    c = scale_col(name, i + r)
                    ins = nc.scalar.activation(deq[:, n % 2, r * width:(r + 1) * width],
                                               raw[:, n % 2, r * width:(r + 1) * width], ACT.Copy,
                                               scale=scales[:, c:c + 1])
                ins.then_inc(deq_ready, 1)
                if n >= 1:
                    for k, (load, cols, dst) in enumerate(GROUPS):
                        if load == n - 1:
                            act.wait_ge(turned_ready, k + 1)
                            nc.scalar.activation(dst, turned[k % 4][:, 0:len(cols), :], ACT.Copy)\
                                .then_inc(turned_out, 1)
            for k, (load, cols, dst) in enumerate(GROUPS):
                if load == len(loads) - 1:
                    act.wait_ge(turned_ready, k + 1)
                    nc.scalar.activation(dst, turned[k % 4][:, 0:len(cols), :], ACT.Copy).then_inc(turned_out, 1)

        @block.tensor
        def _(pe):
            for k, (load, cols, dst) in enumerate(GROUPS):
                pe.wait_ge(deq_ready, load + 1)
                if k >= 4:
                    pe.wait_ge(turned_out, k - 3)
                for t, c in enumerate(cols):
                    ins = nc.tensor.transpose(turned[k % 4][:, t, :], deq[:, load % 2, c:c + P], g["ident"][:])
                ins.then_inc(turned_ready, 1)

        @block.vector
        def _(dve):
            chain = Step(dve, step)
            link = chain.then_wait
            vec = nc.vector
            dve.wait_ge(x_loaded, 16)
            for t in range(RT):
                link(vec.bn_stats(stats[:, t, :], rows[:, t, :]))
                ins = vec.bn_aggr(mean_var[:, t, :], stats[:, t, :])
            link(ins)
            newton.on_vector(dve, link, mean_var[:, :, 1], rstd[:], var_ready, 1)
            for t in range(RT):
                vec.tensor_scalar(normed[:, t, :], rows[:, t, :], mean_var[:, t, 0:1], rstd[:, t:t + 1],
                                  ALU.subtract, ALU.mult).then_inc(normed_ready, 1)

            dve.wait_ge(coords_in, 256)
            vec.tensor_reduce(lo[:], coords[:], AX_X, ALU.min)
            link(vec.tensor_reduce(hi[:], coords[:], AX_X, ALU.max))
            top_q = float(2 ** NBITS - 1)
            d, r, y, t0, t1, yh, yl, dh, dl, pr, er, sc = (small[:, i, :] for i in range(12))
            link(vec.tensor_tensor(d, hi[:], lo[:], ALU.subtract))
            link(vec.tensor_scalar(d, d, 1e-6, None, ALU.add))
            link(vec.reciprocal(r, d))
            link(vec.tensor_scalar(y, r, top_q, None, ALU.mult))

            def halves(v, vh, vl):
                link(vec.tensor_scalar(t0, v, 4097.0, None, ALU.mult))
                link(vec.tensor_tensor(t1, t0, v, ALU.subtract))
                link(vec.tensor_tensor(vh, t0, t1, ALU.subtract))
                link(vec.tensor_tensor(vl, v, vh, ALU.subtract))

            halves(y, yh, yl)
            halves(d, dh, dl)
            link(vec.tensor_tensor(pr, y, d, ALU.mult))
            link(vec.tensor_tensor(er, yh, dh, ALU.mult))
            link(vec.tensor_tensor(er, er, pr, ALU.subtract))
            for a, b in ((yh, dl), (yl, dh), (yl, dl)):
                link(vec.tensor_tensor(t0, a, b, ALU.mult))
                link(vec.tensor_tensor(er, er, t0, ALU.add))
            link(vec.tensor_scalar(t0, pr, -1.0, top_q, ALU.mult, ALU.add))
            link(vec.tensor_tensor(t0, t0, er, ALU.subtract))
            link(vec.tensor_tensor(t0, t0, r, ALU.mult))
            link(vec.tensor_tensor(sc, y, t0, ALU.add))
            for quarter in range(4):
                at = slice(quarter * 32, quarter * 32 + 32)
                ins = vec.tensor_tensor(pos[at], coords[at, :, quarter * P:(quarter + 1) * P],
                                        lo[at].unsqueeze(2).broadcast_to([32, 3, P]), ALU.subtract)
            link(ins)
            link(vec.tensor_tensor(pos[:], pos[:], sc.unsqueeze(2).broadcast_to([P, 3, P]), ALU.mult))
            link(vec.tensor_scalar(near[:], pos[:], FLOOR, FLOOR, ALU.add, ALU.subtract))
            link(vec.tensor_tensor(over[:], near[:], pos[:], ALU.is_gt))
            link(vec.tensor_tensor(near[:], near[:], over[:], ALU.subtract))
            for kind in range(2):
                ins = vec.tensor_scalar(code[:, kind], near[:], 0.0, top_q, ALU.max, ALU.min)
            link(ins)

            X = [code[:, 1, i, :] for i in range(3)]
            for k in range(NBITS - 1, 0, -1):
                mask = (1 << k) - 1
                for i in range(3):
                    link(vec.tensor_scalar(bit[:], X[i], 31 - k, 31, ALU.logical_shift_left,
                                           ALU.arith_shift_right))
                    if i:
                        vec.tensor_tensor(diff[:], X[0], X[i], ALU.bitwise_xor)
                        link(vec.tensor_scalar(notbit[:], bit[:], -1, mask, ALU.bitwise_xor, ALU.bitwise_and))
                        link(vec.tensor_tensor(diff[:], diff[:], notbit[:], ALU.bitwise_and))
                        vec.tensor_tensor(X[i], X[i], diff[:], ALU.bitwise_xor)
                        link(vec.tensor_tensor(X[0], X[0], diff[:], ALU.bitwise_xor))
                    link(vec.scalar_tensor_tensor(X[0], bit[:], mask, X[0], ALU.bitwise_and, ALU.bitwise_xor))
            for i in (1, 2):
                link(vec.tensor_tensor(X[i], X[i], X[i - 1], ALU.bitwise_xor))
            link(vec.tensor_scalar(bit[:], X[2], 1, None, ALU.logical_shift_right))
            for s in (1, 2, 4, 8):
                link(vec.scalar_tensor_tensor(bit[:], bit[:], s, bit[:], ALU.logical_shift_right,
                                              ALU.bitwise_xor))
            for i in range(3):
                ins = vec.tensor_tensor(X[i], X[i], bit[:], ALU.bitwise_xor)
            link(ins)

            for s, m in ((16, 0x030000FF), (8, 0x0300F00F), (4, 0x030C30C3), (2, 0x09249249)):
                link(vec.scalar_tensor_tensor(spread[:], code[:], s, code[:], ALU.logical_shift_left,
                                              ALU.bitwise_or))
                link(vec.tensor_scalar(code[:], spread[:], m, None, ALU.bitwise_and))
            link(vec.scalar_tensor_tensor(key[:], code[:, :, 0, :], 2, code[:, :, 2, :],
                                          ALU.logical_shift_left, ALU.bitwise_or))
            link(vec.scalar_tensor_tensor(key[:], code[:, :, 1, :], 1, key[:], ALU.logical_shift_left,
                                          ALU.bitwise_or))
            link(vec.tensor_scalar(high[:], key[:], 23, None, ALU.logical_shift_right))
            link(vec.tensor_scalar(high[:], high[:], 1, None, ALU.add))
            link(vec.tensor_scalar(low[:], key[:], (1 << 23) - 1, -(1 << 31), ALU.bitwise_and, ALU.bitwise_or))
            vec.scalar_tensor_tensor(key[:], high[:], 23, low[:], ALU.logical_shift_left,
                                     ALU.bitwise_or).then_inc(code_ready, 1)

            dve.wait_ge(keys_in, 128)
            for t in range(N // 8):
                link(vec.max(top[:, t % 2, :], keys[:]))
                vec.max_index(where[:, 8 * t:8 * t + 8], top[:, t % 2, :], keys[:])
                link(vec.match_replace(keys[:], top[:, t % 2, :], keys[:], -3e38))
            vec.tensor_copy(order[:], where[:]).then_inc(order_ready, 1)


def gather_windows(nc, g, layer, sorted_rows):
    feats, orders, perm = g["feats"], g["orders"], PERMS[layer]
    first = layer * C
    with ExitStack() as ctx:
        def sb(name, shape, dt):
            return ctx.enter_context(nc.sbuf_tensor(f"{name}_{layer}", shape, dt))

        handles = []

        def sem(name):
            handles.append(ctx.enter_context(nc.semaphore(f"{name}_{layer}")))
            return handles[-1]

        rows = sb("feature_rows", [P, RT, N], F32)
        by_point = sb("by_point", [P, 4, B, 3, C], BF16)
        rest = sb("rest", [P, 2, 4, P], F32)
        ordered = sb("ordered", [P, 2, METHODS, N], F16)
        hot = sb("hot", [P, 2, 4, METHODS, N], BF16)
        gathered = sb("gathered", [P, 2, 4, METHODS * C], F32)
        products = ctx.enter_context(nc.psum_tensor(f"products_{layer}", [P, 4, 512], F32))
        turned = ctx.enter_context(nc.psum_tensor(f"turned_{layer}", [P, 2, 512], F32))

        rows_in, turned_ready, step = sem("rows_in"), sem("turned_ready"), sem("split_step")
        split_ready = sem("split_ready")
        order_in = [sem("order_in0"), sem("order_in1")]
        hot_ready, products_ready, gathered_ready = sem("hot_ready"), sem("products_ready"), sem("gathered_ready")
        window_turned, rows_ready = sem("window_turned"), sem("rows_ready")
        ctx.callback(lambda: clear_semaphores(nc, handles))
        block = ctx.enter_context(nc.Block())

        def product_view(rc):
            return products[:, rc, 0:3 * P].rearrange("p (s f) -> p s f", s=3)

        @block.sync
        def _(sp):
            for t in range(RT):
                for q in range(BPT):
                    sp.dma_start(rows[q * C:(q + 1) * C, t, :], feats[t * BPT + q, first:first + C, :])\
                        .then_inc(rows_in, 16)

            def load_orders(b, parity):
                src = bass.AP(orders.tensor, orders.offset + b * N, [[0, P], [B * N, METHODS], [1, N]])
                sp.dma_start(ordered[:, parity], src).then_inc(order_in[parity], 16)

            load_orders(0, 0)
            load_orders(1, 1)
            with sp.Fori(0, B // 2 - 1) as bp:
                for half in range(2):
                    sp.wait_ge(hot_ready, bp * 8 + (4 * half + 4))
                    load_orders(bp * 2 + (2 + half), half)

        @block.vector
        def _(dve):
            vec = nc.vector
            chain = Step(dve, step)
            link = chain.then_wait
            for t in range(RT):
                if t:
                    dve.wait_ge(split_ready, t)
                dve.wait_ge(turned_ready, t + 1)
                src = turned[:, t % 2, :].rearrange("p (c f) -> p c f", c=4)
                parts = by_point[:, :, t * BPT:(t + 1) * BPT, :, :].rearrange("p c q s f -> p s c q f")
                as_rows = [rest[:, i].rearrange("p c (q f) -> p c q f", q=BPT) for i in range(2)]
                part = [parts[:, s] for s in range(3)]
                link(vec.tensor_copy(rest[:, 0], src))
                for c in range(4):
                    ins = vec.tensor_copy(part[0][:, c], as_rows[0][:, c])
                link(ins)
                for s in (1, 2):
                    for c in range(4):
                        ins = vec.tensor_tensor(as_rows[s % 2][:, c], as_rows[(s + 1) % 2][:, c],
                                                part[s - 1][:, c], ALU.subtract)
                    link(ins)
                    for c in range(4):
                        ins = vec.tensor_copy(part[s][:, c], as_rows[s % 2][:, c])
                    if s == 1:
                        link(ins)
                ins.then_inc(split_ready, 1)

            def sum_parts(b, half):
                for rc in range(4):
                    dve.wait_ge(products_ready, b * 4 + (rc + 1))
                    vec.tensor_reduce(
                        gathered[:, half, rc, :], product_view(rc).rearrange("p s f -> p f s"),
                        AX_X, ALU.add).then_inc(gathered_ready, 1)

            def make_hot(pair, half):
                dve.wait_ge(order_in[half], pair * 16 + 16)
                for c in range(4):
                    vec.tensor_scalar(hot[:, half, c], ordered[:, half], g["point"][:, c:c + 1], None,
                                      ALU.is_equal).then_inc(hot_ready, 1)

            make_hot(0, 0)
            with dve.Fori(0, B // 2 - 1) as bp:
                make_hot(bp, 1)
                sum_parts(bp * 2, 0)
                make_hot(bp + 1, 0)
                sum_parts(bp * 2 + 1, 1)
            make_hot(B // 2 - 1, 1)
            sum_parts(B - 2, 0)
            sum_parts(B - 1, 1)
            vec.memset(sorted_rows[:, :, 0:BACK], 0.0)
            dve.wait_ge(rows_ready, B)
            vec.tensor_copy(sorted_rows[:, :, BACK + N:SW],
                            sorted_rows[:, :, BACK + N - 1:BACK + N].broadcast_to([P, B, SW - BACK - N]))

        @block.tensor
        def _(pe):
            for t in range(RT):
                pe.wait_ge(rows_in, 16 * B)
                if t >= 2:
                    pe.wait_ge(split_ready, t - 1)
                for c in range(4):
                    ins = nc.tensor.transpose(turned[:, t % 2, c * P:(c + 1) * P], rows[:, t, c * P:(c + 1) * P],
                                              g["ident"][:])
                ins.then_inc(turned_ready, 1)
            pe.wait_ge(split_ready, RT)

            def one_batch(b, half, first_batch=False):
                pe.wait_ge(hot_ready, b * 4 + 4)
                for rc in range(4):
                    if not first_batch:
                        pe.wait_ge(gathered_ready, b * 4 + (rc - 3))
                    for place in range(METHODS):
                        for c in range(4):
                            ins = nc.tensor.matmul(
                                product_view(rc).rearrange("p s (h m f) -> p m s h f", h=HEADS, m=METHODS)[:, place],
                                hot[:, half, c, perm[place], rc * P:(rc + 1) * P],
                                by_point[:, c, b, :, :].rearrange("p s (h f) -> p s h f", h=HEADS), start=(c == 0), stop=(c == 3))
                    ins.then_inc(products_ready, 1)

            def turn_batch(b, half, early=False):
                for rc in range(4):
                    pe.wait_ge(gathered_ready, b * 4 + (rc + 1))
                    if rc == 0 and not early:
                        pe.wait_ge(rows_ready, b * 1 - 1)
                    ins = nc.tensor.transpose(
                        turned[:, half, rc * P:(rc + 1) * P],
                        gathered[:, half, rc, :], g["ident"][:])
                ins.then_inc(window_turned, 1)

            one_batch(0, 0, True)
            one_batch(1, 1)
            turn_batch(0, 0, True)
            one_batch(2, 0)
            turn_batch(1, 1, True)
            with pe.Fori(1, B // 2 - 1) as bp:
                one_batch(bp * 2 + 1, 1)
                turn_batch(bp * 2, 0)
                one_batch(bp * 2 + 2, 0)
                turn_batch(bp * 2 + 1, 1)
            one_batch(B - 1, 1)
            turn_batch(B - 2, 0)
            turn_batch(B - 1, 1)

        @block.scalar
        def _(act):
            def copy_rows(b, half):
                act.wait_ge(window_turned, b + 1)
                nc.scalar.activation(sorted_rows[:, b, BACK:BACK + N], turned[:, half, :], ACT.Copy)\
                    .then_inc(rows_ready, 1)

            for b in range(B):
                copy_rows(b, b % 2)


def window_attention(nc, g, layer, sorted_rows, hmax, hstats):
    O = g["O"][layer]
    GO = P // O
    GH = STRIPS // GO
    feats = g["feats"]
    first = layer * C
    with ExitStack() as ctx:
        def sb(name, shape, dt):
            return ctx.enter_context(nc.sbuf_tensor(f"{name}_{layer}", shape, dt))

        def ps(name, shape):
            return ctx.enter_context(nc.psum_tensor(f"{name}_{layer}", shape, F32))

        handles = []

        def sem(name):
            handles.append(ctx.enter_context(nc.semaphore(f"{name}_{layer}")))
            return handles[-1]

        w_lin = sb("w_lin", [64, 2 * C * METHODS], F32)
        w_conv = sb("w_conv", [O, 64], F32)
        b_lin = sb("b_lin", [64, 1], F32)
        w_convT = sb("w_convT", [64, O], F32)
        w_lin_near = sb("w_lin_near", [64, HEADS, METHODS, 8], F32)
        w_near = sb("w_near", [P, 2, O], F16)
        w_scaled = sb("w_scaled", [P, 2, O], F32)
        w_top = sb("w_top", [P, 1], F32)
        top = sb("top", [1, 1], F32)
        ones_row = sb("ones_row", [1, P], F32)
        w_power = sb("w_power", [P, 1], F32)
        w_scale, w_undo = sb("w_scale", [P, 1], F32), sb("w_undo", [P, 1], F32)
        w_centre = sb("w_centre", [C + 1, O], F32)
        point_sums = sb("point_sums", [P, SUB, TRI], F32)
        of_point = sb("of_point", [P, TRI], F32)
        first_windows = sb("first_windows", [P, B, BACK, WIN], F32)
        centre = sb("centre", [P, 2, SP_PTS * STRIPS + PTS], F32)
        half_centre = sb("half_centre", [C, N + PTS], F16)
        centre_in = sb("centre_in", [C + 1, N + PTS], F32)
        centre_out = sb("centre_out", [P, 2, GH, SP_PAD], F32)
        vectors = sb("vectors", [P, 2, STRIPS * PTS * PITCH], F16)
        by_head = sb("by_head", [P, 2, NBLK, HEADS, 32], F16)
        row_max = sb("row_max", [P, NBLK], F32)
        shifted = sb("shifted", [P, NBLK, WIN], F32)
        exps = sb("exps", [P, 2, NBLK, WIN], F32)
        probs = sb("probs", [P, 2, NBLK, 32], F32)
        row_sum = sb("row_sum", [P, NBLK], F32)
        row_inv = sb("row_inv", [P, NBLK], F32)
        point_inv = sb("point_inv", [P, 2, NBLK, TRI], F32)
        probsT = sb("probsT", [P, STRIPS, P], F32)
        mapped = sb("mapped", [P, 2, NBLK, O], F32)
        fused = sb("fused", [P, 2, GH, SP_PAD * WIN], F32)
        piece = sb("piece", [P, GH, 4, 6], F32)
        scores = [ps(f"scores{i}", [P, 512]) for i in range(2)]
        ps_mapped = ps("ps_mapped", [P, NBLK, O])
        ps_probsT = ps("ps_probsT", [P, STRIPS, P])
        outs = [ps(f"outs{i}", [P, 512]) for i in range(2)]
        misc = ps("misc", [P, 512])

        weights_in = sem("weights_in")
        centre_loaded = [sem("centre_loaded0"), sem("centre_loaded1")]
        raw_loaded, bias_row_ready, zeros_ready = sem("raw_loaded"), sem("bias_row_ready"), sem("zeros_ready")
        conv_turned, conv_ready, joined, split_step = sem("conv_turned"), sem("conv_ready"), sem("joined"), sem("split_step")
        top_ready, top_turned, top_spread = sem("top_ready"), sem("top_turned"), sem("top_spread")
        w_ready, near_ready, edge_ready = sem("w_ready"), sem("near_ready"), sem("edge_ready")
        vectors_ready, by_head_ready, other_heads_ready = (
            sem("vectors_ready"), sem("by_head_ready"), sem("other_heads_ready"))
        scores_ready, max_ready, shifted_ready = sem("scores_ready"), sem("max_ready"), sem("shifted_ready")
        exp_ready, sum_ready, row_inv_ready, inv_ready, probs_ready = (
            sem("exp_ready"), sem("sum_ready"), sem("row_inv_ready"), sem("inv_ready"), sem("probs_ready"))
        probs_turned, probsT_ready = sem("probs_turned"), sem("probsT_ready")
        mapped_done, mapped_ready = sem("mapped_done"), sem("mapped_ready")
        outs_ready, fused_ready, pieces_ready = sem("outs_ready"), sem("fused_ready"), sem("pieces_ready")
        batch_closed = sem("batch_closed")
        half_ready, centre_in_ready, centre_done, centre_out_ready = (
            sem("half_ready"), sem("centre_in_ready"), sem("centre_done"), sem("centre_out_ready"))
        ctx.callback(lambda: clear_semaphores(nc, handles))
        block = ctx.enter_context(nc.Block())

        def spread(copy, parity, h):
            at = slice(32 * h, 32 * h + 32)
            return copy(by_head[at, parity, :, h, 0:BLK].rearrange("p b (q j) -> p b q j", q=TRI),
                        vectors[at, parity, :].rearrange("p (b q j) -> p b q j", q=TRI, j=PITCH)[:, :, :, 0:WIN])

        BLOCKS = [(strip, sub) for strip in range(STRIPS) for sub in range(SUB)]

        def out_view(parity):
            return outs[parity][:, 0:GH * PTS * WIN].rearrange("p (g c) -> p g c", g=GH)

        def over_chunks(engine, chunk):
            with engine.Fori(0, B // 2) as pair:
                for half in range(2):
                    at = pair * (2 * CHUNKS) + half * CHUNKS
                    for k in (0, 1, 2):
                        chunk(pair, half, k, at + k, (half + k) % 2, True)
                    with engine.Fori(0, (CHUNKS - 5) // 2) as i:
                        for j in (3, 4):
                            chunk(pair, half, i * 2 + j, at + (i * 2 + j), (half + j) % 2, False)
                    for k in (CHUNKS - 2, CHUNKS - 1):
                        chunk(pair, half, k, at + k, (half + k) % 2, True)

        @block.sync
        def _(sp):
            sp.dma_start(w_lin[:], g["w_lin"][layer]).then_inc(weights_in, 16)
            sp.dma_start(w_conv[:], g["w_conv"][layer]).then_inc(weights_in, 16)
            sp.dma_start(b_lin[:], g["b_lin"][layer].rearrange("(k a) -> k a", a=1)).then_inc(weights_in, 16)

            def load_centres(b, half):
                for h in range(HEADS):
                    src = bass.AP(feats.tensor, feats.offset + b * (P * N) + (first + 8 * h) * N,
                                  [[0, METHODS], [N, 8], [1, N]])
                    sp.dma_start(centre[32 * h:32 * h + 32, half, 0:N], src).then_inc(centre_loaded[half], 16)

            def load_raw(b):
                sp.dma_start(centre_in[0:C, 0:N], bass.AP(feats.tensor, feats.offset + b * (P * N) + first * N,
                                                         [[N, C], [1, N]])).then_inc(raw_loaded, 16)

            load_centres(0, 0)
            sp.wait_ge(bias_row_ready, 1)
            load_raw(0)
            with sp.Fori(0, B // 2) as pair:
                for half in range(2):
                    b = pair * 2 + half
                    sp.wait_ge(vectors_ready, b * CHUNKS + 1)
                    load_centres((b + 1) % B, 1 - half)
                    sp.wait_ge(centre_done, b + 1)
                    load_raw((b + 1) % B)
            sp.wait_ge(centre_loaded[0], 64 * (B // 2 + 1))
            sp.wait_ge(raw_loaded, 16 * (B + 1))

        @block.gpsimd
        def _(pool):
            gp = nc.gpsimd
            gp.memset(centre_in[:], 1.0).then_inc(bias_row_ready, 1)
            gp.memset(centre[:, :, N:], 0.0)
            gp.memset(vectors[:], 0.0)
            gp.memset(by_head[:], 0.0)
            gp.memset(fused[:, 1], 0.0)
            gp.memset(centre_out[:], 0.0)
            gp.memset(probs[:], 0.0).then_inc(zeros_ready, 1)
            gp.memset(fused[:, 0], 0.0).then_inc(probs_ready, 1)

            def normalise(pair, half, k, n, parity, peeled):
                pool.wait_ge(inv_ready, n + 1)
                gp.tensor_tensor(probs[:, parity, :, 0:BLK].rearrange("p b (q j) -> p b q j", q=TRI),
                                 exps[:, parity].unsqueeze(2).broadcast_to([P, NBLK, TRI, WIN]),
                                 point_inv[:, parity].unsqueeze(3).broadcast_to([P, NBLK, TRI, WIN]),
                                 ALU.mult).then_inc(probs_ready, 1)

            over_chunks(pool, normalise)

        @block.scalar
        def _(act):
            sc = nc.scalar
            act.wait_ge(conv_turned, 1)
            sc.activation(w_convT[:], misc[0:64, 0:O], ACT.Copy).then_inc(conv_ready, 1)

            def make_centre_in(pair_b):
                act.wait_ge(raw_loaded, pair_b * 16 + 16)
                sc.activation(half_centre[:], centre_in[0:C, :], ACT.Copy).then_inc(half_ready, 1)
                act.wait_ge(half_ready, pair_b + 1)
                sc.activation(centre_in[0:C, :], half_centre[:], ACT.Copy).then_inc(centre_in_ready, 1)

            def copy_centre_out(b, half):
                act.wait_ge(centre_done, b + 1)
                sc.activation(centre_out[:, half], misc[:, 0:GH * SP_PAD].rearrange("p (g c) -> p g c", g=GH),
                              ACT.Copy).then_inc(centre_out_ready, 1)

            def copy_mapped(count, parity):
                act.wait_ge(mapped_done, count)
                sc.activation(mapped[:, parity], ps_mapped[:], ACT.Copy, scale=w_undo[:, 0:1]).then_inc(mapped_ready, 1)

            def copy_probsT(count):
                act.wait_ge(probs_turned, count)
                sc.activation(probsT[:], ps_probsT[:], ACT.Copy).then_inc(probsT_ready, 1)

            def spread_heads(count, parity, batch_count=None):
                act.wait_ge(vectors_ready, count)
                if batch_count is not None:
                    act.wait_ge(edge_ready, batch_count)
                for h in range(VECTOR_HEADS, HEADS):
                    ins = spread(sc.copy, parity, h)
                ins.then_inc(other_heads_ready, 1)

            act.wait_ge(zeros_ready, 1)
            spread_heads(1, 0, 1)
            spread_heads(2, 1)
            make_centre_in(0)
            copy_centre_out(0, 0)
            copy_mapped(1, 1)

            def chunk(pair, half, k, n, parity, peeled):
                copy_mapped(n + 2, parity)
                act.wait_ge(shifted_ready, n + 1)
                sc.activation(exps[:, parity], shifted[:], ACT.Exp, scale=1.0 / SQRT_HD).then_inc(exp_ready, 1)
                copy_probsT(n + 1)
                spread_heads(n + 3, parity, pair * 2 + (half + 2) if peeled and k == CHUNKS - 2 else None)
                if peeled and k == 2:
                    make_centre_in(pair * 2 + (half + 1))
                if peeled and k == CHUNKS - 1:
                    copy_centre_out(pair * 2 + (half + 1), 1 - half)

            over_chunks(act, chunk)
            copy_probsT(B * CHUNKS + 1)

        @block.tensor
        def _(pe):
            mm = nc.tensor.matmul
            pe.wait_ge(weights_in, 48)
            nc.tensor.transpose(misc[0:64, 0:O], w_conv[:], g["ident"][0:O, 0:O]).then_inc(conv_turned, 1)
            pe.wait_ge(conv_ready, 1)
            pe.wait_ge(near_ready, 1)
            mm(misc[:, 64:64 + O], w_lin_near[:].rearrange("k h m f -> k (h m f)"), w_convT[:],
               start=True, stop=True)
            for place in range(METHODS):
                mm(misc[0:C, 128:128 + O], w_lin[:, place:C * METHODS:METHODS], w_convT[:],
                   start=(place == 0), stop=(place == METHODS - 1))
            mm(misc[C:C + 1, 128:128 + O], b_lin[:], w_convT[:], start=True, stop=True).then_inc(joined, 1)

            def make_centre_out():
                for strip in range(STRIPS):
                    go, gh = strip % GO, strip // GO
                    ins = mm(misc[go * O:(go + 1) * O, gh * SP_PAD:(gh + 1) * SP_PAD], w_centre[:],
                             centre_in[:, strip * SP_PTS:strip * SP_PTS + SP_PAD], start=True, stop=True)
                ins.then_inc(centre_done, 1)

            def keep_clock(parity, times):
                for _ in range(times):
                    mm(scores[parity][:], by_head[:, parity, 0, :, :].rearrange("p h c -> p (h c)"),
                       by_head[:, parity, 0:4, :, :].rearrange("p b h c -> p (b h c)"), start=True, stop=True,
                       skip_group_check=True)

            def make_scores(parity):
                for strip in range(STRIPS):
                    for point in range(TRI):
                        for sub in range(SUB):
                            block_ = strip * SUB + sub
                            at = block_ * TRI * PITCH + point * 32
                            out = scores[parity][32 * sub:32 * sub + 32, strip * HEADS * WIN:(strip + 1) * HEADS * WIN]
                            ins = mm(out.rearrange("p (h j) -> p h j", h=HEADS), vectors[:, parity, at:at + 32],
                                     by_head[:, parity, block_, :, point * WIN:(point + 1) * WIN],
                                     start=(point == 0), stop=(point == TRI - 1), skip_group_check=True)
                ins.then_inc(scores_ready, 1)

            def map_vectors(parity):
                for block_ in range(NBLK):
                    for part in range(2):
                        ins = mm(ps_mapped[:, block_, :],
                                 by_head[:, parity, block_, :, :].rearrange("p h c -> p (h c)"),
                                 w_near[:, part, :], start=(part == 0), stop=(part == 1))
                ins.then_inc(mapped_done, 1)

            pe.wait_ge(top_ready, 1)
            nc.tensor.transpose(misc[0:1, 256:256 + P], w_top[:], g["ident"][:])\
                .then_inc(top_turned, 1)
            pe.wait_ge(top_ready, 2)
            mm(misc[:, 384:385], ones_row[:], top[:], start=True, stop=True).then_inc(top_spread, 1)
            pe.wait_ge(w_ready, 1)
            pe.wait_ge(centre_in_ready, 1)
            make_centre_out()
            zeros = probs[:, 0].rearrange("p b c -> p (b c)")
            mm(outs[0][:, 0:COLS], zeros[:, 0:P], zeros[:, 0:COLS], start=True, stop=True).then_inc(outs_ready, 1)
            for q in range(O * NBLK // 256):
                ins = mm(ps_mapped[:].rearrange("p b o -> p (b o)")[:, q * 256:(q + 1) * 256], zeros[:, 0:P],
                         zeros[:, 0:256], start=True, stop=True)
            ins.then_inc(mapped_done, 1)
            pe.wait_ge(by_head_ready, 1)
            pe.wait_ge(other_heads_ready, 1)
            keep_clock(0, WARM_FIRST)
            make_scores(0)

            def turn_probs(count, parity):
                pe.wait_ge(probs_ready, count)
                for strip in range(STRIPS):
                    ins = nc.tensor.transpose(
                        ps_probsT[:, strip, :],
                        probs[:, parity, strip * HEADS:(strip + 1) * HEADS, :].rearrange("p h c -> p (h c)"),
                        g["ident"][:])
                ins.then_inc(probs_turned, 1)

            def weigh(count, parity):
                pe.wait_ge(probsT_ready, count)
                for block_, (strip, sub) in enumerate(BLOCKS):
                    go, gh = strip % GO, strip // GO
                    ins = mm(out_view(parity)[go * O:(go + 1) * O, gh, sub * BLK:(sub + 1) * BLK],
                             mapped[:, parity, block_, :], probsT[:, strip, 32 * sub:32 * sub + BLK],
                             start=True, stop=True)
                ins.then_inc(outs_ready, 1)

            def chunk(pair, half, k, n, parity, peeled):
                pe.wait_ge(mapped_ready, n + 1)
                map_vectors(parity)
                if peeled and k == CHUNKS - 1:
                    pe.wait_ge(centre_in_ready, pair * 2 + (half + 2))
                    pe.wait_ge(centre_out_ready, pair * 2 + (half + 1))
                turn_probs(n + 1, 1 - parity)
                pe.wait_ge(by_head_ready, n + 2)
                pe.wait_ge(other_heads_ready, n + 2)
                keep_clock(1 - parity, WARM_EACH)
                make_scores(1 - parity)
                weigh(n + 1, 1 - parity)
                if peeled and k == CHUNKS - 1:
                    make_centre_out()

            over_chunks(pe, chunk)
            turn_probs(B * CHUNKS + 1, 1)
            pe.wait_ge(mapped_ready, B * CHUNKS + 1)
            pe.wait_ge(fused_ready, B * CHUNKS)
            weigh(B * CHUNKS + 1, 1)

        @block.vector
        def _(dve):
            vec = nc.vector
            chain = Step(dve, split_step)
            link = chain.then_wait
            dve.wait_ge(weights_in, 48)
            vec.tensor_copy(w_lin_near[:], w_lin[:, C * METHODS:].rearrange("k (h f m) -> k h m f", h=HEADS,
                                                                            m=METHODS)).then_inc(near_ready, 1)
            link(vec.tensor_copy(first_windows[:], bass.AP(sorted_rows.tensor, sorted_rows.offset + BACK,
                                                           [sorted_rows.ap[0], [SW, B], [0, BACK], [1, WIN]])))
            for i in range(BACK - 1):
                n_last = WIN - (i + BACK + 1)
                ins = vec.tensor_copy(first_windows[:, :, i, i + BACK + 1:WIN],
                                      sorted_rows[:, :, 2 * BACK + i:2 * BACK + i + 1].broadcast_to([P, B, n_last]))
            link(ins)
            dve.wait_ge(joined, 1)
            near_map = misc[:, 64:64 + O]
            link(vec.tensor_scalar(w_scaled[:, 1], near_map, -1.0, None, ALU.mult))
            link(vec.tensor_tensor(w_scaled[:, 0], near_map, w_scaled[:, 1], ALU.max))
            vec.memset(ones_row[:], 1.0)
            vec.tensor_reduce(w_top[:], w_scaled[:, 0], AX_X, ALU.max).then_inc(top_ready, 1)
            dve.wait_ge(top_turned, 1)
            vec.tensor_reduce(top[:], misc[0:1, 256:256 + P], AX_X, ALU.max).then_inc(top_ready, 1)
            link(vec.tensor_reduce(point_sums[:], g["ident"][:].rearrange("p (s c) -> p s c", s=SUB)[:, :, 0:BLK]
                                   .rearrange("p s (q j) -> p s q j", q=TRI), AX_X, ALU.add))
            vec.tensor_reduce(of_point[:], point_sums[:].rearrange("p s q -> p q s"), AX_X, ALU.add)
            dve.wait_ge(top_spread, 1)
            link(vec.tensor_scalar(w_power[:], misc[:, 384:385], 1e-30, None, ALU.max))
            link(vec.tensor_scalar(w_scale[:].bitcast(I32), w_power[:].bitcast(I32), 0x7F800000, None,
                                   ALU.bitwise_and))
            link(vec.tensor_scalar(w_undo[:], w_scale[:], 2.0 ** -12, None, ALU.mult))
            link(vec.reciprocal(w_scale[:], w_undo[:]))
            link(vec.tensor_scalar(w_scaled[:, 0], near_map, w_scale[:, 0:1], None, ALU.mult))
            link(vec.tensor_copy(w_near[:, 0], w_scaled[:, 0]))
            link(vec.tensor_tensor(w_scaled[:, 1], w_scaled[:, 0], w_near[:, 0], ALU.subtract))
            vec.tensor_copy(w_near[:, 1], w_scaled[:, 1])
            vec.tensor_copy(w_centre[:], misc[0:C + 1, 128:128 + O]).then_inc(w_ready, 1)

            def make_vectors(b, half, k, count, parity, batch_count=None):
                rows = bass.AP(sorted_rows.tensor, sorted_rows.offset + b * SW + k * PTS,
                               [sorted_rows.ap[0], [SP_PTS, STRIPS], [1, PTS], [1, WIN]])
                row = centre[:, half, 0:1]
                mids = bass.AP(row.tensor, row.offset + k * PTS,
                               [row.ap[0], [SP_PTS, STRIPS], [1, PTS], [0, WIN]])
                vec.tensor_tensor(vectors[:, parity, :].rearrange("p (s c j) -> p s c j", s=STRIPS, c=PTS)
                                  [:, :, :, 0:WIN], rows, mids, ALU.subtract).then_inc(vectors_ready, 1)
                dve.wait_ge(vectors_ready, count)
                if batch_count is not None:
                    whole = first_windows[:]
                    starts = bass.AP(whole.tensor, whole.offset + b * (BACK * WIN),
                                     [whole.ap[0], [WIN, BACK], [1, WIN]])
                    vec.tensor_tensor(vectors[:, parity, 0:BACK * PITCH].rearrange("p (i j) -> p i j", i=BACK)
                                      [:, :, 0:WIN], starts,
                                      centre[:, half, 0:BACK].unsqueeze(2).broadcast_to([P, BACK, WIN]),
                                      ALU.subtract).then_inc(edge_ready, 1)
                    dve.wait_ge(edge_ready, batch_count)
                for h in range(VECTOR_HEADS):
                    ins = spread(vec.tensor_copy, parity, h)
                ins.then_inc(by_head_ready, 1)

            def fuse(parity, k, count, half):
                dve.wait_ge(outs_ready, count)
                row = centre_out[:, half, 0:1, 0:1]
                mids = bass.AP(row.tensor, row.offset + k * PTS, [row.ap[0], [SP_PAD, GH], [1, PTS], [0, WIN]])
                row = fused[:, half, 0:1, 0:1]
                dst = bass.AP(row.tensor, row.offset + k * (PTS * WIN),
                              [row.ap[0], [SP_PAD * WIN, GH], [WIN, PTS], [1, WIN]])
                vec.tensor_tensor(dst, out_view(parity).rearrange("p g (c j) -> p g c j", c=PTS), mids,
                                  ALU.add).then_inc(fused_ready, 1)

            def close_quarter(q, b, half, fused_count, batch_count=None):
                points = slice(q * SP_PTS // 4, (q + 1) * SP_PTS // 4)
                columns = slice(points.start * WIN, points.stop * WIN)
                dve.wait_ge(fused_ready, fused_count)
                for gh in range(GH):
                    ins = vec.bn_stats(piece[:, gh, q, :], fused[:, half, gh, columns])
                if batch_count is not None:
                    ins.then_inc(pieces_ready, 1)
                vec.tensor_reduce(hmax[:, b, :, points], fused[:, half, :, columns]
                                  .rearrange("p g (c j) -> p g c j", j=WIN), AX_X, ALU.max)
                if batch_count is not None:
                    dve.wait_ge(pieces_ready, batch_count)
                    vec.tensor_scalar(hstats[:, b], piece[:].rearrange("p g q s -> p (g q s)"), 1.0, None,
                                      ALU.mult).then_inc(batch_closed, 1)

            vec.memset(piece[:], 0.0)
            dve.wait_ge(zeros_ready, 1)
            dve.wait_ge(centre_loaded[0], 64)
            make_vectors(0, 0, 0, 1, 0, 1)
            make_vectors(0, 0, 1, 2, 1)

            def chunk(pair, half, k, n, parity, peeled):
                b = pair * 2 + half
                if peeled and k == 1:
                    dve.wait_ge(centre_out_ready, b + 1)
                dve.wait_ge(scores_ready, n + 1)
                view = scores[parity][:, 0:NBLK * WIN].rearrange("p (b c) -> p b c", b=NBLK)
                vec.tensor_reduce(row_max[:], view, AX_X, ALU.max).then_inc(max_ready, 1)
                dve.wait_ge(max_ready, n + 1)
                vec.tensor_tensor(shifted[:], view, row_max[:].unsqueeze(2).broadcast_to([P, NBLK, WIN]),
                                  ALU.subtract).then_inc(shifted_ready, 1)
                dve.wait_ge(mapped_done, n + 2)
                if peeled and k >= CHUNKS - 2:
                    ahead = k + 2 - CHUNKS
                    if ahead == 0:
                        dve.wait_ge(centre_loaded[1 - half], pair * 64 + 64 * (1 + half))
                    make_vectors((b + 1) % B, 1 - half, ahead, n + 3, parity, b + 2 if ahead == 0 else None)
                else:
                    make_vectors(b, half, k + 2, n + 3, parity)
                dve.wait_ge(exp_ready, n + 1)
                vec.tensor_reduce(row_sum[:], exps[:, parity], AX_X, ALU.add).then_inc(sum_ready, 1)
                dve.wait_ge(sum_ready, n + 1)
                vec.reciprocal(row_inv[:], row_sum[:]).then_inc(row_inv_ready, 1)
                dve.wait_ge(row_inv_ready, n + 1)
                vec.tensor_tensor(point_inv[:, parity], row_inv[:].unsqueeze(2).broadcast_to([P, NBLK, TRI]),
                                  of_point[:].unsqueeze(1).broadcast_to([P, NBLK, TRI]), ALU.mult)\
                    .then_inc(inv_ready, 1)
                if peeled and k < 2:
                    fuse(parity, CHUNKS - 2 + k, n + 1, 1 - half)
                else:
                    fuse(parity, k - 2, n + 1, half)
                if peeled and k >= CHUNKS - 2:
                    close_quarter(k + 2 - CHUNKS, b, half, n)
                if peeled and k in (0, 2):
                    before = (b + B - 1) % B
                    if k == 0:
                        close_quarter(2, before, 1 - half, n + 1)
                    else:
                        close_quarter(3, before, 1 - half, n, b + 1)

            over_chunks(dve, chunk)
            for back in (2, 1):
                fuse(back % 2, CHUNKS - back, B * CHUNKS + 3 - back, 1)
            close_quarter(2, B - 1, 1, B * CHUNKS + 1)
            close_quarter(3, B - 1, 1, B * CHUNKS + 2, B + 1)


def close_layer(nc, g, layer, hmax, hstats):
    O = g["O"][layer]
    GO = P // O
    GH = STRIPS // GO
    dst = C if layer == 0 else 2 * C
    with ExitStack() as ctx:
        def sb(name, shape):
            return ctx.enter_context(nc.sbuf_tensor(f"{name}_{layer}", shape, F32))

        handles = []

        def sem(name):
            handles.append(ctx.enter_context(nc.semaphore(f"{name}_{layer}")))
            return handles[-1]

        strip_stats = sb("strip_stats", [P, B, GH, 2])
        mean = sb("mean", [P, B])
        away = sb("away", [P, B, GH])
        var = sb("var", [P, B])
        rstd = sb("norm_rstd", [P, B])
        work = sb("norm_work", [P, 3, B])
        relu = sb("relu", [P, B, GH, SP_PTS])
        sums = ctx.enter_context(nc.psum_tensor(f"sums_{layer}", [P, 2, 512], F32))
        step, aggregated, mean_done, spread_ready, var_done = (
            sem("close_step"), sem("aggregated"), sem("mean_done"), sem("spread_ready"), sem("var_done"))
        eps_ready, std_ready, relu_ready, stored = sem("eps_ready"), sem("std"), sem("relu_ready"), sem("feats_stored")
        newton = Newton(nc, [work[:, i, :] for i in range(3)], std_ready)
        ctx.callback(lambda: clear_semaphores(nc, handles))
        block = ctx.enter_context(nc.Block())

        @block.tensor
        def _(pe):
            pe.wait_ge(aggregated, 1)
            for gh in range(GH):
                ins = nc.tensor.matmul(sums[:, 0, 0:B], g["average"][layer][:], strip_stats[:, :, gh, 0],
                                       start=(gh == 0), stop=(gh == GH - 1))
            ins.then_inc(mean_done, 1)
            pe.wait_ge(spread_ready, 1)
            for gh in range(GH):
                ins = nc.tensor.matmul(sums[:, 1, 0:B], g["average"][layer][:], strip_stats[:, :, gh, 1],
                                       start=(gh == 0), stop=(gh == GH - 1))
            ins.then_inc(var_done, 1)

        @block.scalar
        def _(act):
            newton.on_scalar(act, eps_ready, 1, 1)

        @block.vector
        def _(dve):
            vec = nc.vector
            chain = Step(dve, step)
            link = chain.then_wait
            for b in range(B):
                for gh in range(GH):
                    ins = vec.bn_aggr(strip_stats[:, b, gh, :], hstats[:, b, gh * 24:(gh + 1) * 24])
            ins.then_inc(aggregated, 1)
            dve.wait_ge(mean_done, 1)
            link(vec.tensor_copy(mean[:], sums[:, 0, 0:B]))
            link(vec.tensor_tensor(away[:], strip_stats[:, :, :, 0], mean[:].unsqueeze(2).broadcast_to([P, B, GH]),
                                   ALU.subtract))
            link(vec.tensor_tensor(away[:], away[:], away[:], ALU.mult))
            vec.tensor_tensor(strip_stats[:, :, :, 1], strip_stats[:, :, :, 1], away[:], ALU.add)\
                .then_inc(spread_ready, 1)
            dve.wait_ge(var_done, 1)
            link(vec.tensor_copy(var[:], sums[:, 1, 0:B]))
            newton.on_vector(dve, link, var[:], rstd[:], eps_ready, 1)
            for b in range(B):
                ins = vec.tensor_scalar(hmax[:, b], hmax[:, b], mean[:, b:b + 1], rstd[:, b:b + 1],
                                        ALU.subtract, ALU.mult)
            link(ins)
            flat = "p b g n -> p (b g n)"
            vec.scalar_tensor_tensor(relu[:].rearrange(flat), hmax.rearrange(flat), 0.2, hmax.rearrange(flat),
                                     ALU.mult, ALU.max).then_inc(relu_ready, 1)

        @block.sync
        def _(sp):
            sp.wait_ge(relu_ready, 1)
            for strip in range(STRIPS):
                go, gh = strip % GO, strip // GO
                sp.dma_start(g["feats"][:, dst:dst + O, strip * SP_PTS:(strip + 1) * SP_PTS]
                             .rearrange("b o n -> o b n"), relu[go * O:(go + 1) * O, :, gh, :]).then_inc(stored, 16)
            sp.wait_ge(stored, 16 * STRIPS)


def mix_features(nc, g, x1, query):
    with ExitStack() as ctx:
        def sb(name, shape):
            return ctx.enter_context(nc.sbuf_tensor(name, shape, F32))

        handles = []

        def sem(name):
            handles.append(ctx.enter_context(nc.semaphore(name)))
            return handles[-1]

        mixed = sb("mixed", [P, B, N])
        w_mix = sb("w_mix", [C, P])
        w_mixT = sb("w_mixT", [P, C])
        x_rows = sb("x_rows", [P, RT, N])
        stats = sb("mix_stats", [P, RT, 6])
        mean_var = sb("mix_mean_var", [P, RT, 2])
        rstd = sb("mix_rstd", [P, RT])
        work = sb("mix_work", [P, 3, RT])
        fused = sb("mix_fused", [P, RT, N])
        normed = sb("mix_normed", [P, RT, N])
        products = ctx.enter_context(nc.psum_tensor("mix_products", [P, RT, N], F32))
        turned = ctx.enter_context(nc.psum_tensor("mix_turned", [P, 512], F32))
        w_in, x_in = sem("w_in"), sem("x_in")
        mixed_in = [sem(f"mixed_in{t}") for t in range(RT)]
        w_turned, w_ready, products_ready = sem("w_turned"), sem("mix_w_ready"), sem("mix_products_ready")
        step, eps_ready, std_ready, normed_ready, stored = (
            sem("mix_step"), sem("mix_eps"), sem("mix_std"), sem("mix_normed_ready"), sem("query_stored"))
        newton = Newton(nc, [work[:, i, :] for i in range(3)], std_ready)
        ctx.callback(lambda: clear_semaphores(nc, handles))
        block = ctx.enter_context(nc.Block())

        @block.sync
        def _(sp):
            sp.dma_start(w_mix[:], g["w_mix"]).then_inc(w_in, 16)
            for t in range(RT):
                sp.dma_start(mixed[:, t * BPT:(t + 1) * BPT, :],
                             g["feats"][t * BPT:(t + 1) * BPT].rearrange("b f n -> f b n")).then_inc(mixed_in[t], 16)
            sp.dma_start(x_rows[:], g["x"].rearrange("(t q) c n -> (q c) t n", q=BPT)).then_inc(x_in, 16)
            sp.wait_ge(normed_ready, 1)
            for q in range(BPT):
                sp.dma_start(query.rearrange("(t q) c n -> q c t n", q=BPT)[q], normed[q * C:(q + 1) * C])\
                    .then_inc(stored, 16)
            sp.wait_ge(stored, 16 * BPT)

        @block.tensor
        def _(pe):
            pe.wait_ge(w_in, 16)
            nc.tensor.transpose(turned[:, 0:C], w_mix[:], g["ident"][0:C, 0:C]).then_inc(w_turned, 1)
            pe.wait_ge(w_ready, 1)
            for t in range(RT):
                pe.wait_ge(mixed_in[t], 16)
                for q in range(BPT):
                    ins = nc.tensor.matmul(products[q * C:(q + 1) * C, t, :], w_mixT[:], mixed[:, t * BPT + q, :],
                                           start=True, stop=True)
                ins.then_inc(products_ready, 1)

        @block.scalar
        def _(act):
            act.wait_ge(w_turned, 1)
            nc.scalar.activation(w_mixT[:], turned[:, 0:C], ACT.Copy).then_inc(w_ready, 1)
            newton.on_scalar(act, eps_ready, 1, 1)
            newton.on_scalar(act, eps_ready, 2, 2)

        @block.vector
        def _(dve):
            vec = nc.vector
            chain = Step(dve, step)
            link = chain.then_wait

            def row_stats(tiles):
                for t in range(RT):
                    if tiles is products:
                        dve.wait_ge(products_ready, t + 1)
                    ins = vec.bn_stats(stats[:, t, :], tiles[:, t, :])
                link(ins)
                for t in range(RT):
                    ins = vec.bn_aggr(mean_var[:, t, :], stats[:, t, :])
                link(ins)

            row_stats(products)
            newton.on_vector(dve, link, mean_var[:, :, 1], rstd[:], eps_ready, 1)
            for t in range(RT):
                ins = vec.tensor_scalar(fused[:, t, :], products[:, t, :], mean_var[:, t, 0:1], rstd[:, t:t + 1],
                                        ALU.subtract, ALU.mult)
            link(ins)
            dve.wait_ge(x_in, 16)
            flat = "p t n -> p (t n)"
            link(vec.scalar_tensor_tensor(fused[:].rearrange(flat), fused[:].rearrange(flat), 0.2,
                                          fused[:].rearrange(flat), ALU.mult, ALU.max))
            link(vec.tensor_tensor(x1[:], x_rows[:], fused[:], ALU.add))
            row_stats(x1)
            newton.on_vector(dve, link, mean_var[:, :, 1], rstd[:], eps_ready, 2)
            for t in range(RT):
                ins = vec.tensor_scalar(normed[:, t, :], x1[:, t, :], mean_var[:, t, 0:1], rstd[:, t:t + 1],
                                        ALU.subtract, ALU.mult)
            ins.then_inc(normed_ready, 1)


def batch_attention(nc, g, query, message):
    QL = N // 4
    STEPS, SPAN = 4, QL // 4
    ITS, GROUPS, PAIR = SPAN // 8, 4, 2
    with ExitStack() as ctx:
        def sb(name, shape):
            return ctx.enter_context(nc.sbuf_tensor(name, shape, F32))

        handles = []

        def sem(name):
            handles.append(ctx.enter_context(nc.semaphore(name)))
            return handles[-1]

        queries = sb("queries", [P, B, QL])
        stage = sb("stage", [P, SPAN, B])
        values = sb("values", [P, ITS, P])
        row_max = sb("b_row_max", [P, 4 * ITS])
        logits = sb("logits", [P, 4, ITS, 32])
        row_sum = sb("b_row_sum", [P, 4 * ITS])
        attn = sb("attn", [P, 4, ITS, 32])
        attnT = sb("attnT", [P, 4, ITS, 32])
        said = sb("said", [P, B, QL])
        banks = ctx.enter_context(nc.psum_tensor("attn_banks", [P, 4, 512], F32))
        turned = ctx.enter_context(nc.psum_tensor("attn_turned", [P, ITS, P], F32))
        queries_in, stage_ready, mask_ready = sem("queries_in"), sem("stage_ready"), sem("apart_ready")
        scored, turned_ready, values_ready = sem("scored"), sem("values_turned"), sem("values_ready")
        logits_ready, exp_ready, attnT_ready, weighed, said_ready, stored = (
            sem("logits_ready"), sem("b_exp_ready"), sem("attnT_ready"), sem("weighed"), sem("said_ready"),
            sem("message_stored"))
        chained = sem("softmax_step")
        ctx.callback(lambda: clear_semaphores(nc, handles))
        block = ctx.enter_context(nc.Block())
        LINKS = 7

        @block.sync
        def _(sp):
            for quarter in range(4):
                sp.dma_start(queries[quarter * C:(quarter + 1) * C, :, :],
                             query[:, :, quarter * QL:(quarter + 1) * QL].rearrange("b c l -> c b l"))\
                    .then_inc(queries_in, 16)
            sp.wait_ge(said_ready, STEPS * GROUPS)
            for quarter in range(4):
                sp.dma_start(message[:, :, quarter * QL:(quarter + 1) * QL].rearrange("b c l -> c b l"),
                             said[quarter * C:(quarter + 1) * C, :, :]).then_inc(stored, 16)
            sp.wait_ge(stored, 64)

        @block.tensor
        def _(pe):
            for i in range(STEPS):
                pe.wait_ge(stage_ready, i + 1)
                for run in range(ITS):
                    ins = nc.tensor.transpose(turned[:, run, :], stage[:, run * 8:(run + 1) * 8, :]
                                              .rearrange("p l b -> p (l b)"), g["ident"][:])
                ins.then_inc(turned_ready, 1)
                for run in range(ITS):
                    for quarter in range(4):
                        for group in range(GROUPS):
                            at = run * 8 + group * PAIR
                            pair = stage[32 * quarter:32 * quarter + 32, at:at + PAIR, :].rearrange("p l b -> p (l b)")
                            ins = nc.tensor.matmul(
                                banks[32 * group:32 * group + 32, quarter, run * 32:run * 32 + 32], pair, pair,
                                start=True, stop=True)
                ins.then_inc(scored, 1)
                pe.wait_ge(values_ready, i + 1)
                pe.wait_ge(attnT_ready, i + 1)
                for run in range(ITS):
                    for quarter in range(4):
                        for group in range(GROUPS):
                            rows = slice(32 * group, 32 * group + 32)
                            ins = nc.tensor.matmul(
                                banks[32 * quarter:32 * quarter + 32, group, 256 + run * 32:256 + run * 32 + 32],
                                values[rows, run, 32 * quarter:32 * quarter + 32], attnT[rows, quarter, run, :],
                                start=True, stop=True)
                ins.then_inc(weighed, 1)

        @block.scalar
        def _(act):
            with act.Fori(0, STEPS) as i:
                act.wait_ge(turned_ready, i + 1)
                nc.scalar.activation(values[:], turned[:], ACT.Copy).then_inc(values_ready, 1)
                act.wait_ge(logits_ready, i + 1)
                nc.scalar.activation(attn[:], logits[:], ACT.Exp).then_inc(exp_ready, 1)

        @block.vector
        def _(dve):
            vec = nc.vector
            dve.wait_ge(queries_in, 64)
            whole = queries[:]
            with dve.Fori(0, STEPS) as i:
                vec.tensor_copy(stage[:], bass.AP(whole.tensor, whole.offset + i * SPAN,
                                                  [whole.ap[0], [1, SPAN], [QL, B]])).then_inc(stage_ready, 1)
                link = LoopStep(dve, chained, i, 5)
                dve.wait_ge(scored, i + 1)
                flat = "p q r c -> p (q r) c"
                link(vec.scalar_tensor_tensor(logits[:].rearrange("p q r c -> p q (r c)"), banks[:, :, 0:ITS * 32],
                                              1.0 / SQRT_HD, g["apart"][:].unsqueeze(1).broadcast_to([P, 4, ITS * 32]),
                                              ALU.mult, ALU.add))
                link(vec.tensor_reduce(row_max[:], logits[:].rearrange(flat), AX_X, ALU.max))
                vec.tensor_tensor(logits[:].rearrange(flat), logits[:].rearrange(flat),
                                  row_max[:].unsqueeze(2).broadcast_to([P, 4 * ITS, 32]), ALU.subtract)\
                    .then_inc(logits_ready, 1)
                dve.wait_ge(exp_ready, i + 1)
                link(vec.tensor_reduce(row_sum[:], attn[:].rearrange(flat), AX_X, ALU.add))
                link(vec.reciprocal(row_sum[:], row_sum[:]))
                link(vec.tensor_tensor(attn[:].rearrange(flat), attn[:].rearrange(flat),
                                       row_sum[:].unsqueeze(2).broadcast_to([P, 4 * ITS, 32]), ALU.mult))
                vec.transpose(attnT[:].rearrange("p q r c -> p (q r c)"), attn[:].rearrange("p q r c -> p (q r c)"))\
                    .then_inc(attnT_ready, 1)
                dve.wait_ge(weighed, i + 1)
                for group in range(GROUPS):
                    there, here = (bass.AP(tile.tensor, tile.offset + (i * SPAN + group * PAIR),
                                           [tile.ap[0], [8, ITS], [1, PAIR], [QL, B]]) for tile in (said[:], whole))
                    vec.tensor_tensor(there, banks[:, group, 256:256 + ITS * 32]
                                      .rearrange("p (r l b) -> p r l b", r=ITS, l=PAIR), here, ALU.add)\
                        .then_inc(said_ready, 1)


def feed_forward(nc, g, x1, message, out):
    HC, FC = H // P, FF // P
    with ExitStack() as ctx:
        def sb(name, shape):
            return ctx.enter_context(nc.sbuf_tensor(name, shape, F32))

        handles = []

        def sem(name):
            handles.append(ctx.enter_context(nc.semaphore(name)))
            return handles[-1]

        x2 = sb("x2", [P, RT, N])
        stats = sb("ff_stats", [P, RT, 6])
        mean_var = sb("ff_mean_var", [P, RT, 2])
        rstd = sb("ff_rstd", [P, RT])
        work = sb("ff_work", [P, 3, RT])
        normed = sb("ff_normed", [P, RT, H])
        normedT = sb("normedT", [P, HC, RT * P])
        sig = sb("sig", [P, 2, RT * P])
        silu = sb("silu", [P, 2, RT * P])
        hidden = sb("hidden", [P, FC, RT * P])
        result = sb("result", [P, RT, H])
        banks = ctx.enter_context(nc.psum_tensor("ff_banks", [P, 8, 512], F32))
        said_in, step, eps_ready, std_ready = sem("said_in"), sem("ff_step"), sem("ff_eps"), sem("ff_std")
        normed_ready, turned_ready, normedT_ready = sem("ff_normed_ready"), sem("ff_turned"), sem("normedT_ready")
        gated, sig_ready, silu_ready, hidden_ready = sem("gated"), sem("sig_ready"), sem("silu_ready"), sem("hidden_ready")
        down_done, result_ready, out_stored = sem("down_done"), sem("result_ready"), sem("out_stored")
        newton = Newton(nc, [work[:, i, :] for i in range(3)], std_ready)
        block = ctx.enter_context(nc.Block())

        @block.sync
        def _(sp):
            for q in range(BPT):
                sp.dma_start(x2[q * C:(q + 1) * C], message.rearrange("(t q) c n -> q c t n", q=BPT)[q])\
                    .then_inc(said_in, 16)
            for t in range(RT):
                sp.wait_ge(result_ready, t + 1)
                for q in range(BPT):
                    sp.dma_start(out[t * BPT + q], result[q * C:(q + 1) * C, t, :]).then_inc(out_stored, 16)
            sp.wait_ge(out_stored, 16 * B)

        @block.tensor
        def _(pe):
            for t in range(RT):
                pe.wait_ge(normed_ready, t + 1)
                for c in range(HC):
                    ins = nc.tensor.transpose(banks[:, t, c * P:(c + 1) * P], normed[:, t, c * P:(c + 1) * P],
                                              g["ident"][:])
                ins.then_inc(turned_ready, 1)
            pe.wait_ge(normedT_ready, RT)
            for f in range(FC):
                if f >= 2:
                    pe.wait_ge(hidden_ready, f - 1)
                for bank, w in ((4 + f % 2, g["gateT"]), (6 + f % 2, g["upT"])):
                    for c in range(HC):
                        ins = nc.tensor.matmul(banks[:, bank, :], w[:, c, f * P:(f + 1) * P], normedT[:, c, :],
                                               start=(c == 0), stop=(c == HC - 1))
                ins.then_inc(gated, 1)
            for t in range(RT):
                for f in range(FC):
                    if t == 0:
                        pe.wait_ge(hidden_ready, f + 1)
                    ins = nc.tensor.matmul(banks[:, t, :], hidden[:, f, t * P:(t + 1) * P], g["downT"][:, f, :],
                                           start=(f == 0), stop=(f == FC - 1))
                ins.then_inc(down_done, 1)

        @block.scalar
        def _(act):
            newton.on_scalar(act, eps_ready, 1, 1)
            for t in range(RT):
                act.wait_ge(turned_ready, t + 1)
                nc.scalar.activation(normedT[:, :, t * P:(t + 1) * P],
                                     banks[:, t, :].rearrange("p (c k) -> p c k", c=HC), ACT.Copy)\
                    .then_inc(normedT_ready, 1)
            for f in range(FC):
                act.wait_ge(gated, f + 1)
                if f >= 2:
                    act.wait_ge(silu_ready, f - 1)
                nc.scalar.activation(sig[:, f % 2], banks[:, 4 + f % 2, :], ACT.Sigmoid).then_inc(sig_ready, 1)

        @block.vector
        def _(dve):
            vec = nc.vector
            chain = Step(dve, step)
            link = chain.then_wait
            dve.wait_ge(said_in, 16 * BPT)
            link(vec.tensor_tensor(x2[:], x2[:], x1[:], ALU.add))
            for t in range(RT):
                ins = vec.bn_stats(stats[:, t, :], x2[:, t, :])
            link(ins)
            for t in range(RT):
                ins = vec.bn_aggr(mean_var[:, t, :], stats[:, t, :])
            link(ins)
            newton.on_vector(dve, link, mean_var[:, :, 1], rstd[:], eps_ready, 1)
            for t in range(RT):
                vec.tensor_scalar(normed[:, t, :], x2[:, t, :], mean_var[:, t, 0:1], rstd[:, t:t + 1],
                                  ALU.subtract, ALU.mult).then_inc(normed_ready, 1)
            for f in range(FC):
                dve.wait_ge(sig_ready, f + 1)
                vec.tensor_tensor(silu[:, f % 2], sig[:, f % 2], banks[:, 4 + f % 2, :], ALU.mult)\
                    .then_inc(silu_ready, 1)
                dve.wait_ge(silu_ready, f + 1)
                vec.tensor_tensor(hidden[:, f, :], silu[:, f % 2], banks[:, 6 + f % 2, :], ALU.mult)\
                    .then_inc(hidden_ready, 1)
            for t in range(RT):
                dve.wait_ge(down_done, t + 1)
                vec.tensor_tensor(result[:, t, :], banks[:, t, :], x2[:, t, :], ALU.add).then_inc(result_ready, 1)


def setup_constants(nc, g):
    with ExitStack() as ctx:
        done = ctx.enter_context(nc.semaphore("constants_step"))
        made = ctx.enter_context(nc.semaphore("partition_bit"))
        number = ctx.enter_context(nc.sbuf_tensor("partition_number", [P, P], I32))
        ctx.callback(lambda: clear_semaphores(nc, [done, made]))
        block = ctx.enter_context(nc.Block())

        @block.gpsimd
        def _(pool):
            gp = nc.gpsimd
            count = 0
            gp.iota(number[:], pattern=[[0, P]], base=0, channel_multiplier=1).then_inc(made, 1)
            gp.iota(g["point"][:], pattern=[[P, 4]], base=0, channel_multiplier=1,
                    allow_small_or_imprecise_dtypes=True)
            for tile, period, value in ((g["ident"], P, 1.0), (g["average"][0], g["O"][0], 1.0 / STRIPS),
                                        (g["average"][1], g["O"][1], 1.0 / STRIPS)):
                ins = gp.memset(tile[:], 0.0)
                for shift in range(-(P // period - 1) * period, P, period):
                    count += 1
                    ins.then_inc(done, 1)
                    pool.wait_ge(done, count)
                    ins = gp.affine_select(out=tile[:], in_=tile[:], compare_op=ALU.not_equal, fill=value,
                                           base=shift, pattern=[[-1, P]], channel_multiplier=1)

        @block.vector
        def _(dve):
            vec = nc.vector
            chain = Step(dve, made)
            chain.count = 1
            dve.wait_ge(made, 1)
            chain.then_wait(vec.tensor_scalar(number[:], number[:], 4, 1, ALU.logical_shift_right, ALU.bitwise_and))
            halves = [v[:].rearrange("p (r j b) -> p r j b", j=2, b=B) for v in (g["apart"], number)]
            vec.tensor_scalar(halves[0][:, :, 0, :], halves[1][:, :, 0, :], -MASK, None, ALU.mult)
            vec.tensor_scalar(halves[0][:, :, 1, :], halves[1][:, :, 1, :], MASK, -MASK, ALU.mult, ALU.add)


def program(nc, g, out):
    g["O"] = (C, 2 * C)
    with ExitStack() as ctx:
        def sb(name, shape, dt=F32):
            return ctx.enter_context(nc.sbuf_tensor(name, shape, dt))

        g["feats"] = nc.dram_tensor("feats_scratch", [B, P, N], F32).ap()
        g["orders"] = nc.dram_tensor("orders_scratch", [METHODS * B, N], F16).ap()
        query = nc.dram_tensor("query_scratch", [B, C, N], F32).ap()
        message = nc.dram_tensor("message_scratch", [B, C, N], F32).ap()
        g["gateT"] = sb("gateT", [P, H // P, FF])
        g["upT"] = sb("upT", [P, H // P, FF])
        g["downT"] = sb("downT", [P, FF // P, H])
        g["ident"] = sb("ident", [P, P])
        g["average"] = [sb("average0", [P, P]), sb("average1", [P, P])]
        g["point"] = sb("point", [P, 4])
        g["apart"] = sb("apart", [P, P])
        g["raw_in"] = [ctx.enter_context(nc.semaphore(f"raw_in{i}")) for i in range(2)]
        g["scales_in"] = ctx.enter_context(nc.semaphore("scales_in"))
        setup_constants(nc, g)
        sort_and_prepare(nc, g)
        for layer in range(2):
            strips = P // g["O"][layer]
            with nc.sbuf_tensor(f"sorted_rows_{layer}", [P, B, SW], F32) as sorted_rows, \
                 nc.sbuf_tensor(f"hmax_{layer}", [P, B, STRIPS // strips, SP_PTS], F32) as hmax, \
                 nc.sbuf_tensor(f"hstats_{layer}", [P, B, STRIPS // strips * 24], F32) as hstats:
                gather_windows(nc, g, layer, sorted_rows[:])
                window_attention(nc, g, layer, sorted_rows[:], hmax[:], hstats[:])
                close_layer(nc, g, layer, hmax[:], hstats[:])
        x1 = sb("x1", [P, RT, N])
        mix_features(nc, g, x1, query)
        batch_attention(nc, g, query, message)
        feed_forward(nc, g, x1, message, out)


_INS = ["x", "ctx_4096", "L0_xattn_W_lin1", "L0_xattn_b_lin1", "L0_xattn_W_lin2", "L0_xattn_b_lin2",
        "L0_xattn_W_conv1", "L0_xattn_W_conv2", "L0_xattn_W_conv3", "L0_ffn_gate_wq", "L0_ffn_gate_scale",
        "L0_ffn_up_wq", "L0_ffn_up_scale", "L0_ffn_down_wq", "L0_ffn_down_scale"]


def kernel(**inputs):
    import concourse.bacc as bacc
    from concourse.bass_utils import run_bass_kernel_spmd

    nc = bacc.Bacc("TRN2", target_bir_lowering=False, num_devices=1)
    arrays, aps = {}, {}
    for name in _INS:
        a = np.ascontiguousarray(inputs[name])
        arrays[f"in_{name}"] = a
        aps[name] = nc.dram_tensor(f"in_{name}", a.shape, mybir.dt.from_np(a.dtype), kind="ExternalInput").ap()
    out = nc.dram_tensor("out_x", (B, C, N), F32, kind="ExternalOutput").ap()
    x = "L0_xattn_"
    g = {"x": aps["x"], "ctx": aps["ctx_4096"],
         "w_lin": [aps[x + "W_lin1"], aps[x + "W_lin2"]], "b_lin": [aps[x + "b_lin1"], aps[x + "b_lin2"]],
         "w_conv": [aps[x + "W_conv1"], aps[x + "W_conv2"]], "w_mix": aps[x + "W_conv3"]}
    for name in ("gate", "up", "down"):
        g[name + "_wq"] = aps[f"L0_ffn_{name}_wq"]
        g[name + "_scale"] = aps[f"L0_ffn_{name}_scale"]
    program(nc, g, out)
    r = run_bass_kernel_spmd(nc, [arrays], core_ids=[0])
    return r.results[0]["out_x"]
```

```python
from contextlib import ExitStack

import numpy as np
import concourse.bass as bass
from concourse import mybir

ALU = mybir.AluOpType
ACT = mybir.ActivationFunctionType
AX_X = mybir.AxisListType.X
F32, F16, BF16 = mybir.dt.float32, mybir.dt.float16, mybir.dt.bfloat16
I32, U32 = mybir.dt.int32, mybir.dt.uint32

P = 128
B, C, N, H = 16, 32, 512, 512
FF = 1792
RT = B * C // P
BPT = P // C
NBITS = 10
METHODS, WIN, HEADS, HD = 4, 10, 4, 32
PERMS = ((2, 0, 3, 1), (1, 3, 0, 2))
BACK = 5
SQRT_HD = float(np.float32(np.sqrt(HD)))
EPS = 1e-5

STRIPS, SUB, TRI = 4, 4, 3
PTS = SUB * TRI
SP_PTS = N // STRIPS
CHUNKS = -(-SP_PTS // PTS)
SP_PAD = CHUNKS * PTS
COLS = STRIPS * PTS * WIN
BLK = TRI * WIN
PITCH = 32 + WIN
NBLK = STRIPS * SUB
SW = BACK + N + 8
MASK = float(2 ** 22)
VECTOR_HEADS = 2
WARM_FIRST, WARM_EACH, WARM_EDGE = 4, (1, 0), 3
FLOOR = float(2 ** 23)


class Step:

    def __init__(self, engine, sem):
        self.engine, self.sem, self.count = engine, sem, 0

    def then_wait(self, ins):
        self.count += 1
        ins.then_inc(self.sem, 1)
        self.engine.wait_ge(self.sem, self.count)


class LoopStep:

    def __init__(self, engine, sem, i, per):
        self.engine, self.sem, self.i, self.per, self.count = engine, sem, i, per, 0

    def __call__(self, ins):
        self.count += 1
        assert self.count <= self.per
        ins.then_inc(self.sem, 1)
        self.engine.wait_ge(self.sem, self.i * self.per + self.count)


def clear_semaphores(nc, handles):
    with nc.Block() as block:
        @block.sync
        def _(sp):
            numbers = sorted(h.num for h in handles)
            start = numbers[0]
            for n, after in zip(numbers, numbers[1:] + [None]):
                if after != n + 1:
                    sp.sem_clear(range(start, n + 1))
                    start = after


class Newton:

    def __init__(self, nc, work, std_ready):
        self.nc, self.work, self.std_ready = nc, work, std_ready

    def on_scalar(self, act, shifted_ready, count, value):
        act.wait_ge(shifted_ready, value)
        self.nc.scalar.activation(self.work[1], self.work[0], ACT.Sqrt).then_inc(self.std_ready, 1)

    def on_vector(self, dve, link, var, rstd, shifted_ready, value):
        vec = self.nc.vector
        a, s, t = self.work[0], self.work[1], self.work[2]
        vec.tensor_scalar(a, var, EPS, None, ALU.add).then_inc(shifted_ready, 1)
        dve.wait_ge(self.std_ready, value)
        link(vec.reciprocal(rstd, s))
        link(vec.tensor_tensor(t, rstd, rstd, ALU.mult))
        link(vec.tensor_tensor(t, t, a, ALU.mult))
        link(vec.tensor_scalar(t, t, -0.5, 1.5, ALU.mult, ALU.add))
        link(vec.tensor_tensor(rstd, rstd, t, ALU.mult))


def sort_and_prepare(nc, g):
    ctx_in, x_in, feats, orders = g["ctx"], g["x"], g["feats"], g["orders"]
    with ExitStack() as ctx:
        def sb(name, shape, dt):
            return ctx.enter_context(nc.sbuf_tensor(name, shape, dt))

        handles = []

        def sem(name):
            handles.append(ctx.enter_context(nc.semaphore(name)))
            return handles[-1]

        coords = sb("coords", [P, 3, N], F32)
        lo = sb("lo", [P, 3], F32)
        hi = sb("hi", [P, 3], F32)
        small = sb("small", [P, 14, 3], F32)
        pos = sb("pos", [P, 3, P], F32)
        near = sb("near", [P, 3, P], F32)
        over = sb("over", [P, 3, P], F32)
        code = sb("code", [P, 2, 3, P], I32)
        spread = sb("spread", [P, 2, 3, P], I32)
        bit = sb("bit", [P, P], I32)
        bits = sb("bits", [P, 3, P], I32)
        notbits = sb("notbits", [P, 2, P], I32)
        turned_over = sb("turned_over", [P, P], I32)
        diff = sb("diff", [P, P], I32)
        key = sb("key", [P, 2, P], I32)
        high = sb("high", [P, 2, P], I32)
        low = sb("low", [P, 2, P], I32)
        keys = sb("keys", [METHODS * B, N], F32)
        top = sb("top", [METHODS * B, 2, 8], F32)
        where = sb("where", [METHODS * B, N], U32)
        order = sb("order", [METHODS * B, N], F16)
        rows = sb("rows", [P, RT, N], F32)
        normed = sb("normed", [P, RT, N], F32)
        stats = sb("stats", [P, RT, 6], F32)
        mean_var = sb("mean_var", [P, RT, 2], F32)
        rstd = sb("rstd", [P, RT], F32)
        work = sb("work", [P, 3, RT], F32)
        newton_std = sem("newton_std")
        newton = Newton(nc, [work[:, i, :] for i in range(3)], newton_std)
        raw = sb("raw", [P, 2, FF], I32)
        scales = sb("scales", [P, 32], F32)
        deq = sb("deq", [P, 2, FF], F32)
        turned = [ctx.enter_context(nc.psum_tensor(f"turned{i}", [P, 4, P], F32)) for i in range(4)]

        coords_in, x_loaded = sem("coords_in"), sem("x_loaded")
        raw_in, scales_in = g["raw_in"], g["scales_in"]
        step, var_ready, normed_ready = sem("step"), sem("var_ready"), sem("normed_ready")
        code_ready, keys_in, order_ready, stored = sem("code_ready"), sem("keys_in"), sem("order_ready"), sem("stored")
        deq_ready, turned_ready, turned_out = sem("deq_ready"), sem("turned_ready"), sem("turned_out")
        ctx.callback(lambda: clear_semaphores(nc, handles))
        block = ctx.enter_context(nc.Block())

        gate_blocks = [("gate", i, H) for i in range(FF // P)]
        up_blocks = [("up", i, H) for i in range(FF // P)]
        down_blocks = [("down", i, FF) for i in range(H // P)]
        loads = []
        for name in ("gate", "up"):
            i = 0
            while i < FF // P:
                m = min(3, FF // P - i)
                loads.append((name, i, m))
                i += m
        loads += [("down", i, 1) for i in range(H // P)]

        def scale_col(name, i):
            return {"gate": 0, "up": FF // P, "down": 2 * (FF // P)}[name] + i

        def groups():
            out = []
            for n, (name, i0, m) in enumerate(loads):
                if name == "down":
                    for j in range(0, FF // P, 4):
                        k = min(4, FF // P - j)
                        out.append((n, [(j + t) * P for t in range(k)],
                                    g["downT"][:, j:j + k, i0 * P:(i0 + 1) * P]))
                else:
                    for r in range(m):
                        out.append((n, [r * H + t * P for t in range(4)],
                                    g[name + "T"][:, :, (i0 + r) * P:(i0 + r + 1) * P]))
            return out

        GROUPS = groups()

        def load_coords(engine, quarter):
            at = quarter * 32
            engine.dma_start(coords[at:at + B, :, :], ctx_in[:, 0:3, :]).then_inc(coords_in, 16)
            engine.dma_start(coords[at + B:at + 2 * B, 0:3:2, :], ctx_in[:, 1:3, :]).then_inc(coords_in, 16)
            engine.dma_start(coords[at + B:at + 2 * B, 1, :], ctx_in[:, 0, :]).then_inc(coords_in, 16)

        def gather_keys(engine, kind):
            engine.wait_ge(code_ready, 1)
            for quarter in range(4):
                engine.dma_start(keys[kind * 32:kind * 32 + 32, quarter * P:(quarter + 1) * P],
                                 key[quarter * 32:quarter * 32 + 32, kind, :].bitcast(F32)).then_inc(keys_in, 16)

        @block.sync
        def _(sp):
            load_coords(sp, 0)
            load_coords(sp, 1)
            sp.dma_start(rows[:], x_in.rearrange("(t q) c n -> (q c) t n", q=BPT)).then_inc(x_loaded, 16)
            gather_keys(sp, 0)
            sp.wait_ge(normed_ready, RT)
            for t in range(RT):
                for q in range(BPT):
                    sp.dma_start(feats[t * BPT + q, 0:C, :], normed[q * C:(q + 1) * C, t, :]).then_inc(stored, 16)
            sp.wait_ge(order_ready, 1)
            sp.dma_start(orders[:, :], order[:]).then_inc(stored, 16)
            sp.wait_ge(stored, 16 * (B + 1))

        @block.gpsimd
        def _(pool):
            wq = {"gate": g["gate_wq"], "up": g["up_wq"], "down": g["down_wq"]}
            for name in ("gate", "up", "down"):
                n = FF // P if name != "down" else H // P
                c = scale_col(name, 0)
                with nc.allow_non_contiguous_dma("scales, one per partition"):
                    pool.dma_start(scales[:, c:c + n], g[name + "_scale"].rearrange("(n p) -> p n", p=P))\
                        .then_inc(scales_in, 16)
            for n, (name, i, m) in enumerate(loads):
                if n >= 2:
                    pool.wait_ge(deq_ready, n - 1)
                width = H if name != "down" else FF
                src = wq[name][i * P:(i + m) * P, :].rearrange("(m p) w -> p m w", p=P)
                dst = raw[:, n % 2, 0:m * width].rearrange("p (m w) -> p m w", m=m)
                pool.dma_start(dst, src).then_inc(raw_in[n % 2], 16)

        @block.scalar
        def _(act):
            load_coords(act, 2)
            load_coords(act, 3)
            act.wait_ge(scales_in, 48)
            done = 0
            for n, (name, i, m) in enumerate(loads):
                width = H if name != "down" else FF
                act.wait_ge(raw_in[n % 2], 16 * (n // 2 + 1))
                if n >= 2:
                    act.wait_ge(turned_ready, sum(1 for q in GROUPS if q[0] <= n - 2))
                for r in range(m):
                    c = scale_col(name, i + r)
                    ins = nc.scalar.activation(deq[:, n % 2, r * width:(r + 1) * width],
                                               raw[:, n % 2, r * width:(r + 1) * width], ACT.Copy,
                                               scale=scales[:, c:c + 1])
                ins.then_inc(deq_ready, 1)
                if n >= 1:
                    for k, (load, cols, dst) in enumerate(GROUPS):
                        if load == n - 1:
                            act.wait_ge(turned_ready, k + 1)
                            nc.scalar.activation(dst, turned[k % 4][:, 0:len(cols), :], ACT.Copy)\
                                .then_inc(turned_out, 1)
            for k, (load, cols, dst) in enumerate(GROUPS):
                if load == len(loads) - 1:
                    act.wait_ge(turned_ready, k + 1)
                    nc.scalar.activation(dst, turned[k % 4][:, 0:len(cols), :], ACT.Copy).then_inc(turned_out, 1)
            gather_keys(act, 1)
            newton.on_scalar(act, var_ready, 1, 1)

        @block.tensor
        def _(pe):
            for k, (load, cols, dst) in enumerate(GROUPS):
                pe.wait_ge(deq_ready, load + 1)
                if k >= 4:
                    pe.wait_ge(turned_out, k - 3)
                for t, c in enumerate(cols):
                    ins = nc.tensor.transpose(turned[k % 4][:, t, :], deq[:, load % 2, c:c + P], g["ident"][:])
                ins.then_inc(turned_ready, 1)

        @block.vector
        def _(dve):
            chain = Step(dve, step)
            link = chain.then_wait
            vec = nc.vector
            dve.wait_ge(coords_in, 192)
            vec.tensor_reduce(lo[:], coords[:], AX_X, ALU.min)
            link(vec.tensor_reduce(hi[:], coords[:], AX_X, ALU.max))
            top_q = float(2 ** NBITS - 1)
            d, r, y, t0, t1, yh, yl, dh, dl, pr, er, sc = (small[:, i, :] for i in range(12))
            link(vec.tensor_tensor(d, hi[:], lo[:], ALU.subtract))
            link(vec.tensor_scalar(d, d, 1e-6, None, ALU.add))
            link(vec.reciprocal(r, d))
            link(vec.tensor_scalar(y, r, top_q, None, ALU.mult))

            def halves(v, vh, vl):
                link(vec.tensor_scalar(t0, v, 4097.0, None, ALU.mult))
                link(vec.tensor_tensor(t1, t0, v, ALU.subtract))
                link(vec.tensor_tensor(vh, t0, t1, ALU.subtract))
                link(vec.tensor_tensor(vl, v, vh, ALU.subtract))

            halves(y, yh, yl)
            halves(d, dh, dl)
            link(vec.tensor_tensor(pr, y, d, ALU.mult))
            link(vec.tensor_tensor(er, yh, dh, ALU.mult))
            link(vec.tensor_tensor(er, er, pr, ALU.subtract))
            for a, b in ((yh, dl), (yl, dh), (yl, dl)):
                link(vec.tensor_tensor(t0, a, b, ALU.mult))
                link(vec.tensor_tensor(er, er, t0, ALU.add))
            link(vec.tensor_scalar(t0, pr, -1.0, top_q, ALU.mult, ALU.add))
            link(vec.tensor_tensor(t0, t0, er, ALU.subtract))
            link(vec.tensor_tensor(t0, t0, r, ALU.mult))
            link(vec.tensor_tensor(sc, y, t0, ALU.add))
            for quarter in range(4):
                at = slice(quarter * 32, quarter * 32 + 32)
                ins = vec.tensor_tensor(pos[at], coords[at, :, quarter * P:(quarter + 1) * P],
                                        lo[at].unsqueeze(2).broadcast_to([32, 3, P]), ALU.subtract)
            link(ins)
            link(vec.tensor_tensor(pos[:], pos[:], sc.unsqueeze(2).broadcast_to([P, 3, P]), ALU.mult))
            link(vec.tensor_scalar(near[:], pos[:], FLOOR, FLOOR, ALU.add, ALU.subtract))
            link(vec.tensor_tensor(over[:], near[:], pos[:], ALU.is_gt))
            link(vec.tensor_tensor(near[:], near[:], over[:], ALU.subtract))
            for kind in range(2):
                ins = vec.tensor_scalar(code[:, kind], near[:], 0.0, top_q, ALU.max, ALU.min)
            link(ins)

            X = [code[:, 1, i, :] for i in range(3)]
            for k in range(NBITS - 1, 0, -1):
                mask = (1 << k) - 1
                link(vec.tensor_scalar(bits[:], code[:, 1], 31 - k, 31, ALU.logical_shift_left,
                                       ALU.arith_shift_right))
                vec.tensor_scalar(notbits[:], bits[:, 1:3], -1, mask, ALU.bitwise_xor, ALU.bitwise_and)
                link(vec.scalar_tensor_tensor(X[0], bits[:, 0], mask, X[0], ALU.bitwise_and, ALU.bitwise_xor))
                for i in (1, 2):
                    vec.tensor_tensor(diff[:], X[0], X[i], ALU.bitwise_xor)
                    link(vec.scalar_tensor_tensor(turned_over[:], bits[:, i], mask, X[0], ALU.bitwise_and,
                                                  ALU.bitwise_xor))
                    link(vec.tensor_tensor(diff[:], diff[:], notbits[:, i - 1], ALU.bitwise_and))
                    vec.tensor_tensor(X[i], X[i], diff[:], ALU.bitwise_xor)
                    link(vec.tensor_tensor(X[0], turned_over[:], diff[:], ALU.bitwise_xor))
            for i in (1, 2):
                link(vec.tensor_tensor(X[i], X[i], X[i - 1], ALU.bitwise_xor))
            link(vec.tensor_scalar(bit[:], X[2], 1, None, ALU.logical_shift_right))
            for s in (1, 2, 4, 8):
                link(vec.scalar_tensor_tensor(bit[:], bit[:], s, bit[:], ALU.logical_shift_right,
                                              ALU.bitwise_xor))
            for i in range(3):
                ins = vec.tensor_tensor(X[i], X[i], bit[:], ALU.bitwise_xor)
            link(ins)

            for s, m in ((16, 0x030000FF), (8, 0x0300F00F), (4, 0x030C30C3), (2, 0x09249249)):
                link(vec.scalar_tensor_tensor(spread[:], code[:], s, code[:], ALU.logical_shift_left,
                                              ALU.bitwise_or))
                link(vec.tensor_scalar(code[:], spread[:], m, None, ALU.bitwise_and))
            link(vec.scalar_tensor_tensor(key[:], code[:, :, 0, :], 2, code[:, :, 2, :],
                                          ALU.logical_shift_left, ALU.bitwise_or))
            link(vec.scalar_tensor_tensor(key[:], code[:, :, 1, :], 1, key[:], ALU.logical_shift_left,
                                          ALU.bitwise_or))
            link(vec.tensor_scalar(high[:], key[:], 23, None, ALU.logical_shift_right))
            link(vec.tensor_scalar(high[:], high[:], 1, None, ALU.add))
            link(vec.tensor_scalar(low[:], key[:], (1 << 23) - 1, -(1 << 31), ALU.bitwise_and, ALU.bitwise_or))
            vec.scalar_tensor_tensor(key[:], high[:], 23, low[:], ALU.logical_shift_left,
                                     ALU.bitwise_or).then_inc(code_ready, 1)

            dve.wait_ge(x_loaded, 16)
            for t in range(RT):
                link(vec.bn_stats(stats[:, t, :], rows[:, t, :]))
                ins = vec.bn_aggr(mean_var[:, t, :], stats[:, t, :])
            link(ins)
            newton.on_vector(dve, link, mean_var[:, :, 1], rstd[:], var_ready, 1)
            for t in range(RT):
                vec.tensor_scalar(normed[:, t, :], rows[:, t, :], mean_var[:, t, 0:1], rstd[:, t:t + 1],
                                  ALU.subtract, ALU.mult).then_inc(normed_ready, 1)

            dve.wait_ge(keys_in, 128)
            for t in range(N // 8):
                link(vec.max(top[:, t % 2, :], keys[:]))
                vec.max_index(where[:, 8 * t:8 * t + 8], top[:, t % 2, :], keys[:])
                link(vec.match_replace(keys[:], top[:, t % 2, :], keys[:], -3e38))
            vec.tensor_copy(order[:], where[:]).then_inc(order_ready, 1)


def gather_windows(nc, g, layer, sorted_rows):
    feats, orders, perm = g["feats"], g["orders"], PERMS[layer]
    first = layer * C
    with ExitStack() as ctx:
        def sb(name, shape, dt):
            return ctx.enter_context(nc.sbuf_tensor(f"{name}_{layer}", shape, dt))

        handles = []

        def sem(name):
            handles.append(ctx.enter_context(nc.semaphore(f"{name}_{layer}")))
            return handles[-1]

        rows = sb("feature_rows", [P, RT, N], F32)
        by_point = sb("by_point", [P, 4, B, 3, C], BF16)
        rest = sb("rest", [P, 2, 4, P], F32)
        ordered = sb("ordered", [P, 2, METHODS, N], F16)
        hot = sb("hot", [P, 2, 4, METHODS, N], BF16)
        parts = sb("parts", [P, 2, 4, 3, C], BF16)
        gathered = sb("gathered", [P, 2, N], F32)
        to_heads = sb("to_heads", [P, P], F32)
        products = ctx.enter_context(nc.psum_tensor(f"products_{layer}", [P, 2, 512], F32))
        permuted = ctx.enter_context(nc.psum_tensor(f"permuted_{layer}", [P, 2, 512], F32))
        turned = ctx.enter_context(nc.psum_tensor(f"turned_{layer}", [P, RT, 512], F32))

        rows_in = [sem(f"rows_in{t}") for t in range(RT)]
        turned_ready, step = sem("turned_ready"), sem("split_step")
        split_ready = sem("split_ready")
        order_in = [sem("order_in0"), sem("order_in1")]
        hot_ready, products_ready, gathered_ready = sem("hot_ready"), sem("products_ready"), sem("gathered_ready")
        window_turned, rows_ready, to_heads_ready = sem("window_turned"), sem("rows_ready"), sem("to_heads_ready")
        ctx.callback(lambda: clear_semaphores(nc, handles))
        block = ctx.enter_context(nc.Block())

        @block.sync
        def _(sp):
            def load_rows(t):
                for q in range(BPT):
                    sp.dma_start(rows[q * C:(q + 1) * C, t, :], feats[t * BPT + q, first:first + C, :])\
                        .then_inc(rows_in[t], 16)

            def load_orders(b, parity):
                src = bass.AP(orders.tensor, orders.offset + b * N, [[0, P], [B * N, METHODS], [1, N]])
                sp.dma_start(ordered[:, parity], src).then_inc(order_in[parity], 16)

            load_orders(0, 0)
            load_rows(0)
            load_orders(1, 1)
            for t in range(1, RT):
                load_rows(t)
            with sp.Fori(0, B // 2 - 1) as bp:
                for half in range(2):
                    sp.wait_ge(hot_ready, bp * 10 + (5 * half + 4))
                    load_orders(bp * 2 + (2 + half), half)

        @block.vector
        def _(dve):
            vec = nc.vector
            chain = Step(dve, step)
            link = chain.then_wait

            def make_hot(b, pair, half, used=None):
                if used is not None:
                    dve.wait_ge(products_ready, used)
                dve.wait_ge(order_in[half], pair * 16 + 16)
                for c in range(4):
                    vec.tensor_scalar(hot[:, half, c], ordered[:, half], g["point"][:, c:c + 1], None,
                                      ALU.is_equal).then_inc(hot_ready, 1)

            def take_parts(b, half):
                vec.tensor_copy(parts[:, half], by_point[:, :, b, :, :]).then_inc(hot_ready, 1)

            make_hot(0, 0, 0)
            def split(t):
                if t:
                    dve.wait_ge(split_ready, t)
                dve.wait_ge(turned_ready, t + 1)
                src = turned[:, t, :].rearrange("p (c f) -> p c f", c=4)
                tile_parts = by_point[:, :, t * BPT:(t + 1) * BPT, :, :].rearrange("p c q s f -> p s c q f")
                as_rows = [rest[:, i].rearrange("p c (q f) -> p c q f", q=BPT) for i in range(2)]
                part = [tile_parts[:, s] for s in range(3)]
                link(vec.tensor_copy(rest[:, 0], src))
                for c in range(4):
                    ins = vec.tensor_copy(part[0][:, c], as_rows[0][:, c])
                link(ins)
                for s in (1, 2):
                    for c in range(4):
                        ins = vec.tensor_tensor(as_rows[s % 2][:, c], as_rows[(s + 1) % 2][:, c],
                                                part[s - 1][:, c], ALU.subtract)
                    link(ins)
                    for c in range(4):
                        ins = vec.tensor_copy(part[s][:, c], as_rows[s % 2][:, c])
                    if s == 1:
                        link(ins)
                ins.then_inc(split_ready, 1)

            def hot_pairs(start, stop, splits):
                with dve.Fori(start, stop) as bp:
                    dve.wait_ge(split_ready, splits)
                    for half in range(2):
                        make_hot(bp * 2 + half, bp, half, bp * 2 + (half - 1))
                        take_parts(bp * 2 + half, half)

            split(0)
            dve.wait_ge(split_ready, 1)
            take_parts(0, 0)
            make_hot(1, 0, 1)
            take_parts(1, 1)
            for t in range(1, RT):
                split(t)
                hot_pairs(2 * t - 1, 2 * t + 1 if t < RT - 1 else B // 2, t + 1)
            vec.memset(sorted_rows[:, :, 0:BACK], 0.0)
            dve.wait_ge(rows_ready, B)
            vec.tensor_copy(sorted_rows[:, :, BACK + N:SW],
                            sorted_rows[:, :, BACK + N - 1:BACK + N].broadcast_to([P, B, SW - BACK - N]))

        @block.tensor
        def _(pe):
            for t in range(RT):
                pe.wait_ge(rows_in[t], 16 * BPT)
                for c in range(4):
                    ins = nc.tensor.transpose(turned[:, t, c * P:(c + 1) * P], rows[:, t, c * P:(c + 1) * P],
                                              g["ident"][:])
                ins.then_inc(turned_ready, 1)
            def one_batch(b, half):
                pe.wait_ge(hot_ready, b * 5 + 5)
                for c in range(4):
                    for s in range(3):
                        for place in range(METHODS):
                            ins = nc.tensor.matmul(products[32 * place:32 * place + 32, half, :],
                                                   parts[:, half, c, s, :], hot[:, half, c, perm[place], :],
                                                   start=(c == 0 and s == 0), stop=(c == 3 and s == 2),
                                                   skip_group_check=True)
                ins.then_inc(products_ready, 1)

            def to_heads_of(b, half):
                pe.wait_ge(gathered_ready, b + 1)
                nc.tensor.matmul(permuted[:, half, :], to_heads[:], gathered[:, half, :], start=True, stop=True)\
                    .then_inc(window_turned, 1)

            pe.wait_ge(to_heads_ready, 1)
            one_batch(0, 0)
            one_batch(1, 1)
            to_heads_of(0, 0)
            with pe.Fori(1, B // 2) as bp:
                one_batch(bp * 2, 0)
                to_heads_of(bp * 2 - 1, 1)
                one_batch(bp * 2 + 1, 1)
                to_heads_of(bp * 2, 0)
            to_heads_of(B - 1, 1)

        @block.scalar
        def _(act):
            def copy_rows(b, half):
                act.wait_ge(window_turned, b + 1)
                nc.scalar.activation(sorted_rows[:, b, BACK:BACK + N], permuted[:, half, :], ACT.Copy)\
                    .then_inc(rows_ready, 1)

            def copy_products(b, half):
                act.wait_ge(products_ready, b + 1)
                nc.scalar.activation(gathered[:, half, :], products[:, half, :], ACT.Copy)\
                    .then_inc(gathered_ready, 1)

            nc.scalar.activation(to_heads[:].rearrange("p (h m f) -> p m h f", h=HEADS, m=METHODS),
                                 g["ident"][:].rearrange("p (m h f) -> p m h f", h=HEADS, m=METHODS), ACT.Copy)\
                .then_inc(to_heads_ready, 1)
            copy_products(0, 0)
            for b in range(B):
                if b + 1 < B:
                    copy_products(b + 1, (b + 1) % 2)
                copy_rows(b, b % 2)


def window_attention(nc, g, layer, sorted_rows, hmax, hstats):
    O = g["O"][layer]
    GO = P // O
    GH = STRIPS // GO
    feats = g["feats"]
    first = layer * C
    with ExitStack() as ctx:
        def sb(name, shape, dt):
            return ctx.enter_context(nc.sbuf_tensor(f"{name}_{layer}", shape, dt))

        def ps(name, shape):
            return ctx.enter_context(nc.psum_tensor(f"{name}_{layer}", shape, F32))

        handles = []

        def sem(name):
            handles.append(ctx.enter_context(nc.semaphore(f"{name}_{layer}")))
            return handles[-1]

        w_lin = sb("w_lin", [64, 2 * C * METHODS], F32)
        w_conv = sb("w_conv", [O, 64], F32)
        b_lin = sb("b_lin", [64, 1], F32)
        w_convT = sb("w_convT", [64, O], F32)
        w_lin_near = sb("w_lin_near", [64, HEADS, METHODS, 8], F32)
        w_near = sb("w_near", [P, 2, O], F16)
        w_scaled = sb("w_scaled", [P, 2, O], F32)
        w_tops, w_top = sb("w_tops", [P, 2], F32), sb("w_top", [P, 1], F32)
        top = sb("top", [1, 1], F32)
        ones_row = sb("ones_row", [1, P], F32)
        w_power = sb("w_power", [P, 1], F32)
        w_scale, w_undo = sb("w_scale", [P, 1], F32), sb("w_undo", [P, 1], F32)
        w_centre = sb("w_centre", [C + 1, 2, O], F16)
        c_scaled = sb("c_scaled", [C + 1, 2, O], F32)
        point_sums = sb("point_sums", [P, SUB, TRI], F32)
        of_point = sb("of_point", [P, TRI], F32)
        first_windows = sb("first_windows", [P, B, BACK, WIN], F32)
        centre = sb("centre", [P, 2, SP_PTS * STRIPS + PTS], F32)
        centre_rows = sb("centre_rows", [C, N], F32)
        centre_in = sb("centre_in", [C + 1, N + PTS], F16)
        centre_out = sb("centre_out", [P, 2, GH, SP_PAD], F32)
        vectors = sb("vectors", [P, 2, STRIPS * PTS * PITCH], F16)
        by_head = sb("by_head", [P, 2, NBLK, HEADS, 32], F16)
        row_max = sb("row_max", [P, NBLK], F32)
        shifted = sb("shifted", [P, NBLK, WIN], F32)
        exps = sb("exps", [P, 2, NBLK, WIN], F32)
        probs = sb("probs", [P, 2, NBLK, 32], F32)
        row_sum = sb("row_sum", [P, NBLK], F32)
        row_inv = sb("row_inv", [P, NBLK], F32)
        point_inv = sb("point_inv", [P, 2, NBLK, TRI], F32)
        probsT = sb("probsT", [P, STRIPS, P], F32)
        mapped = sb("mapped", [P, 2, NBLK, O], F32)
        fused = sb("fused", [P, 2, GH, SP_PAD * WIN], F32)
        piece = sb("piece", [P, GH, 4, 6], F32)
        scores = [ps(f"scores{i}", [P, 512]) for i in range(2)]
        ps_mapped = ps("ps_mapped", [P, NBLK, O])
        ps_probsT = ps("ps_probsT", [P, STRIPS, P])
        outs = [ps(f"outs{i}", [P, 512]) for i in range(2)]
        misc = ps("misc", [P, 512])

        weights_in = sem("weights_in")
        centre_loaded = [sem("centre_loaded0"), sem("centre_loaded1")]
        raw_loaded, zeros_ready = sem("raw_loaded"), sem("zeros_ready")
        conv_turned, conv_ready, joined, split_step = sem("conv_turned"), sem("conv_ready"), sem("joined"), sem("split_step")
        top_ready, top_turned, top_spread = sem("top_ready"), sem("top_turned"), sem("top_spread")
        w_ready, near_ready, edge_ready = sem("w_ready"), sem("near_ready"), sem("edge_ready")
        vectors_ready, by_head_ready, other_heads_ready = (
            sem("vectors_ready"), sem("by_head_ready"), sem("other_heads_ready"))
        scores_ready, max_ready, shifted_ready = sem("scores_ready"), sem("max_ready"), sem("shifted_ready")
        exp_ready, sum_ready, row_inv_ready, inv_ready, probs_ready = (
            sem("exp_ready"), sem("sum_ready"), sem("row_inv_ready"), sem("inv_ready"), sem("probs_ready"))
        probs_turned, probsT_ready = sem("probs_turned"), sem("probsT_ready")
        mapped_done, mapped_ready = sem("mapped_done"), sem("mapped_ready")
        outs_ready, fused_ready, pieces_ready = sem("outs_ready"), sem("fused_ready"), sem("pieces_ready")
        batch_closed = sem("batch_closed")
        centre_in_ready, centre_done, centre_out_ready = (
            sem("centre_in_ready"), sem("centre_done"), sem("centre_out_ready"))
        ctx.callback(lambda: clear_semaphores(nc, handles))
        block = ctx.enter_context(nc.Block())

        def spread(copy, parity, h):
            at = slice(32 * h, 32 * h + 32)
            return copy(by_head[at, parity, :, h, 0:BLK].rearrange("p b (q j) -> p b q j", q=TRI),
                        vectors[at, parity, :].rearrange("p (b q j) -> p b q j", q=TRI, j=PITCH)[:, :, :, 0:WIN])

        BLOCKS = [(strip, sub) for strip in range(STRIPS) for sub in range(SUB)]

        def out_view(parity):
            return outs[parity][:, 0:GH * PTS * WIN].rearrange("p (g c) -> p g c", g=GH)

        def over_chunks(engine, chunk):
            with engine.Fori(0, B // 2) as pair:
                for half in range(2):
                    at = pair * (2 * CHUNKS) + half * CHUNKS
                    for k in (0, 1, 2):
                        chunk(pair, half, k, at + k, (half + k) % 2, True)
                    with engine.Fori(0, (CHUNKS - 5) // 2) as i:
                        for j in (3, 4):
                            chunk(pair, half, i * 2 + j, at + (i * 2 + j), (half + j) % 2, False)
                    for k in (CHUNKS - 2, CHUNKS - 1):
                        chunk(pair, half, k, at + k, (half + k) % 2, True)

        @block.sync
        def _(sp):
            sp.dma_start(w_lin[:], g["w_lin"][layer]).then_inc(weights_in, 16)
            sp.dma_start(w_conv[:], g["w_conv"][layer]).then_inc(weights_in, 16)
            sp.dma_start(b_lin[:], g["b_lin"][layer].rearrange("(k a) -> k a", a=1)).then_inc(weights_in, 16)

            def load_centres(b, half):
                for h in range(HEADS):
                    src = bass.AP(feats.tensor, feats.offset + b * (P * N) + (first + 8 * h) * N,
                                  [[0, METHODS], [N, 8], [1, N]])
                    sp.dma_start(centre[32 * h:32 * h + 32, half, 0:N], src).then_inc(centre_loaded[half], 16)

            def load_raw(b):
                sp.dma_start(centre_rows[:], bass.AP(feats.tensor, feats.offset + b * (P * N) + first * N,
                                                         [[N, C], [1, N]])).then_inc(raw_loaded, 16)

            load_centres(0, 0)
            load_raw(0)
            with sp.Fori(0, B // 2) as pair:
                for half in range(2):
                    b = pair * 2 + half
                    sp.wait_ge(vectors_ready, b * CHUNKS + 1)
                    load_centres((b + 1) % B, 1 - half)
                    sp.wait_ge(centre_in_ready, b + 1)
                    load_raw((b + 1) % B)
            sp.wait_ge(centre_loaded[0], 64 * (B // 2 + 1))
            sp.wait_ge(raw_loaded, 16 * (B + 1))

        @block.gpsimd
        def _(pool):
            gp = nc.gpsimd
            gp.memset(centre_in[:], 1.0)
            gp.memset(centre[:, :, N:], 0.0)
            gp.memset(vectors[:], 0.0)
            gp.memset(by_head[:], 0.0)
            gp.memset(fused[:, 1], 0.0)
            gp.memset(centre_out[:], 0.0)
            gp.memset(probs[:], 0.0).then_inc(zeros_ready, 1)
            gp.memset(fused[:, 0], 0.0).then_inc(probs_ready, 1)

            def normalise(pair, half, k, n, parity, peeled):
                pool.wait_ge(inv_ready, n + 1)
                gp.tensor_tensor(probs[:, parity, :, 0:BLK].rearrange("p b (q j) -> p b q j", q=TRI),
                                 exps[:, parity].unsqueeze(2).broadcast_to([P, NBLK, TRI, WIN]),
                                 point_inv[:, parity].unsqueeze(3).broadcast_to([P, NBLK, TRI, WIN]),
                                 ALU.mult).then_inc(probs_ready, 1)

            over_chunks(pool, normalise)

        @block.scalar
        def _(act):
            sc = nc.scalar
            act.wait_ge(conv_turned, 1)
            sc.activation(w_convT[:], misc[0:64, 0:O], ACT.Copy).then_inc(conv_ready, 1)

            def make_centre_in(pair_b):
                act.wait_ge(raw_loaded, pair_b * 16 + 16)
                sc.activation(centre_in[0:C, 0:N], centre_rows[:], ACT.Copy).then_inc(centre_in_ready, 1)

            def copy_centre_out(b, half):
                act.wait_ge(centre_done, b + 1)
                sc.activation(centre_out[:, half], misc[:, 0:GH * SP_PAD].rearrange("p (g c) -> p g c", g=GH),
                              ACT.Copy, scale=w_undo[:, 0:1]).then_inc(centre_out_ready, 1)

            def copy_mapped(count, parity):
                act.wait_ge(mapped_done, count)
                sc.activation(mapped[:, parity], ps_mapped[:], ACT.Copy, scale=w_undo[:, 0:1]).then_inc(mapped_ready, 1)

            def copy_probsT(count):
                act.wait_ge(probs_turned, count)
                sc.activation(probsT[:], ps_probsT[:], ACT.Copy).then_inc(probsT_ready, 1)

            def spread_heads(count, parity, batch_count=None):
                act.wait_ge(vectors_ready, count)
                if batch_count is not None:
                    act.wait_ge(edge_ready, batch_count)
                for h in range(VECTOR_HEADS, HEADS):
                    ins = spread(sc.copy, parity, h)
                ins.then_inc(other_heads_ready, 1)

            act.wait_ge(zeros_ready, 1)
            spread_heads(1, 0, 1)
            spread_heads(2, 1)
            make_centre_in(0)
            copy_centre_out(0, 0)
            copy_mapped(1, 1)

            def chunk(pair, half, k, n, parity, peeled):
                act.wait_ge(shifted_ready, n + 1)
                sc.activation(exps[:, parity], shifted[:], ACT.Exp, scale=1.0 / SQRT_HD).then_inc(exp_ready, 1)
                copy_probsT(n + 1)
                copy_mapped(n + 2, parity)
                spread_heads(n + 3, parity, pair * 2 + (half + 2) if peeled and k == CHUNKS - 2 else None)
                if peeled and k == 2:
                    make_centre_in(pair * 2 + (half + 1))
                if peeled and k == CHUNKS - 1:
                    copy_centre_out(pair * 2 + (half + 1), 1 - half)

            over_chunks(act, chunk)
            copy_probsT(B * CHUNKS + 1)

        @block.tensor
        def _(pe):
            mm = nc.tensor.matmul
            pe.wait_ge(weights_in, 48)
            nc.tensor.transpose(misc[0:64, 0:O], w_conv[:], g["ident"][0:O, 0:O]).then_inc(conv_turned, 1)
            pe.wait_ge(conv_ready, 1)
            pe.wait_ge(near_ready, 1)
            mm(misc[:, 64:64 + O], w_lin_near[:].rearrange("k h m f -> k (h m f)"), w_convT[:],
               start=True, stop=True)
            for place in range(METHODS):
                mm(misc[0:C, 128:128 + O], w_lin[:, place:C * METHODS:METHODS], w_convT[:],
                   start=(place == 0), stop=(place == METHODS - 1))
            mm(misc[C:C + 1, 128:128 + O], b_lin[:], w_convT[:], start=True, stop=True).then_inc(joined, 1)

            def make_centre_out():
                for gh in range(GH):
                    for part in range(2):
                        for go in range(GO):
                            at = (gh * GO + go) * SP_PTS
                            ins = mm(misc[go * O:(go + 1) * O, gh * SP_PAD:(gh + 1) * SP_PAD],
                                     w_centre[:, part, :], centre_in[:, at:at + SP_PAD], start=(part == 0),
                                     stop=(part == 1), skip_group_check=True)
                ins.then_inc(centre_done, 1)

            def keep_clock(parity, times):
                for _ in range(times):
                    mm(scores[parity][:], by_head[:, parity, 0, :, :].rearrange("p h c -> p (h c)"),
                       by_head[:, parity, 0:4, :, :].rearrange("p b h c -> p (b h c)"), start=True, stop=True,
                       skip_group_check=True)

            def make_scores(parity):
                for strip in range(STRIPS):
                    for point in range(TRI):
                        for sub in range(SUB):
                            block_ = strip * SUB + sub
                            at = block_ * TRI * PITCH + point * 32
                            out = scores[parity][32 * sub:32 * sub + 32, strip * HEADS * WIN:(strip + 1) * HEADS * WIN]
                            ins = mm(out.rearrange("p (h j) -> p h j", h=HEADS), vectors[:, parity, at:at + 32],
                                     by_head[:, parity, block_, :, point * WIN:(point + 1) * WIN],
                                     start=(point == 0), stop=(point == TRI - 1), skip_group_check=True)
                ins.then_inc(scores_ready, 1)

            def map_vectors(parity):
                for block_ in range(NBLK):
                    for part in range(2):
                        ins = mm(ps_mapped[:, block_, :],
                                 by_head[:, parity, block_, :, :].rearrange("p h c -> p (h c)"),
                                 w_near[:, part, :], start=(part == 0), stop=(part == 1))
                ins.then_inc(mapped_done, 1)

            pe.wait_ge(top_ready, 1)
            nc.tensor.transpose(misc[0:1, 256:256 + P], w_top[:], g["ident"][:])\
                .then_inc(top_turned, 1)
            pe.wait_ge(top_ready, 2)
            mm(misc[:, 384:385], ones_row[:], top[:], start=True, stop=True).then_inc(top_spread, 1)
            pe.wait_ge(w_ready, 1)
            pe.wait_ge(centre_in_ready, 1)
            make_centre_out()
            zeros = probs[:, 0].rearrange("p b c -> p (b c)")
            mm(outs[0][:, 0:COLS], zeros[:, 0:P], zeros[:, 0:COLS], start=True, stop=True).then_inc(outs_ready, 1)
            for q in range(O * NBLK // 256):
                ins = mm(ps_mapped[:].rearrange("p b o -> p (b o)")[:, q * 256:(q + 1) * 256], zeros[:, 0:P],
                         zeros[:, 0:256], start=True, stop=True)
            ins.then_inc(mapped_done, 1)
            pe.wait_ge(by_head_ready, 1)
            pe.wait_ge(other_heads_ready, 1)
            keep_clock(0, WARM_FIRST)
            make_scores(0)

            def turn_probs(count, parity):
                pe.wait_ge(probs_ready, count)
                for strip in range(STRIPS):
                    ins = nc.tensor.transpose(
                        ps_probsT[:, strip, :],
                        probs[:, parity, strip * HEADS:(strip + 1) * HEADS, :].rearrange("p h c -> p (h c)"),
                        g["ident"][:])
                ins.then_inc(probs_turned, 1)

            def weigh(count, parity):
                pe.wait_ge(probsT_ready, count)
                for block_, (strip, sub) in sorted(enumerate(BLOCKS), key=lambda b: (b[1][1], b[1][0])):
                    go, gh = strip % GO, strip // GO
                    ins = mm(out_view(parity)[go * O:(go + 1) * O, gh, sub * BLK:(sub + 1) * BLK],
                             mapped[:, parity, block_, :], probsT[:, strip, 32 * sub:32 * sub + BLK],
                             start=True, stop=True)
                ins.then_inc(outs_ready, 1)

            def chunk(pair, half, k, n, parity, peeled):
                pe.wait_ge(mapped_ready, n + 1)
                map_vectors(parity)
                if peeled and k == CHUNKS - 1:
                    pe.wait_ge(centre_in_ready, pair * 2 + (half + 2))
                    pe.wait_ge(centre_out_ready, pair * 2 + (half + 1))
                turn_probs(n + 1, 1 - parity)
                pe.wait_ge(by_head_ready, n + 2)
                pe.wait_ge(other_heads_ready, n + 2)
                keep_clock(1 - parity, WARM_EDGE if peeled else WARM_EACH[layer])
                make_scores(1 - parity)
                weigh(n + 1, 1 - parity)
                if peeled and k == CHUNKS - 1:
                    make_centre_out()

            over_chunks(pe, chunk)
            turn_probs(B * CHUNKS + 1, 1)
            pe.wait_ge(mapped_ready, B * CHUNKS + 1)
            pe.wait_ge(fused_ready, B * CHUNKS)
            weigh(B * CHUNKS + 1, 1)

        @block.vector
        def _(dve):
            vec = nc.vector
            chain = Step(dve, split_step)
            link = chain.then_wait
            dve.wait_ge(weights_in, 48)
            vec.tensor_copy(w_lin_near[:], w_lin[:, C * METHODS:].rearrange("k (h f m) -> k h m f", h=HEADS,
                                                                            m=METHODS)).then_inc(near_ready, 1)
            link(vec.tensor_copy(first_windows[:], bass.AP(sorted_rows.tensor, sorted_rows.offset + BACK,
                                                           [sorted_rows.ap[0], [SW, B], [0, BACK], [1, WIN]])))
            for i in range(BACK - 1):
                n_last = WIN - (i + BACK + 1)
                ins = vec.tensor_copy(first_windows[:, :, i, i + BACK + 1:WIN],
                                      sorted_rows[:, :, 2 * BACK + i:2 * BACK + i + 1].broadcast_to([P, B, n_last]))
            link(ins)
            dve.wait_ge(joined, 1)
            near_map = misc[:, 64:64 + O]
            centre_map = misc[0:C + 1, 128:128 + O]
            w_abs = exps[:].rearrange("p t b j -> p t (b j)")[:, :, 0:O]
            vec.memset(ones_row[:], 1.0)
            vec.memset(w_abs, 0.0)
            vec.tensor_scalar(c_scaled[:, 1], centre_map, -1.0, None, ALU.mult)
            link(vec.tensor_scalar(w_scaled[:, 1], near_map, -1.0, None, ALU.mult))
            vec.tensor_tensor(w_abs[:, 0], near_map, w_scaled[:, 1], ALU.max)
            link(vec.tensor_tensor(w_abs[0:C + 1, 1], centre_map, c_scaled[:, 1], ALU.max))
            link(vec.tensor_reduce(w_tops[:], w_abs, AX_X, ALU.max))
            vec.tensor_tensor(w_top[:], w_tops[:, 0:1], w_tops[:, 1:2], ALU.max).then_inc(top_ready, 1)
            dve.wait_ge(top_turned, 1)
            vec.tensor_reduce(top[:], misc[0:1, 256:256 + P], AX_X, ALU.max).then_inc(top_ready, 1)
            link(vec.tensor_reduce(point_sums[:], g["ident"][:].rearrange("p (s c) -> p s c", s=SUB)[:, :, 0:BLK]
                                   .rearrange("p s (q j) -> p s q j", q=TRI), AX_X, ALU.add))
            vec.tensor_reduce(of_point[:], point_sums[:].rearrange("p s q -> p q s"), AX_X, ALU.add)
            dve.wait_ge(top_spread, 1)
            link(vec.tensor_scalar(w_power[:], misc[:, 384:385], 1e-30, None, ALU.max))
            link(vec.tensor_scalar(w_scale[:].bitcast(I32), w_power[:].bitcast(I32), 0x7F800000, None,
                                   ALU.bitwise_and))
            link(vec.tensor_scalar(w_undo[:], w_scale[:], 2.0 ** -12, None, ALU.mult))
            link(vec.reciprocal(w_scale[:], w_undo[:]))
            link(vec.tensor_scalar(w_scaled[:, 0], near_map, w_scale[:, 0:1], None, ALU.mult))
            link(vec.tensor_copy(w_near[:, 0], w_scaled[:, 0]))
            link(vec.tensor_tensor(w_scaled[:, 1], w_scaled[:, 0], w_near[:, 0], ALU.subtract))
            vec.tensor_copy(w_near[:, 1], w_scaled[:, 1])
            link(vec.tensor_scalar(c_scaled[:, 0], centre_map, w_scale[0:C + 1, 0:1], None, ALU.mult))
            link(vec.tensor_copy(w_centre[:, 0], c_scaled[:, 0]))
            link(vec.tensor_tensor(c_scaled[:, 1], c_scaled[:, 0], w_centre[:, 0], ALU.subtract))
            vec.tensor_copy(w_centre[:, 1], c_scaled[:, 1]).then_inc(w_ready, 1)

            def make_vectors(b, half, k, count, parity, batch_count=None):
                rows = bass.AP(sorted_rows.tensor, sorted_rows.offset + b * SW + k * PTS,
                               [sorted_rows.ap[0], [SP_PTS, STRIPS], [1, PTS], [1, WIN]])
                row = centre[:, half, 0:1]
                mids = bass.AP(row.tensor, row.offset + k * PTS,
                               [row.ap[0], [SP_PTS, STRIPS], [1, PTS], [0, WIN]])
                vec.tensor_tensor(vectors[:, parity, :].rearrange("p (s c j) -> p s c j", s=STRIPS, c=PTS)
                                  [:, :, :, 0:WIN], rows, mids, ALU.subtract).then_inc(vectors_ready, 1)
                dve.wait_ge(vectors_ready, count)
                if batch_count is not None:
                    whole = first_windows[:]
                    starts = bass.AP(whole.tensor, whole.offset + b * (BACK * WIN),
                                     [whole.ap[0], [WIN, BACK], [1, WIN]])
                    vec.tensor_tensor(vectors[:, parity, 0:BACK * PITCH].rearrange("p (i j) -> p i j", i=BACK)
                                      [:, :, 0:WIN], starts,
                                      centre[:, half, 0:BACK].unsqueeze(2).broadcast_to([P, BACK, WIN]),
                                      ALU.subtract).then_inc(edge_ready, 1)
                    dve.wait_ge(edge_ready, batch_count)
                for h in range(VECTOR_HEADS):
                    ins = spread(vec.tensor_copy, parity, h)
                ins.then_inc(by_head_ready, 1)

            def fuse(parity, k, count, half):
                dve.wait_ge(outs_ready, count)
                row = centre_out[:, half, 0:1, 0:1]
                mids = bass.AP(row.tensor, row.offset + k * PTS, [row.ap[0], [SP_PAD, GH], [1, PTS], [0, WIN]])
                row = fused[:, half, 0:1, 0:1]
                dst = bass.AP(row.tensor, row.offset + k * (PTS * WIN),
                              [row.ap[0], [SP_PAD * WIN, GH], [WIN, PTS], [1, WIN]])
                vec.tensor_tensor(dst, out_view(parity).rearrange("p g (c j) -> p g c j", c=PTS), mids,
                                  ALU.add).then_inc(fused_ready, 1)

            def close_quarter(q, b, half, fused_count, batch_count=None):
                points = slice(q * SP_PTS // 4, (q + 1) * SP_PTS // 4)
                columns = slice(points.start * WIN, points.stop * WIN)
                dve.wait_ge(fused_ready, fused_count)
                for gh in range(GH):
                    ins = vec.bn_stats(piece[:, gh, q, :], fused[:, half, gh, columns])
                if batch_count is not None:
                    ins.then_inc(pieces_ready, 1)
                vec.tensor_reduce(hmax[:, b, :, points], fused[:, half, :, columns]
                                  .rearrange("p g (c j) -> p g c j", j=WIN), AX_X, ALU.max)
                if batch_count is not None:
                    dve.wait_ge(pieces_ready, batch_count)
                    vec.tensor_scalar(hstats[:, b], piece[:].rearrange("p g q s -> p (g q s)"), 1.0, None,
                                      ALU.mult).then_inc(batch_closed, 1)

            vec.memset(piece[:], 0.0)
            dve.wait_ge(zeros_ready, 1)
            dve.wait_ge(centre_loaded[0], 64)
            make_vectors(0, 0, 0, 1, 0, 1)
            make_vectors(0, 0, 1, 2, 1)

            def chunk(pair, half, k, n, parity, peeled):
                b = pair * 2 + half
                if peeled and k == 1:
                    dve.wait_ge(centre_out_ready, b + 1)
                dve.wait_ge(scores_ready, n + 1)
                view = scores[parity][:, 0:NBLK * WIN].rearrange("p (b c) -> p b c", b=NBLK)
                vec.tensor_reduce(row_max[:], view, AX_X, ALU.max).then_inc(max_ready, 1)
                dve.wait_ge(max_ready, n + 1)
                vec.tensor_tensor(shifted[:], view, row_max[:].unsqueeze(2).broadcast_to([P, NBLK, WIN]),
                                  ALU.subtract).then_inc(shifted_ready, 1)
                dve.wait_ge(mapped_done, n + 2)
                if peeled and k >= CHUNKS - 2:
                    ahead = k + 2 - CHUNKS
                    if ahead == 0:
                        dve.wait_ge(centre_loaded[1 - half], pair * 64 + 64 * (1 + half))
                    make_vectors((b + 1) % B, 1 - half, ahead, n + 3, parity, b + 2 if ahead == 0 else None)
                else:
                    make_vectors(b, half, k + 2, n + 3, parity)
                dve.wait_ge(exp_ready, n + 1)
                vec.tensor_reduce(row_sum[:], exps[:, parity], AX_X, ALU.add).then_inc(sum_ready, 1)
                dve.wait_ge(sum_ready, n + 1)
                vec.reciprocal(row_inv[:], row_sum[:]).then_inc(row_inv_ready, 1)
                dve.wait_ge(row_inv_ready, n + 1)
                vec.tensor_tensor(point_inv[:, parity], row_inv[:].unsqueeze(2).broadcast_to([P, NBLK, TRI]),
                                  of_point[:].unsqueeze(1).broadcast_to([P, NBLK, TRI]), ALU.mult)\
                    .then_inc(inv_ready, 1)
                if peeled and k < 2:
                    fuse(parity, CHUNKS - 2 + k, n + 1, 1 - half)
                else:
                    fuse(parity, k - 2, n + 1, half)
                if peeled and k >= CHUNKS - 2:
                    close_quarter(k + 2 - CHUNKS, b, half, n)
                if peeled and k in (0, 2):
                    before = (b + B - 1) % B
                    if k == 0:
                        close_quarter(2, before, 1 - half, n + 1)
                    else:
                        close_quarter(3, before, 1 - half, n, b + 1)

            over_chunks(dve, chunk)
            for back in (2, 1):
                fuse(back % 2, CHUNKS - back, B * CHUNKS + 3 - back, 1)
            close_quarter(2, B - 1, 1, B * CHUNKS + 1)
            close_quarter(3, B - 1, 1, B * CHUNKS + 2, B + 1)


def close_layer(nc, g, layer, hmax, hstats):
    O = g["O"][layer]
    GO = P // O
    GH = STRIPS // GO
    dst = C if layer == 0 else 2 * C
    with ExitStack() as ctx:
        def sb(name, shape):
            return ctx.enter_context(nc.sbuf_tensor(f"{name}_{layer}", shape, F32))

        handles = []

        def sem(name):
            handles.append(ctx.enter_context(nc.semaphore(f"{name}_{layer}")))
            return handles[-1]

        strip_stats = sb("strip_stats", [P, B, GH, 2])
        mean = sb("mean", [P, B])
        away = sb("away", [P, B, GH])
        var = sb("var", [P, B])
        rstd = sb("norm_rstd", [P, B])
        work = sb("norm_work", [P, 3, B])
        relu = sb("relu", [P, B, GH, SP_PTS])
        sums = ctx.enter_context(nc.psum_tensor(f"sums_{layer}", [P, 2, 512], F32))
        step, aggregated, mean_done, spread_ready, var_done = (
            sem("close_step"), sem("aggregated"), sem("mean_done"), sem("spread_ready"), sem("var_done"))
        eps_ready, std_ready, relu_ready, stored = sem("eps_ready"), sem("std"), sem("relu_ready"), sem("feats_stored")
        newton = Newton(nc, [work[:, i, :] for i in range(3)], std_ready)
        ctx.callback(lambda: clear_semaphores(nc, handles))
        block = ctx.enter_context(nc.Block())

        @block.tensor
        def _(pe):
            pe.wait_ge(aggregated, 1)
            for gh in range(GH):
                ins = nc.tensor.matmul(sums[:, 0, 0:B], g["average"][layer][:], strip_stats[:, :, gh, 0],
                                       start=(gh == 0), stop=(gh == GH - 1))
            ins.then_inc(mean_done, 1)
            pe.wait_ge(spread_ready, 1)
            for gh in range(GH):
                ins = nc.tensor.matmul(sums[:, 1, 0:B], g["average"][layer][:], strip_stats[:, :, gh, 1],
                                       start=(gh == 0), stop=(gh == GH - 1))
            ins.then_inc(var_done, 1)

        @block.scalar
        def _(act):
            newton.on_scalar(act, eps_ready, 1, 1)

        @block.vector
        def _(dve):
            vec = nc.vector
            chain = Step(dve, step)
            link = chain.then_wait
            for b in range(B):
                for gh in range(GH):
                    ins = vec.bn_aggr(strip_stats[:, b, gh, :], hstats[:, b, gh * 24:(gh + 1) * 24])
            ins.then_inc(aggregated, 1)
            dve.wait_ge(mean_done, 1)
            link(vec.tensor_copy(mean[:], sums[:, 0, 0:B]))
            link(vec.tensor_tensor(away[:], strip_stats[:, :, :, 0], mean[:].unsqueeze(2).broadcast_to([P, B, GH]),
                                   ALU.subtract))
            link(vec.tensor_tensor(away[:], away[:], away[:], ALU.mult))
            vec.tensor_tensor(strip_stats[:, :, :, 1], strip_stats[:, :, :, 1], away[:], ALU.add)\
                .then_inc(spread_ready, 1)
            dve.wait_ge(var_done, 1)
            link(vec.tensor_copy(var[:], sums[:, 1, 0:B]))
            newton.on_vector(dve, link, var[:], rstd[:], eps_ready, 1)
            for b in range(B):
                ins = vec.tensor_scalar(hmax[:, b], hmax[:, b], mean[:, b:b + 1], rstd[:, b:b + 1],
                                        ALU.subtract, ALU.mult)
            link(ins)
            flat = "p b g n -> p (b g n)"
            vec.scalar_tensor_tensor(relu[:].rearrange(flat), hmax.rearrange(flat), 0.2, hmax.rearrange(flat),
                                     ALU.mult, ALU.max).then_inc(relu_ready, 1)

        @block.sync
        def _(sp):
            sp.wait_ge(relu_ready, 1)
            for strip in range(STRIPS):
                go, gh = strip % GO, strip // GO
                sp.dma_start(g["feats"][:, dst:dst + O, strip * SP_PTS:(strip + 1) * SP_PTS]
                             .rearrange("b o n -> o b n"), relu[go * O:(go + 1) * O, :, gh, :]).then_inc(stored, 16)
            sp.wait_ge(stored, 16 * STRIPS)


def mix_features(nc, g, x1, query):
    with ExitStack() as ctx:
        def sb(name, shape):
            return ctx.enter_context(nc.sbuf_tensor(name, shape, F32))

        handles = []

        def sem(name):
            handles.append(ctx.enter_context(nc.semaphore(name)))
            return handles[-1]

        mixed = sb("mixed", [P, B, N])
        w_mix = sb("w_mix", [C, P])
        w_mixT = sb("w_mixT", [P, C])
        x_rows = sb("x_rows", [P, RT, N])
        stats = sb("mix_stats", [P, RT, 6])
        mean_var = sb("mix_mean_var", [P, RT, 2])
        rstd = sb("mix_rstd", [P, RT])
        work = sb("mix_work", [P, 3, RT])
        fused = sb("mix_fused", [P, RT, N])
        normed = sb("mix_normed", [P, RT, N])
        products = ctx.enter_context(nc.psum_tensor("mix_products", [P, RT, N], F32))
        turned = ctx.enter_context(nc.psum_tensor("mix_turned", [P, 512], F32))
        w_in, x_in = sem("w_in"), sem("x_in")
        mixed_in = [sem(f"mixed_in{t}") for t in range(RT)]
        w_turned, w_ready, products_ready = sem("w_turned"), sem("mix_w_ready"), sem("mix_products_ready")
        step, eps_ready, std_ready, normed_ready, stored = (
            sem("mix_step"), sem("mix_eps"), sem("mix_std"), sem("mix_normed_ready"), sem("query_stored"))
        newton = Newton(nc, [work[:, i, :] for i in range(3)], std_ready)
        ctx.callback(lambda: clear_semaphores(nc, handles))
        block = ctx.enter_context(nc.Block())

        @block.sync
        def _(sp):
            sp.dma_start(w_mix[:], g["w_mix"]).then_inc(w_in, 16)
            for t in range(RT):
                sp.dma_start(mixed[:, t * BPT:(t + 1) * BPT, :],
                             g["feats"][t * BPT:(t + 1) * BPT].rearrange("b f n -> f b n")).then_inc(mixed_in[t], 16)
            sp.dma_start(x_rows[:], g["x"].rearrange("(t q) c n -> (q c) t n", q=BPT)).then_inc(x_in, 16)
            sp.wait_ge(normed_ready, 1)
            for q in range(BPT):
                sp.dma_start(query.rearrange("(t q) c n -> q c t n", q=BPT)[q], normed[q * C:(q + 1) * C])\
                    .then_inc(stored, 16)
            sp.wait_ge(stored, 16 * BPT)

        @block.tensor
        def _(pe):
            pe.wait_ge(w_in, 16)
            nc.tensor.transpose(turned[:, 0:C], w_mix[:], g["ident"][0:C, 0:C]).then_inc(w_turned, 1)
            pe.wait_ge(w_ready, 1)
            for t in range(RT):
                pe.wait_ge(mixed_in[t], 16)
                for q in range(BPT):
                    ins = nc.tensor.matmul(products[q * C:(q + 1) * C, t, :], w_mixT[:], mixed[:, t * BPT + q, :],
                                           start=True, stop=True)
                ins.then_inc(products_ready, 1)

        @block.scalar
        def _(act):
            act.wait_ge(w_turned, 1)
            nc.scalar.activation(w_mixT[:], turned[:, 0:C], ACT.Copy).then_inc(w_ready, 1)
            newton.on_scalar(act, eps_ready, 1, 1)
            newton.on_scalar(act, eps_ready, 2, 2)

        @block.vector
        def _(dve):
            vec = nc.vector
            chain = Step(dve, step)
            link = chain.then_wait

            def row_stats(tiles):
                for t in range(RT):
                    if tiles is products:
                        dve.wait_ge(products_ready, t + 1)
                    ins = vec.bn_stats(stats[:, t, :], tiles[:, t, :])
                link(ins)
                for t in range(RT):
                    ins = vec.bn_aggr(mean_var[:, t, :], stats[:, t, :])
                link(ins)

            row_stats(products)
            newton.on_vector(dve, link, mean_var[:, :, 1], rstd[:], eps_ready, 1)
            for t in range(RT):
                ins = vec.tensor_scalar(fused[:, t, :], products[:, t, :], mean_var[:, t, 0:1], rstd[:, t:t + 1],
                                        ALU.subtract, ALU.mult)
            link(ins)
            dve.wait_ge(x_in, 16)
            flat = "p t n -> p (t n)"
            link(vec.scalar_tensor_tensor(fused[:].rearrange(flat), fused[:].rearrange(flat), 0.2,
                                          fused[:].rearrange(flat), ALU.mult, ALU.max))
            link(vec.tensor_tensor(x1[:], x_rows[:], fused[:], ALU.add))
            row_stats(x1)
            newton.on_vector(dve, link, mean_var[:, :, 1], rstd[:], eps_ready, 2)
            for t in range(RT):
                ins = vec.tensor_scalar(normed[:, t, :], x1[:, t, :], mean_var[:, t, 0:1], rstd[:, t:t + 1],
                                        ALU.subtract, ALU.mult)
            ins.then_inc(normed_ready, 1)


def batch_attention(nc, g, query, message):
    QL = N // 4
    STEPS, SPAN = 4, QL // 4
    ITS, GROUPS, PAIR = SPAN // 8, 4, 2
    with ExitStack() as ctx:
        def sb(name, shape):
            return ctx.enter_context(nc.sbuf_tensor(name, shape, F32))

        handles = []

        def sem(name):
            handles.append(ctx.enter_context(nc.semaphore(name)))
            return handles[-1]

        queries = sb("queries", [P, B, QL])
        stage = sb("stage", [P, 2, SPAN, B])
        values = sb("values", [P, 2, ITS, P])
        row_max = sb("b_row_max", [P, 4 * ITS])
        logits = sb("logits", [P, 4, ITS, 32])
        row_sum = sb("b_row_sum", [P, 4 * ITS])
        attn = sb("attn", [P, 4, ITS, 32])
        attnT = sb("attnT", [P, 4, ITS, 32])
        said = sb("said", [P, B, QL])
        banks = ctx.enter_context(nc.psum_tensor("attn_banks", [P, 4, 512], F32))
        turned = ctx.enter_context(nc.psum_tensor("attn_turned", [P, ITS, P], F32))
        queries_in, stage_ready, mask_ready = sem("queries_in"), sem("stage_ready"), sem("apart_ready")
        scored, turned_ready, values_ready = sem("scored"), sem("values_turned"), sem("values_ready")
        logits_ready, exp_ready, attnT_ready, weighed, said_ready, stored = (
            sem("logits_ready"), sem("b_exp_ready"), sem("attnT_ready"), sem("weighed"), sem("said_ready"),
            sem("message_stored"))
        chained, scores_read = sem("softmax_step"), sem("scores_read")
        ctx.callback(lambda: clear_semaphores(nc, handles))
        block = ctx.enter_context(nc.Block())

        @block.sync
        def _(sp):
            for quarter in range(4):
                sp.dma_start(queries[quarter * C:(quarter + 1) * C, :, :],
                             query[:, :, quarter * QL:(quarter + 1) * QL].rearrange("b c l -> c b l"))\
                    .then_inc(queries_in, 16)
            sp.wait_ge(said_ready, STEPS * GROUPS)
            for quarter in range(4):
                sp.dma_start(message[:, :, quarter * QL:(quarter + 1) * QL].rearrange("b c l -> c b l"),
                             said[quarter * C:(quarter + 1) * C, :, :]).then_inc(stored, 16)
            sp.wait_ge(stored, 64)

        @block.tensor
        def _(pe):
            def score(i):
                if i:
                    pe.wait_ge(values_ready, i)
                pe.wait_ge(stage_ready, i + 1)
                for run in range(ITS):
                    ins = nc.tensor.transpose(turned[:, run, :], stage[:, i % 2, run * 8:(run + 1) * 8, :]
                                              .rearrange("p l b -> p (l b)"), g["ident"][:])
                ins.then_inc(turned_ready, 1)
                if i:
                    pe.wait_ge(scores_read, i)
                for run in range(ITS):
                    for quarter in range(4):
                        for group in range(GROUPS):
                            at = run * 8 + group * PAIR
                            pair = stage[32 * quarter:32 * quarter + 32, i % 2, at:at + PAIR, :]\
                                .rearrange("p l b -> p (l b)")
                            ins = nc.tensor.matmul(
                                banks[32 * group:32 * group + 32, quarter, run * 32:run * 32 + 32], pair, pair,
                                start=True, stop=True)
                ins.then_inc(scored, 1)

            def weigh(i):
                pe.wait_ge(values_ready, i + 1)
                pe.wait_ge(attnT_ready, i + 1)
                for run in range(ITS):
                    for quarter in range(4):
                        for group in range(GROUPS):
                            rows = slice(32 * group, 32 * group + 32)
                            ins = nc.tensor.matmul(
                                banks[32 * quarter:32 * quarter + 32, group, 256 + run * 32:256 + run * 32 + 32],
                                values[rows, i % 2, run, 32 * quarter:32 * quarter + 32],
                                attnT[rows, quarter, run, :], start=True, stop=True)
                ins.then_inc(weighed, 1)

            score(0)
            for i in range(STEPS):
                if i + 1 < STEPS:
                    score(i + 1)
                weigh(i)

        @block.scalar
        def _(act):
            def copy_values(i):
                act.wait_ge(turned_ready, i + 1)
                nc.scalar.activation(values[:, i % 2], turned[:], ACT.Copy).then_inc(values_ready, 1)

            copy_values(0)
            for i in range(STEPS):
                act.wait_ge(logits_ready, i + 1)
                nc.scalar.activation(attn[:], logits[:], ACT.Exp).then_inc(exp_ready, 1)
                if i + 1 < STEPS:
                    copy_values(i + 1)

        @block.vector
        def _(dve):
            vec = nc.vector
            dve.wait_ge(queries_in, 64)
            whole = queries[:]
            chain = Step(dve, chained)
            link = chain.then_wait
            flat = "p q r c -> p (q r) c"

            def make_stage(i):
                vec.tensor_copy(stage[:, i % 2], bass.AP(whole.tensor, whole.offset + i * SPAN,
                                                         [whole.ap[0], [1, SPAN], [QL, B]])).then_inc(stage_ready, 1)

            def read_scores(i):
                dve.wait_ge(scored, i + 1)
                vec.scalar_tensor_tensor(logits[:].rearrange("p q r c -> p q (r c)"), banks[:, :, 0:ITS * 32],
                                         1.0 / SQRT_HD, g["apart"][:].unsqueeze(1).broadcast_to([P, 4, ITS * 32]),
                                         ALU.mult, ALU.add).then_inc(scores_read, 1)
                dve.wait_ge(scores_read, i + 1)

            make_stage(0)
            make_stage(1)
            for i in range(STEPS):
                read_scores(i)
                link(vec.tensor_reduce(row_max[:], logits[:].rearrange(flat), AX_X, ALU.max))
                vec.tensor_tensor(logits[:].rearrange(flat), logits[:].rearrange(flat),
                                  row_max[:].unsqueeze(2).broadcast_to([P, 4 * ITS, 32]), ALU.subtract)\
                    .then_inc(logits_ready, 1)
                dve.wait_ge(exp_ready, i + 1)
                link(vec.tensor_reduce(row_sum[:], attn[:].rearrange(flat), AX_X, ALU.add))
                link(vec.reciprocal(row_sum[:], row_sum[:]))
                link(vec.tensor_tensor(attn[:].rearrange(flat), attn[:].rearrange(flat),
                                       row_sum[:].unsqueeze(2).broadcast_to([P, 4 * ITS, 32]), ALU.mult))
                vec.transpose(attnT[:].rearrange("p q r c -> p (q r c)"), attn[:].rearrange("p q r c -> p (q r c)"))\
                    .then_inc(attnT_ready, 1)
                dve.wait_ge(weighed, i + 1)
                if i + 2 < STEPS:
                    make_stage(i + 2)
                for group in range(GROUPS):
                    there, here = (bass.AP(tile.tensor, tile.offset + (i * SPAN + group * PAIR),
                                           [tile.ap[0], [8, ITS], [1, PAIR], [QL, B]]) for tile in (said[:], whole))
                    vec.tensor_tensor(there, banks[:, group, 256:256 + ITS * 32]
                                      .rearrange("p (r l b) -> p r l b", r=ITS, l=PAIR), here, ALU.add)\
                        .then_inc(said_ready, 1)


def feed_forward(nc, g, x1, message, out):
    HC, FC = H // P, FF // P
    with ExitStack() as ctx:
        def sb(name, shape):
            return ctx.enter_context(nc.sbuf_tensor(name, shape, F32))

        handles = []

        def sem(name):
            handles.append(ctx.enter_context(nc.semaphore(name)))
            return handles[-1]

        x2 = sb("x2", [P, RT, N])
        stats = sb("ff_stats", [P, RT, 6])
        mean_var = sb("ff_mean_var", [P, RT, 2])
        rstd = sb("ff_rstd", [P, RT])
        work = sb("ff_work", [P, 3, RT])
        normed = sb("ff_normed", [P, RT, H])
        normedT = sb("normedT", [P, HC, RT * P])
        sig = sb("sig", [P, 2, RT * P])
        silu = sb("silu", [P, 2, RT * P])
        hidden = sb("hidden", [P, FC, RT * P])
        result = sb("result", [P, RT, H])
        banks = ctx.enter_context(nc.psum_tensor("ff_banks", [P, 8, 512], F32))
        said_in, step, eps_ready, std_ready = sem("said_in"), sem("ff_step"), sem("ff_eps"), sem("ff_std")
        normed_ready, turned_ready, normedT_ready = sem("ff_normed_ready"), sem("ff_turned"), sem("normedT_ready")
        gated, sig_ready, silu_ready, hidden_ready = sem("gated"), sem("sig_ready"), sem("silu_ready"), sem("hidden_ready")
        down_done, result_ready, out_stored = sem("down_done"), sem("result_ready"), sem("out_stored")
        newton = Newton(nc, [work[:, i, :] for i in range(3)], std_ready)
        block = ctx.enter_context(nc.Block())

        @block.sync
        def _(sp):
            for q in range(BPT):
                sp.dma_start(x2[q * C:(q + 1) * C], message.rearrange("(t q) c n -> q c t n", q=BPT)[q])\
                    .then_inc(said_in, 16)
            for t in range(RT):
                sp.wait_ge(result_ready, t + 1)
                for q in range(BPT):
                    sp.dma_start(out[t * BPT + q], result[q * C:(q + 1) * C, t, :]).then_inc(out_stored, 16)
            sp.wait_ge(out_stored, 16 * B)

        @block.tensor
        def _(pe):
            for t in range(RT):
                pe.wait_ge(normed_ready, t + 1)
                for c in range(HC):
                    ins = nc.tensor.transpose(banks[:, t, c * P:(c + 1) * P], normed[:, t, c * P:(c + 1) * P],
                                              g["ident"][:])
                ins.then_inc(turned_ready, 1)
            pe.wait_ge(normedT_ready, RT)
            for f in range(FC):
                if f >= 2:
                    pe.wait_ge(hidden_ready, f - 1)
                for bank, w in ((4 + f % 2, g["gateT"]), (6 + f % 2, g["upT"])):
                    for c in range(HC):
                        ins = nc.tensor.matmul(banks[:, bank, :], w[:, c, f * P:(f + 1) * P], normedT[:, c, :],
                                               start=(c == 0), stop=(c == HC - 1))
                ins.then_inc(gated, 1)
            for t in range(RT):
                for f in range(FC):
                    if t == 0:
                        pe.wait_ge(hidden_ready, f + 1)
                    ins = nc.tensor.matmul(banks[:, t, :], hidden[:, f, t * P:(t + 1) * P], g["downT"][:, f, :],
                                           start=(f == 0), stop=(f == FC - 1))
                ins.then_inc(down_done, 1)

        @block.scalar
        def _(act):
            newton.on_scalar(act, eps_ready, 1, 1)
            for t in range(RT):
                act.wait_ge(turned_ready, t + 1)
                nc.scalar.activation(normedT[:, :, t * P:(t + 1) * P],
                                     banks[:, t, :].rearrange("p (c k) -> p c k", c=HC), ACT.Copy)\
                    .then_inc(normedT_ready, 1)
            for f in range(FC):
                act.wait_ge(gated, f + 1)
                if f >= 2:
                    act.wait_ge(silu_ready, f - 1)
                nc.scalar.activation(sig[:, f % 2], banks[:, 4 + f % 2, :], ACT.Sigmoid).then_inc(sig_ready, 1)

        @block.vector
        def _(dve):
            vec = nc.vector
            chain = Step(dve, step)
            link = chain.then_wait
            dve.wait_ge(said_in, 16 * BPT)
            link(vec.tensor_tensor(x2[:], x2[:], x1[:], ALU.add))
            for t in range(RT):
                ins = vec.bn_stats(stats[:, t, :], x2[:, t, :])
            link(ins)
            for t in range(RT):
                ins = vec.bn_aggr(mean_var[:, t, :], stats[:, t, :])
            link(ins)
            newton.on_vector(dve, link, mean_var[:, :, 1], rstd[:], eps_ready, 1)
            for t in range(RT):
                vec.tensor_scalar(normed[:, t, :], x2[:, t, :], mean_var[:, t, 0:1], rstd[:, t:t + 1],
                                  ALU.subtract, ALU.mult).then_inc(normed_ready, 1)
            for f in range(FC):
                dve.wait_ge(sig_ready, f + 1)
                vec.tensor_tensor(silu[:, f % 2], sig[:, f % 2], banks[:, 4 + f % 2, :], ALU.mult)\
                    .then_inc(silu_ready, 1)
                dve.wait_ge(silu_ready, f + 1)
                vec.tensor_tensor(hidden[:, f, :], silu[:, f % 2], banks[:, 6 + f % 2, :], ALU.mult)\
                    .then_inc(hidden_ready, 1)
            for t in range(RT):
                dve.wait_ge(down_done, t + 1)
                vec.tensor_tensor(result[:, t, :], banks[:, t, :], x2[:, t, :], ALU.add).then_inc(result_ready, 1)


def setup_constants(nc, g):
    with ExitStack() as ctx:
        done = ctx.enter_context(nc.semaphore("constants_step"))
        made = ctx.enter_context(nc.semaphore("partition_bit"))
        number = ctx.enter_context(nc.sbuf_tensor("partition_number", [P, P], I32))
        ctx.callback(lambda: clear_semaphores(nc, [done, made]))
        block = ctx.enter_context(nc.Block())

        @block.gpsimd
        def _(pool):
            gp = nc.gpsimd
            count = 0
            gp.iota(number[:], pattern=[[0, P]], base=0, channel_multiplier=1).then_inc(made, 1)
            gp.iota(g["point"][:], pattern=[[P, 4]], base=0, channel_multiplier=1,
                    allow_small_or_imprecise_dtypes=True)
            for tile, period, value in ((g["ident"], P, 1.0), (g["average"][0], g["O"][0], 1.0 / STRIPS),
                                        (g["average"][1], g["O"][1], 1.0 / STRIPS)):
                ins = gp.memset(tile[:], 0.0)
                for shift in range(-(P // period - 1) * period, P, period):
                    count += 1
                    ins.then_inc(done, 1)
                    pool.wait_ge(done, count)
                    ins = gp.affine_select(out=tile[:], in_=tile[:], compare_op=ALU.not_equal, fill=value,
                                           base=shift, pattern=[[-1, P]], channel_multiplier=1)

        @block.vector
        def _(dve):
            vec = nc.vector
            chain = Step(dve, made)
            chain.count = 1
            dve.wait_ge(made, 1)
            chain.then_wait(vec.tensor_scalar(number[:], number[:], 4, 1, ALU.logical_shift_right, ALU.bitwise_and))
            halves = [v[:].rearrange("p (r j b) -> p r j b", j=2, b=B) for v in (g["apart"], number)]
            vec.tensor_scalar(halves[0][:, :, 0, :], halves[1][:, :, 0, :], -MASK, None, ALU.mult)
            vec.tensor_scalar(halves[0][:, :, 1, :], halves[1][:, :, 1, :], MASK, -MASK, ALU.mult, ALU.add)


def program(nc, g, out):
    g["O"] = (C, 2 * C)
    with ExitStack() as ctx:
        def sb(name, shape, dt=F32):
            return ctx.enter_context(nc.sbuf_tensor(name, shape, dt))

        g["feats"] = nc.dram_tensor("feats_scratch", [B, P, N], F32).ap()
        g["orders"] = nc.dram_tensor("orders_scratch", [METHODS * B, N], F16).ap()
        query = nc.dram_tensor("query_scratch", [B, C, N], F32).ap()
        message = nc.dram_tensor("message_scratch", [B, C, N], F32).ap()
        g["gateT"] = sb("gateT", [P, H // P, FF])
        g["upT"] = sb("upT", [P, H // P, FF])
        g["downT"] = sb("downT", [P, FF // P, H])
        g["ident"] = sb("ident", [P, P])
        g["average"] = [sb("average0", [P, P]), sb("average1", [P, P])]
        g["point"] = sb("point", [P, 4])
        g["apart"] = sb("apart", [P, P])
        g["raw_in"] = [ctx.enter_context(nc.semaphore(f"raw_in{i}")) for i in range(2)]
        g["scales_in"] = ctx.enter_context(nc.semaphore("scales_in"))
        setup_constants(nc, g)
        sort_and_prepare(nc, g)
        for layer in range(2):
            strips = P // g["O"][layer]
            with nc.sbuf_tensor(f"sorted_rows_{layer}", [P, B, SW], F32) as sorted_rows, \
                 nc.sbuf_tensor(f"hmax_{layer}", [P, B, STRIPS // strips, SP_PTS], F32) as hmax, \
                 nc.sbuf_tensor(f"hstats_{layer}", [P, B, STRIPS // strips * 24], F32) as hstats:
                gather_windows(nc, g, layer, sorted_rows[:])
                window_attention(nc, g, layer, sorted_rows[:], hmax[:], hstats[:])
                close_layer(nc, g, layer, hmax[:], hstats[:])
        x1 = sb("x1", [P, RT, N])
        mix_features(nc, g, x1, query)
        batch_attention(nc, g, query, message)
        feed_forward(nc, g, x1, message, out)


_INS = ["x", "ctx_4096", "L0_xattn_W_lin1", "L0_xattn_b_lin1", "L0_xattn_W_lin2", "L0_xattn_b_lin2",
        "L0_xattn_W_conv1", "L0_xattn_W_conv2", "L0_xattn_W_conv3", "L0_ffn_gate_wq", "L0_ffn_gate_scale",
        "L0_ffn_up_wq", "L0_ffn_up_scale", "L0_ffn_down_wq", "L0_ffn_down_scale"]


def kernel(**inputs):
    import concourse.bacc as bacc
    from concourse.bass_utils import run_bass_kernel_spmd

    nc = bacc.Bacc("TRN2", target_bir_lowering=False, num_devices=1)
    arrays, aps = {}, {}
    for name in _INS:
        a = np.ascontiguousarray(inputs[name])
        arrays[f"in_{name}"] = a
        aps[name] = nc.dram_tensor(f"in_{name}", a.shape, mybir.dt.from_np(a.dtype), kind="ExternalInput").ap()
    out = nc.dram_tensor("out_x", (B, C, N), F32, kind="ExternalOutput").ap()
    x = "L0_xattn_"
    g = {"x": aps["x"], "ctx": aps["ctx_4096"],
         "w_lin": [aps[x + "W_lin1"], aps[x + "W_lin2"]], "b_lin": [aps[x + "b_lin1"], aps[x + "b_lin2"]],
         "w_conv": [aps[x + "W_conv1"], aps[x + "W_conv2"]], "w_mix": aps[x + "W_conv3"]}
    for name in ("gate", "up", "down"):
        g[name + "_wq"] = aps[f"L0_ffn_{name}_wq"]
        g[name + "_scale"] = aps[f"L0_ffn_{name}_scale"]
    program(nc, g, out)
    r = run_bass_kernel_spmd(nc, [arrays], core_ids=[0])
    return r.results[0]["out_x"]
```
